# Optimizing a Trainium2 kernel written in Bass

```python
import numpy as np
import jax
import jax.numpy as jnp

def _softmax(x, axis=-1):
    return jax.nn.softmax(x, axis=axis)

def _gelu(x):
    return jax.nn.gelu(x, approximate=True)

def _silu(x):
    return jax.nn.silu(x)

def _sigmoid(x):
    return jax.nn.sigmoid(x)

def _layernorm(x, axis=-1, eps=1e-05):
    m = jnp.mean(x, axis=axis, keepdims=True)
    v = jnp.var(x, axis=axis, keepdims=True)
    return (x - m) / jnp.sqrt(v + eps)

def _scatter_add(tgt, idx, src, axis=0):
    return tgt.at[idx].add(src)

def _segment_sum(src, seg, n):
    return jax.ops.segment_sum(src, seg, n)
kernel_name = 'mk_gnn_ffn_d2_gnn_r8_b6a415'

def setup_inputs(seed: int=0):
    np.random.seed(seed)
    _w = jnp.asarray

    def _rec_inputs():
        import jax
        import jax.numpy as jnp
        _gk = jax.random.key(seed)
        x = -0.0002117 + 1 * jax.random.normal(jax.random.fold_in(_gk, 1), (6250, 256), jnp.float32)
        _s = jax.random.randint(jax.random.fold_in(_gk, 2), (50000,), 0, 6250, jnp.int32)
        _d = jax.random.randint(jax.random.fold_in(_gk, 3), (50000,), 0, 6250, jnp.int32)
        _loop = jnp.arange(6250, dtype=jnp.int32)
        src = jnp.concatenate([_s, _d, _loop])
        dst = jnp.concatenate([_d, _s, _loop])
        _o = jnp.argsort(dst, stable=True)
        src = src[_o]
        dst = dst[_o]
        return (x, src, dst)
    x, src, dst = _rec_inputs()

    def _L0_gnn_setup():
        import jax, jax.numpy as jnp
        import numpy as np
        N_NODES = 12500
        N_EDGES = 200000
        D_IN = 256
        HID = 256

        def _gcn_layer(h_in, W, b, src, dst, norm, deg_inv, n):
            h = h_in @ W
            msg = h[src] * norm[:, None]
            agg = jax.ops.segment_sum(msg, dst, num_segments=n)
            return agg + h * deg_inv[:, None] + b
        key = jax.random.key(seed)
        ks = jax.random.split(key, 12)
        x = jax.random.normal(ks[0], (N_NODES, D_IN), dtype=jnp.float32)
        edge_index = jax.random.randint(ks[1], (2, N_EDGES), 0, N_NODES, dtype=jnp.int32)

        def lin(k, fan_in, fan_out):
            s = 1.0 / np.sqrt(fan_in)
            kw, kb = jax.random.split(k)
            W = jax.random.uniform(kw, (fan_in, fan_out), jnp.float32, -s, s)
            b = jax.random.uniform(kb, (fan_out,), jnp.float32, -s, s)
            return (W, b)
        W1, b1 = lin(ks[2], D_IN, HID)
        W2, b2 = lin(ks[3], HID, HID)
        W3, b3 = lin(ks[4], HID, HID // 2)
        Wp, bp = lin(ks[5], HID // 2, D_IN)
        return {'x': x, 'edge_index': edge_index, 'W1': W1, 'b1': b1, 'W2': W2, 'b2': b2, 'W3': W3, 'b3': b3, 'Wp': Wp, 'bp': bp}
    _L0_gnn_all = _L0_gnn_setup()
    _L0_gnn_in = {k: v for k, v in _L0_gnn_all.items() if k in ('W1', 'b1', 'W2', 'b2', 'W3', 'b3', 'Wp', 'bp')}
    del _L0_gnn_all

    def _L0_ffn_setup():
        import math
        import jax, jax.numpy as jnp
        import numpy as np
        CAPACITY_FACTOR = 1.25
        TOP_K = 2
        LN_EPS = 1e-05

        def _layer_norm(x, gamma, beta):
            mu = jnp.mean(x, axis=-1, keepdims=True)
            var = jnp.var(x, axis=-1, keepdims=True)
            return (x - mu) * jax.lax.rsqrt(var + LN_EPS) * gamma + beta
        key = jax.random.key(seed)
        ks = jax.random.split(key, 4)
        B, S, D, F, E = (8, 512, 256, 512, 8)
        x = jax.random.normal(ks[0], (B, S, D), dtype=jnp.float32)
        Wr = jax.random.normal(ks[1], (D, E), dtype=jnp.float32) / np.sqrt(D)
        br = jnp.zeros((E,), jnp.float32)
        W1 = jax.random.normal(ks[2], (E, D, F), dtype=jnp.float32) / np.sqrt(D)
        b1 = jnp.zeros((E, F), jnp.float32)
        W2 = jax.random.normal(ks[3], (E, F, D), dtype=jnp.float32) / np.sqrt(F)
        b2 = jnp.zeros((E, D), jnp.float32)
        gamma = jnp.ones((D,), jnp.float32)
        beta = jnp.zeros((D,), jnp.float32)
        return {'x': x, 'Wr': Wr, 'br': br, 'W1': W1, 'b1': b1, 'W2': W2, 'b2': b2, 'gamma': gamma, 'beta': beta}
    _L0_ffn_all = _L0_ffn_setup()
    _L0_ffn_in = {k: v for k, v in _L0_ffn_all.items() if k in ('Wr', 'br', 'W1', 'b1', 'W2', 'b2', 'gamma', 'beta')}
    del _L0_ffn_all

    def _L1_gnn_setup():
        import jax, jax.numpy as jnp
        import numpy as np
        N, IN_CH, HEADS, OUT_CH, E = (6250, 256, 4, 64, 100000)
        key = jax.random.key(seed)
        k1, k2, k3, k4, k5 = jax.random.split(key, 5)
        x = jax.random.normal(k1, (N, IN_CH), dtype=jnp.float32)
        edge_index = jax.random.randint(k2, (2, E), 0, N, dtype=jnp.int64)
        bw = float(np.sqrt(6.0 / (IN_CH + HEADS * OUT_CH)))
        ba = float(np.sqrt(6.0 / (HEADS + OUT_CH)))
        weight = jax.random.uniform(k3, (IN_CH, HEADS * OUT_CH), jnp.float32, -bw, bw)
        attn_l = jax.random.uniform(k4, (HEADS, OUT_CH), jnp.float32, -ba, ba)
        attn_r = jax.random.uniform(k5, (HEADS, OUT_CH), jnp.float32, -ba, ba)
        return {'x': x, 'edge_index': edge_index, 'weight': weight, 'attn_l': attn_l, 'attn_r': attn_r}
    _L1_gnn_all = _L1_gnn_setup()
    _L1_gnn_in = {k: v for k, v in _L1_gnn_all.items() if k in ('weight', 'attn_l', 'attn_r')}
    del _L1_gnn_all

    def _L1_ffn_setup():
        import math
        import jax, jax.numpy as jnp
        import numpy as np
        CAPACITY_FACTOR = 1.25
        key = jax.random.key(seed)
        ks = jax.random.split(key, 5)
        B, L, D, F, E = (8, 1024, 256, 1024, 8)
        h = jax.random.normal(ks[0], (B, L, D), dtype=jnp.float32)
        gate_w = jax.random.normal(ks[1], (D, E), dtype=jnp.float32) * 0.02
        gate_b = jnp.zeros((E,), dtype=jnp.float32)
        w1 = jax.random.normal(ks[2], (E, D, F), dtype=jnp.float32) * (1.0 / math.sqrt(D))
        b1 = jnp.zeros((E, F), dtype=jnp.float32)
        w2 = jax.random.normal(ks[3], (E, F, D), dtype=jnp.float32) * (1.0 / math.sqrt(F))
        b2 = jnp.zeros((E, D), dtype=jnp.float32)
        return {'h': h, 'gate_w': gate_w, 'gate_b': gate_b, 'w1': w1, 'b1': b1, 'w2': w2, 'b2': b2}
    _L1_ffn_all = _L1_ffn_setup()
    _L1_ffn_in = {k: v for k, v in _L1_ffn_all.items() if k in ('gate_w', 'gate_b', 'w1', 'b1', 'w2', 'b2')}
    del _L1_ffn_all
    return {'x': x, 'src': src, 'dst': dst, 'L0_gnn_W1': _L0_gnn_in['W1'], 'L0_gnn_b1': _L0_gnn_in['b1'], 'L0_gnn_W2': _L0_gnn_in['W2'], 'L0_gnn_b2': _L0_gnn_in['b2'], 'L0_gnn_W3': _L0_gnn_in['W3'], 'L0_gnn_b3': _L0_gnn_in['b3'], 'L0_gnn_Wp': _L0_gnn_in['Wp'], 'L0_gnn_bp': _L0_gnn_in['bp'], 'L0_ffn_Wr': _L0_ffn_in['Wr'], 'L0_ffn_br': _L0_ffn_in['br'], 'L0_ffn_W1': _L0_ffn_in['W1'], 'L0_ffn_b1': _L0_ffn_in['b1'], 'L0_ffn_W2': _L0_ffn_in['W2'], 'L0_ffn_b2': _L0_ffn_in['b2'], 'L0_ffn_gamma': _L0_ffn_in['gamma'], 'L0_ffn_beta': _L0_ffn_in['beta'], 'L1_gnn_weight': _L1_gnn_in['weight'], 'L1_gnn_attn_l': _L1_gnn_in['attn_l'], 'L1_gnn_attn_r': _L1_gnn_in['attn_r'], 'L1_ffn_gate_w': _L1_ffn_in['gate_w'], 'L1_ffn_gate_b': _L1_ffn_in['gate_b'], 'L1_ffn_w1': _L1_ffn_in['w1'], 'L1_ffn_b1': _L1_ffn_in['b1'], 'L1_ffn_w2': _L1_ffn_in['w2'], 'L1_ffn_b2': _L1_ffn_in['b2']}

def reference(x, src, dst, L0_gnn_W1, L0_gnn_b1, L0_gnn_W2, L0_gnn_b2, L0_gnn_W3, L0_gnn_b3, L0_gnn_Wp, L0_gnn_bp, L0_ffn_Wr, L0_ffn_br, L0_ffn_W1, L0_ffn_b1, L0_ffn_W2, L0_ffn_b2, L0_ffn_gamma, L0_ffn_beta, L1_gnn_weight, L1_gnn_attn_l, L1_gnn_attn_r, L1_ffn_gate_w, L1_ffn_gate_b, L1_ffn_w1, L1_ffn_b1, L1_ffn_w2, L1_ffn_b2):
    import jax
    import jax.numpy as jnp

    def _L0_gnn_ref(x, edge_index, W1, b1, W2, b2, W3, b3, Wp, bp):
        import jax, jax.numpy as jnp
        import numpy as np
        N_NODES = 12500
        N_EDGES = 200000
        D_IN = 256
        HID = 256

        def _gcn_layer(h_in, W, b, src, dst, norm, deg_inv, n):
            h = h_in @ W
            msg = h[src] * norm[:, None]
            agg = jax.ops.segment_sum(msg, dst, num_segments=n)
            return agg + h * deg_inv[:, None] + b
        n = x.shape[0]
        src, dst = (edge_index[0], edge_index[1])
        deg = jax.ops.segment_sum(jnp.ones(src.shape[0], x.dtype), dst, num_segments=n) + 1.0
        dinv_sqrt = jax.lax.rsqrt(deg)
        norm = dinv_sqrt[src] * dinv_sqrt[dst]
        deg_inv = 1.0 / deg
        h = jax.nn.relu(_gcn_layer(x, W1, b1, src, dst, norm, deg_inv, n))
        h = jax.nn.relu(_gcn_layer(h, W2, b2, src, dst, norm, deg_inv, n))
        h = jax.nn.relu(_gcn_layer(h, W3, b3, src, dst, norm, deg_inv, n))
        return h @ Wp + bp

    def _L0_ffn_ref(x, Wr, br, W1, b1, W2, b2, gamma, beta):
        import math
        import jax, jax.numpy as jnp
        import numpy as np
        CAPACITY_FACTOR = 1.25
        TOP_K = 2
        LN_EPS = 1e-05

        def _layer_norm(x, gamma, beta):
            mu = jnp.mean(x, axis=-1, keepdims=True)
            var = jnp.var(x, axis=-1, keepdims=True)
            return (x - mu) * jax.lax.rsqrt(var + LN_EPS) * gamma + beta
        B, S, D = x.shape
        E = Wr.shape[1]
        N = B * S
        K = TOP_K
        logits = jnp.mean(x, axis=1) @ Wr + br
        routing_weights = jax.nn.softmax(logits, axis=-1)
        capacity = float(math.ceil(N * CAPACITY_FACTOR / E))
        expected_loads = routing_weights.sum(axis=0) * (N / B)
        scale = jnp.where(expected_loads > capacity, capacity / expected_loads, 1.0)
        routing_weights = jax.nn.softmax(routing_weights * scale, axis=-1)
        rw_tok = jnp.broadcast_to(routing_weights[:, None, :], (B, S, E)).reshape(N, E)
        top_w, top_i = jax.lax.top_k(rw_tok, K)
        top_w = jax.nn.softmax(top_w, axis=-1)
        xf = x.reshape(N, D)
        h = jax.nn.gelu(jnp.einsum('nd,edf->enf', xf, W1) + b1[:, None, :], approximate=False)
        y = jnp.einsum('enf,efd->end', h, W2) + b2[:, None, :]
        w_dense = jnp.zeros((N, E), x.dtype).at[jnp.arange(N)[:, None], top_i].add(top_w)
        out = jnp.einsum('ne,end->nd', w_dense, y).reshape(B, S, D)
        out = _layer_norm(out + x, gamma, beta)
        return out

    def _L1_gnn_ref(x, edge_index, weight, attn_l, attn_r):
        import jax, jax.numpy as jnp
        import numpy as np
        N, IN_CH, HEADS, OUT_CH, E = (6250, 256, 4, 64, 100000)
        heads, out_ch = attn_l.shape
        n = x.shape[0]
        xt = jnp.matmul(x, weight).reshape(-1, heads, out_ch)
        row, col = (edge_index[0], edge_index[1])
        alpha_l = jnp.einsum('ehd,hd->eh', xt[row], attn_l)
        alpha_r = jnp.einsum('ehd,hd->eh', xt[col], attn_r)
        alpha = jax.nn.softmax(jax.nn.leaky_relu(alpha_l + alpha_r, 0.01), axis=1)
        tmp = jnp.einsum('nh,nhd->nd', alpha[:n], xt[col[:n]])
        out = jnp.broadcast_to(tmp[:, None, :], (n, heads, out_ch))
        return out.reshape(n, heads * out_ch)

    def _L1_ffn_ref(h, gate_w, gate_b, w1, b1, w2, b2):
        import math
        import jax, jax.numpy as jnp
        import numpy as np
        CAPACITY_FACTOR = 1.25
        B, L, D = h.shape
        E = gate_w.shape[1]
        T = B * L
        C = max(1, math.ceil(CAPACITY_FACTOR * T / E))
        x = h.reshape(T, D)
        logits = x @ gate_w + gate_b
        probs = jax.nn.softmax(logits, axis=-1)
        idx = jnp.argmax(probs, axis=-1)
        prb = jnp.take_along_axis(probs, idx[:, None], axis=1)[:, 0]
        one_hot = jax.nn.one_hot(idx, E, dtype=jnp.float32)
        pos = (jnp.cumsum(one_hot, axis=0) * one_hot).sum(-1).astype(jnp.int32) - 1
        kept = pos < C
        pos_safe = jnp.where(kept, pos, C)
        buf = jnp.zeros((E, C, D), dtype=h.dtype).at[idx, pos_safe].set(x, mode='drop')
        hmid = jax.nn.relu(jnp.einsum('ecd,edf->ecf', buf, w1) + b1[:, None, :])
        ybuf = jnp.einsum('ecf,efd->ecd', hmid, w2) + b2[:, None, :]
        pos_g = jnp.minimum(pos, C - 1)
        y_tok = ybuf[idx, pos_g] * (prb * kept)[:, None]
        y = y_tok.reshape(B, L, D)
        y = jnp.nan_to_num(y, nan=0.0, posinf=10000.0, neginf=-10000.0)
        return y
    edge_index = jnp.stack([src, dst])
    x = x + _L0_gnn_ref(_layernorm(x, axis=-1), edge_index, L0_gnn_W1, L0_gnn_b1, L0_gnn_W2, L0_gnn_b2, L0_gnn_W3, L0_gnn_b3, L0_gnn_Wp, L0_gnn_bp)
    x = x + _L0_ffn_ref(_layernorm(x, axis=-1)[None], L0_ffn_Wr, L0_ffn_br, L0_ffn_W1, L0_ffn_b1, L0_ffn_W2, L0_ffn_b2, L0_ffn_gamma, L0_ffn_beta)[0]
    x = x + _L1_gnn_ref(_layernorm(x, axis=-1), edge_index, L1_gnn_weight, L1_gnn_attn_l, L1_gnn_attn_r)
    x = x + _L1_ffn_ref(_layernorm(x, axis=-1)[None], L1_ffn_gate_w, L1_ffn_gate_b, L1_ffn_w1, L1_ffn_b1, L1_ffn_w2, L1_ffn_b2)[0]
    return x

_drawn_inputs = setup_inputs


def setup_inputs(seed=0):
    import zlib

    import numpy as np

    out = dict(_drawn_inputs(seed))
    spreads = {'L0_ffn_br': (0.0, 0.8),
     'L0_ffn_b1': (0.0, 1.567),
     'L0_ffn_b2': (0.0, 0.8),
     'L0_ffn_gamma': (1.0, 0.6),
     'L0_ffn_beta': (0.0, 0.646),
     'L1_ffn_gate_b': (0.0, 0.8),
     'L1_ffn_b1': (0.0, 2.0),
     'L1_ffn_b2': (0.0, 2.0)}
    factors = {'L0_gnn_W1': 8.0,
     'L0_gnn_b1': 8.0,
     'L0_gnn_W2': 8.0,
     'L0_gnn_b2': 8.0,
     'L0_gnn_W3': 5.057,
     'L0_gnn_b3': 3.695,
     'L0_gnn_Wp': 2.9,
     'L0_ffn_Wr': 8.0,
     'L0_gnn_bp': 8.0,
     'L1_gnn_attn_l': 7.674,
     'L1_ffn_gate_w': 4.407,
     'L1_ffn_w1': 8.0,
     'L1_ffn_w2': 6.793}
    for name, (base, spread) in spreads.items():
        noise = np.random.default_rng([zlib.crc32(name.encode()), seed]).standard_normal(out[name].shape)
        drawn = base * np.exp(spread * noise) if base else spread * noise
        out[name] = jnp.asarray(drawn.astype(out[name].dtype))
    for name, factor in factors.items():
        out[name] = (out[name] * factor).astype(out[name].dtype)
    return out
```

```python
from contextlib import ExitStack

import concourse.bass as bass
from concourse import mybir

ALU = mybir.AluOpType
ACT = mybir.ActivationFunctionType
AX = mybir.AxisListType
F32 = mybir.dt.float32
BF16 = mybir.dt.bfloat16
I32 = mybir.dt.int32
U32 = mybir.dt.uint32
ds = bass.ds

P = 128
D = 256
DK = D // P
EPS = 1e-5
TILE_RING = 7
CHUNK_RING = 8
HOT_RING = 4
WINDOW = P


def ceil_div(a, b):
    return (a + b - 1) // b


class Shared:
    pass


class Stage(ExitStack):

    def __init__(self, nc):
        super().__init__()
        self.nc, self.sems = nc, []

    def sem(self, name):
        self.sems.append(self.nc.alloc_semaphore(name))
        return self.sems[-1]

    def __exit__(self, *error):
        super().__exit__(*error)
        if self.sems and error[0] is None:
            self.nc.clear_and_free_semaphores(self.sems)
            self.nc.all_engine_barrier(sem_only=True)


def load_inputs(nc, m, a, slots):
    n_main = m.full_tiles * P
    with Stage(nc) as ctx:
        pads_zero = ctx.sem("pads_zero")
        edges_landed = ctx.sem("edges_landed")
        x_landed = ctx.sem("x_landed")
        w_landed = ctx.sem("w_landed")
        iota_made = ctx.sem("iota_made")
        zeroed = ctx.sem("zeroed")
        block = ctx.enter_context(nc.Block())

        @block.sync
        def _(sp):
            sp.wait_ge(pads_zero, 3)
            sp.dma_start(m.src[:, 0:m.full_chunks], a["src_main"]).then_inc(edges_landed, 16)
            sp.dma_start(m.dst[:, 0:m.full_chunks], a["dst_main"]).then_inc(edges_landed, 16)
            sp.dma_start(m.src[0:m.tail_edges, m.full_chunks:m.full_chunks + 1], a["src_tail"]).then_inc(edges_landed, 16)
            sp.dma_start(m.dst[0:m.tail_edges, m.full_chunks:m.full_chunks + 1], a["dst_tail"]).then_inc(edges_landed, 16)
            sp.dma_start(m.x[:, 0:m.full_tiles, :],
                         a["x"][0:n_main, :].rearrange("(t p) d -> p t d", p=P)).then_inc(x_landed, 16)
            sp.dma_start(m.x[0:m.tail_nodes, m.full_tiles, :], a["x"][n_main:m.nodes, :]).then_inc(x_landed, 16)
            sp.wait_ge(edges_landed, 64)
            sp.wait_ge(x_landed, 32)

        @block.scalar
        def _(act):
            act.dma_start(m.w1[:], a["gnn_w1"].rearrange("(k p) n -> p k n", p=P)).then_inc(w_landed, 16)
            act.dma_start(m.w2[:], a["gnn_w2"].rearrange("(k p) n -> p k n", p=P)).then_inc(w_landed, 16)
            act.dma_start(m.w3[:], a["gnn_w3"].rearrange("(k p) n -> p k n", p=P)).then_inc(w_landed, 16)
            act.dma_start(m.wp[:], a["gnn_wp"]).then_inc(w_landed, 16)
            act.dma_start(m.b1[:], a["gnn_b1"].partition_broadcast(P)).then_inc(w_landed, 16)
            act.dma_start(m.b2[:], a["gnn_b2"].partition_broadcast(P)).then_inc(w_landed, 16)
            act.dma_start(m.b3[:], a["gnn_b3"].partition_broadcast(P)).then_inc(w_landed, 16)
            act.dma_start(m.bp[:], a["gnn_bp"].partition_broadcast(P)).then_inc(w_landed, 16)
            act.wait_ge(w_landed, 16 * 8)
            act.wait_ge(m.zero_made, 1)
            full = slots.shape[0] // P
            half = full // 2
            for lo, hi in ((0, half), (half, full)):
                act.dma_start(slots[lo * P:hi * P, :].rearrange("(t p) w -> p t w", p=P),
                              m.zero[:].unsqueeze(1).to_broadcast([P, hi - lo, D + 1])).then_inc(m.slots_zeroed, 16)
            act.dma_start(slots[full * P:, :], m.zero[0:slots.shape[0] - full * P, :]).then_inc(m.slots_zeroed, 16)

        @block.vector
        def _(dve):
            nc.vector.memset(m.x[:, m.full_tiles, :], 0.0).then_inc(pads_zero, 1)
            nc.vector.memset(m.src[:, m.full_chunks:m.chunks], 0).then_inc(pads_zero, 1)
            nc.vector.memset(m.dst[:, m.full_chunks:m.chunks], 0).then_inc(pads_zero, 1)
            nc.vector.memset(m.agg[:, :, m.tiles * P:], 0.0)
            nc.vector.memset(m.ones[:], 1.0)
            nc.vector.memset(m.zero[:], 0.0).then_inc(m.zero_made, 1)

        @block.gpsimd
        def _(pool):
            nc.gpsimd.iota(m.iota_i[:], pattern=[[1, P]], base=0, channel_multiplier=0).then_inc(iota_made, 1)
            nc.gpsimd.iota(m.part_i[:], pattern=[[1, 1]], base=0, channel_multiplier=1).then_inc(iota_made, 1)
            nc.gpsimd.memset(m.ident[:], 0.0).then_inc(zeroed, 1)
            nc.gpsimd.memset(m.first_row[:], 1.0).then_inc(zeroed, 1)
            pool.wait_ge(iota_made, 2)
            nc.gpsimd.tensor_copy(m.iota[:], m.iota_i[:])
            nc.gpsimd.tensor_copy(m.iota_b[:], m.iota_i[:])
            nc.gpsimd.tensor_copy(m.part[:], m.part_i[:])
            pool.wait_ge(zeroed, 2)
            nc.gpsimd.affine_select(out=m.ident[:], in_=m.ident[:], compare_op=ALU.not_equal, fill=1.0, base=0,
                                    pattern=[[-1, P]], channel_multiplier=1)
            nc.gpsimd.affine_select(out=m.first_row[:], in_=m.first_row[:], compare_op=ALU.is_ge, fill=0.0, base=0,
                                    pattern=[[0, P]], channel_multiplier=-1)


def degrees(nc, m):
    half = m.chunks // 2
    groups = m.chunks // CHUNK_RING
    with Stage(nc) as ctx:
        dst_f = m.dst_f
        ends = ctx.enter_context(nc.sbuf_tensor("ends", [P, 2], F32))
        astray = ctx.enter_context(nc.sbuf_tensor("astray", [P, 4], F32))
        ends_done, astray_done, counted = ctx.sem("ends_done"), ctx.sem("astray_done"), ctx.sem("counted")
        hi_i = ctx.enter_context(nc.sbuf_tensor("hi_i", [P, m.chunks], I32))
        lo_i = ctx.enter_context(nc.sbuf_tensor("lo_i", [P, m.chunks], I32))
        hi = ctx.enter_context(nc.sbuf_tensor("hi", [P, m.chunks], F32))
        lo = ctx.enter_context(nc.sbuf_tensor("lo", [P, m.chunks], F32))
        hot_lo = ctx.enter_context(nc.sbuf_tensor("hot_lo", [P, 2, CHUNK_RING, P], BF16))
        hot_hi = ctx.enter_context(nc.sbuf_tensor("hot_hi", [P, 2, CHUNK_RING, m.tiles], BF16))
        deg = ctx.enter_context(nc.sbuf_tensor("deg", [P, m.tiles], F32))
        root = ctx.enter_context(nc.sbuf_tensor("root", [P, m.tiles], F32))
        ints_done = ctx.sem("ints_done")
        floats_done = ctx.sem("floats_done")
        base_spread = ctx.sem("base_spread")
        dloc_made = ctx.sem("dloc_made")
        pads_marked = ctx.sem("pads_marked")
        hot_ready = ctx.sem("hot_ready")
        group_used = ctx.sem("group_used")
        deg_done = ctx.sem("deg_done")
        root_done = ctx.sem("root_done")
        block = ctx.enter_context(nc.Block())
        base_ps = m.ps[:, 0:2, 0:half]
        deg_ps = m.ps[:, 2, 0:m.tiles]

        @block.vector
        def _(dve):
            nc.vector.tensor_copy(dst_f[:], m.dst[:]).then_inc(floats_done, 1)
            nc.vector.tensor_scalar(hi_i[:], m.dst[:], 7, None, ALU.logical_shift_right).then_inc(ints_done, 1)
            nc.vector.tensor_scalar(lo_i[:], m.dst[:], P - 1, None, ALU.bitwise_and).then_inc(ints_done, 1)
            dve.wait_ge(ints_done, 2)
            nc.vector.tensor_copy(hi[:], hi_i[:]).then_inc(floats_done, 1)
            nc.vector.tensor_copy(lo[:], lo_i[:])
            dve.wait_ge(base_spread, 1)
            dve.wait_ge(floats_done, 2)
            nc.vector.tensor_tensor(m.dloc[:].rearrange("p (h c) -> p h c", h=2),
                                    dst_f[:].rearrange("p (h c) -> p h c", h=2), base_ps,
                                    ALU.subtract).then_inc(dloc_made, 1)
            dve.wait_ge(pads_marked, 5)
            nc.vector.reduce_max(ends[:, 0:1], m.dloc[:], AX.X).then_inc(ends_done, 1)
            nc.vector.tensor_reduce(ends[:, 1:2], m.dloc[:], AX.X, ALU.min).then_inc(ends_done, 1)
            dve.wait_ge(ends_done, 2)
            nc.vector.tensor_scalar(astray[:, 0:1], ends[:, 0:1], float(WINDOW - 1), None, ALU.is_gt).then_inc(astray_done, 1)
            nc.vector.tensor_scalar(astray[:, 1:2], ends[:, 1:2], 0.0, None, ALU.is_lt).then_inc(astray_done, 1)

            def put(g, h):
                for j in range(CHUNK_RING):
                    hot = nc.vector.tensor_scalar(hot_lo[:, h, j, :], m.iota_b[:],
                                                  lo[:, ds(g * CHUNK_RING + j, 1)], None, ALU.is_equal)
                nc.vector.tensor_tensor(hot_hi[:, h, :, :],
                                        hi[:, ds(g * CHUNK_RING, CHUNK_RING)].unsqueeze(2)
                                        .to_broadcast([P, CHUNK_RING, m.tiles]),
                                        m.iota[:, 0:m.tiles].unsqueeze(1).to_broadcast([P, CHUNK_RING, m.tiles]),
                                        ALU.is_equal).then_inc(hot_ready, 1)

            put(0, 0)
            put(1, 1)
            with dve.Fori(0, (groups - 2) // 2) as g:
                for h in range(2):
                    dve.wait_ge(group_used, g * 2 + (1 + h))
                    put(g * 2 + (2 + h), h)
            dve.wait_ge(counted, 1)
            nc.vector.reduce_max(astray[0:1, 2:3], m.ps[0:1, 3, 0:2], AX.X).then_inc(astray_done, 1)
            dve.wait_ge(astray_done, 3)
            nc.vector.tensor_scalar(m.astray[0:1, :], astray[0:1, 2:3], 0.0, None, ALU.is_gt)
            dve.wait_ge(group_used, groups)
            nc.vector.tensor_scalar(deg[:], deg_ps, 1.0, None, ALU.add).then_inc(deg_done, 1)
            dve.wait_ge(root_done, 1)
            nc.vector.reciprocal(m.dinv[:], root[:])

        @block.gpsimd
        def _(pool):
            c = m.full_chunks
            pool.wait_ge(dloc_made, 1)
            for targets in (m.dloc, dst_f):
                nc.gpsimd.affine_select(out=targets[:, c:c + 1], in_=targets[:, c:c + 1], compare_op=ALU.is_ge,
                                        fill=0.5, base=m.tail_edges - 1, pattern=[[0, 1]],
                                        channel_multiplier=-1).then_inc(pads_marked, 1)
            nc.gpsimd.memset(m.dloc[:, c + 1:m.chunks], 0.5)
            nc.gpsimd.memset(dst_f[:, c + 1:m.chunks], 0.5).then_inc(pads_marked, 1)
            nc.gpsimd.affine_select(out=hi[:, c:c + 1], in_=hi[:, c:c + 1], compare_op=ALU.is_ge, fill=-1.0,
                                    base=m.tail_edges - 1, pattern=[[0, 1]],
                                    channel_multiplier=-1).then_inc(pads_marked, 1)
            nc.gpsimd.memset(hi[:, c + 1:m.chunks], -1.0).then_inc(pads_marked, 1)

        @block.tensor
        def _(pe):
            pe.wait_ge(floats_done, 1)
            for h in range(2):
                last = nc.tensor.matmul(base_ps[:, h, :], m.first_row[:], dst_f[:, h * half:(h + 1) * half],
                                        start=True, stop=True)
            last.then_inc(base_spread, 1)
            pe.wait_ge(astray_done, 2)
            nc.tensor.matmul(m.ps[0:1, 3, 0:2], m.ones[:, 0:1], astray[:, 0:2], start=True, stop=True).then_inc(counted, 1)
            pe.wait_ge(hot_ready, 1)
            for j in range(CHUNK_RING):
                mm = nc.tensor.matmul(deg_ps, hot_lo[:, 0, j, :], hot_hi[:, 0, j, :], start=(j == 0), stop=False,
                                      skip_group_check=True)
            mm.then_inc(group_used, 1)
            with pe.Fori(0, (groups - 2) // 2) as g:
                for h in range(2):
                    pe.wait_ge(hot_ready, g * 2 + (2 + h))
                    for j in range(CHUNK_RING):
                        mm = nc.tensor.matmul(deg_ps, hot_lo[:, 1 - h, j, :], hot_hi[:, 1 - h, j, :], start=False,
                                              stop=False, skip_group_check=True)
                    mm.then_inc(group_used, 1)
            pe.wait_ge(hot_ready, groups)
            for j in range(CHUNK_RING):
                mm = nc.tensor.matmul(deg_ps, hot_lo[:, 1, j, :], hot_hi[:, 1, j, :], start=False,
                                      stop=(j == CHUNK_RING - 1), skip_group_check=True)
            mm.then_inc(group_used, 1)

        @block.scalar
        def _(act):
            act.wait_ge(deg_done, 1)
            nc.scalar.activation(root[:], deg[:], ACT.Sqrt).then_inc(root_done, 1)


def tile_loop(eng, tiles, steps):
    R = TILE_RING
    lags = max(lag for lag, _ in steps)
    assert tiles % R == 0 and lags < R
    for s in range(2 * R):
        for lag, body in steps:
            if s >= lag:
                body(s - lag, (s - lag) % R, s - lag >= R, (s - lag) // R)
    with eng.Fori(2, tiles // R) as g:
        for j in range(R):
            for lag, body in steps:
                body(g * R + (j - lag), (j - lag) % R, True, g + (j - lag) // R)
    for s in range(tiles, tiles + lags):
        for lag, body in steps:
            if s - lag < tiles:
                body(s - lag, (s - lag) % R, True, (s - lag) // R)


def tile_of(buf, t):
    return buf[:, ds(t, 1), :].rearrange("p t d -> p (t d)")


def row_stats(nc, m, tag, rows_of, with_degree=False):
    loops = m.tiles // TILE_RING
    R = TILE_RING
    with Stage(nc) as ctx:
        sem = lambda name: ctx.sem(f"{tag}_{name}")
        stats = ctx.enter_context(nc.sbuf_tensor(f"{tag}_stats", [P, R, 6], F32))
        mv_ring = ctx.enter_context(nc.sbuf_tensor(f"{tag}_mv_ring", [P, R, 2], F32))
        veps = ctx.enter_context(nc.sbuf_tensor(f"{tag}_veps", [P, m.tiles], F32))
        std = ctx.enter_context(nc.sbuf_tensor(f"{tag}_std", [P, m.tiles], F32))
        rstd = ctx.enter_context(nc.sbuf_tensor(f"{tag}_rstd", [P, m.tiles], F32))
        stats_done, mv_done, mv_kept = sem("stats"), sem("mv"), sem("mv_kept")
        veps_done, std_done, rstd_done = sem("veps"), sem("std"), sem("rstd")
        block = ctx.enter_context(nc.Block())

        @block.vector
        def _(dve):
            with dve.Fori(0, loops) as g:
                for j in range(R):
                    nc.vector.bn_stats(stats[:, j, :], rows_of(g * R + j)).then_inc(stats_done, 1)
                for j in range(R):
                    dve.wait_ge(stats_done, g * R + (j + 1))
                    nc.vector.nop(nofuse=True)
                    nc.vector.bn_aggr(mv_ring[:, j, :], stats[:, j, :]).then_inc(mv_done, 1)
                dve.wait_ge(mv_done, (g + 1) * R)
                nc.vector.tensor_copy(m.mv[:, ds(g * R, R), :], mv_ring[:]).then_inc(mv_kept, 1)
                dve.wait_ge(mv_kept, g + 1)
            nc.vector.tensor_scalar(veps[:], m.mv[:, :, 1], EPS, None, ALU.add).then_inc(veps_done, 1)
            dve.wait_ge(std_done, 1)
            if with_degree:
                nc.vector.reciprocal(rstd[:], std[:]).then_inc(rstd_done, 1)
                dve.wait_ge(rstd_done, 1)
                nc.vector.tensor_tensor(m.scale[:], rstd[:], m.dinv[:], ALU.mult)
            else:
                nc.vector.reciprocal(m.scale[:], std[:])

        @block.scalar
        def _(act):
            act.wait_ge(veps_done, 1)
            nc.scalar.activation(std[:], veps[:], ACT.Sqrt).then_inc(std_done, 1)


def normalize(nc, m, tag, table=None, column_sums=False):
    R = TILE_RING
    with Stage(nc) as ctx:
        sem = lambda name: ctx.sem(f"{tag}_{name}")
        ring = ctx.enter_context(nc.sbuf_tensor(f"{tag}_ring", [P, R, D], F32))
        rows_ready, turned, turned_kept, sums_done = sem("rows"), sem("turned"), sem("turned_kept"), sem("sums")
        stored = [sem(f"stored{j}") for j in range(R)]
        block = ctx.enter_context(nc.Block())

        def turned_ps(j):
            return m.ps[:, j, 0:D].rearrange("p (k n) -> p k n", k=DK)

        @block.vector
        def _(dve):
            def rows(t, j, again, round_):
                if again:
                    dve.wait_ge(turned, t + (1 - R))
                    if table is not None:
                        dve.wait_ge(stored[j], round_ * 16)
                nc.vector.tensor_scalar(ring[:, j, :], tile_of(m.x, t), m.mv[:, ds(t, 1), 0], m.scale[:, ds(t, 1)],
                                        ALU.subtract, ALU.mult).then_inc(rows_ready, 1)
            tile_loop(dve, m.tiles, [(0, rows)])
            if column_sums:
                dve.wait_ge(turned, m.tiles)
                nc.vector.tensor_scalar(m.mean_row[0:1, :], m.ps[0:1, R, 0:D], 1.0 / m.nodes, None, ALU.mult)

        @block.scalar
        def _(act):
            def keep(t, j, again, round_):
                act.wait_ge(turned, t + 1)
                nc.scalar.copy(m.agg[:, :, ds(t * P, P)], turned_ps(j)).then_inc(turned_kept, 1)
            tile_loop(act, m.tiles, [(0, keep)])

        @block.tensor
        def _(pe):
            def turn(t, j, again, round_):
                pe.wait_ge(rows_ready, t + 1)
                if again:
                    pe.wait_ge(turned_kept, t + (1 - R))
                if column_sums:
                    nc.tensor.matmul(m.ps[0:1, R, 0:D], m.ones[:, 0:1], ring[:, j, :], start=not again and j == 0,
                                     stop=False, skip_group_check=True)
                for k in range(DK):
                    last = nc.tensor.transpose(turned_ps(j)[:, k, :], ring[:, j, k * P:(k + 1) * P], m.ident[:])
                last.then_inc(turned, 1)
            tile_loop(pe, m.tiles, [(0, turn)])

        if table is not None:
            @block.sync
            def _(sp):
                def store(t, j, again, round_):
                    sp.wait_ge(rows_ready, t + 1)
                    sp.dma_start(table[ds(t * P, P), :], ring[:, j, :]).then_inc(stored[j], 16)
                tile_loop(sp, m.tiles, [(0, store)])
                for j in range(R):
                    sp.wait_ge(stored[j], m.tiles // R * 16)


def sum_edges(nc, m, tag, table):
    R = 2 * CHUNK_RING
    B = 8
    H = CHUNK_RING
    loops = m.chunks // R
    with Stage(nc) as ctx:
        sem = lambda name: ctx.sem(f"{tag}_{name}")
        rows = ctx.enter_context(nc.sbuf_tensor(f"{tag}_rows", [P, R, D], F32))
        hot = ctx.enter_context(nc.sbuf_tensor(f"{tag}_hot", [P, R, P], F32))
        index = ctx.enter_context(nc.sbuf_tensor(f"{tag}_index", [P, R], I32))
        landed = [sem(f"landed{j}") for j in range(R)]
        group_free, tile_free, moved = sem("group_free"), sem("tile_free"), sem("moved")
        index_ready, hot_ready, summed, added = sem("index_ready"), sem("hot_ready"), sem("summed"), sem("added")
        places = ctx.enter_context(nc.sbuf_tensor(f"{tag}_places", [P, P], F32))
        block = ctx.enter_context(nc.Block())

        def branch(eng, in_windows, anywhere):
            astray = eng.value_load(m.astray[0:1, 0:1], min_val=0, max_val=1)
            with eng.If(astray == 0):
                in_windows()
            with eng.Else():
                anywhere()

        def part_ps(j):
            return m.ps[:, j % B, 0:DK * P].rearrange("p (k n) -> p k n", k=DK)

        @block.scalar
        def _(act):
            def in_windows():
                def put(g, h):
                    nc.scalar.copy(index[:, h * H:(h + 1) * H], m.src[:, ds(g * R + h * H, H)]).then_inc(index_ready, 1)
                for h in range(2):
                    put(0, h)
                with act.Fori(1, loops) as g:
                    for h in range(2):
                        for j in range(h * H, (h + 1) * H):
                            act.wait_ge(landed[j], g * 16)
                        put(g, h)

            def anywhere():
                with act.Fori(0, m.tiles) as w:
                    with act.Fori(0, loops) as g:
                        act.wait_ge(group_free, w * loops + (g + 1))
                        nc.scalar.copy(index[:], m.src[:, ds(g * R, R)]).then_inc(index_ready, 1)

            branch(act, in_windows, anywhere)

        @block.gpsimd
        def _(pool):
            def in_windows():
                def gather_half(g, h):
                    pool.wait_ge(index_ready, g * 2 + (1 + h))
                    nc.gpsimd.nop(nofuse=True)
                    for j in range(h * H, (h + 1) * H):
                        nc.gpsimd.indirect_dma_start(
                            out=rows[:, j, :], out_offset=None, in_=table[:, :],
                            in_offset=bass.IndirectOffsetOnAxis(ap=index[:, j:j + 1], axis=0)).then_inc(landed[j], 16)

                for h in range(2):
                    gather_half(0, h)
                with pool.Fori(1, loops) as g:
                    for h in range(2):
                        pool.wait_ge(summed, g * R + ((h + 1) * H - R))
                        gather_half(g, h)

            def anywhere():
                with pool.Fori(0, m.tiles) as w:
                    with pool.Fori(0, loops) as g:
                        pool.wait_ge(index_ready, w * loops + (g + 1))
                        nc.gpsimd.nop(nofuse=True)
                        for j in range(R):
                            nc.gpsimd.indirect_dma_start(
                                out=rows[:, j, :], out_offset=None, in_=table[:, :],
                                in_offset=bass.IndirectOffsetOnAxis(ap=index[:, j:j + 1], axis=0)).then_inc(landed[j], 16)

            branch(pool, in_windows, anywhere)

        @block.vector
        def _(dve):
            def in_windows():
                def make_hot(c, j):
                    nc.vector.tensor_scalar(hot[:, j, :], m.iota[:], m.dloc[:, ds(c, 1)], None,
                                            ALU.is_equal).then_inc(hot_ready, 1)

                for j in range(R):
                    make_hot(j, j)

                def add(c, j, base, first=False):
                    dve.wait_ge(summed, c + 1)
                    if not first:
                        dve.wait_ge(added, c)
                    window = m.agg[:, :, ds(base, WINDOW)]
                    nc.vector.tensor_tensor(window, window, part_ps(j), ALU.add).then_inc(added, 1)

                def bases(c):
                    _, values = nc.values_load_multi_w_load_instructions(
                        m.dst[0:1, ds(c, H)], engines=(dve.engine,), min_val=0, max_val=m.nodes - 1,
                        skip_runtime_bounds_check_because="targets are node numbers")
                    return values

                for h in range(2):
                    for j, base in enumerate(bases(h * H), h * H):
                        add(j, j, base, first=(j == 0))
                        make_hot(R + j, j)
                with dve.Fori(1, loops - 1) as g:
                    for h in range(2):
                        for j, base in enumerate(bases(g * R + h * H), h * H):
                            add(g * R + j, j, base)
                            make_hot((g + 1) * R + j, j)
                for h in range(2):
                    for j, base in enumerate(bases((loops - 1) * R + h * H), h * H):
                        add((loops - 1) * R + j, j, base)

            def anywhere():
                nc.vector.tensor_copy(places[:], m.iota[:]).then_inc(moved, 1)
                nc.vector.nop().then_inc(tile_free, 1)
                with dve.Fori(0, m.tiles) as w:
                    dve.wait_ge(moved, w + 1)
                    nc.vector.nop(nofuse=True)
                    with dve.Fori(0, loops) as g:
                        dve.wait_ge(group_free, w * loops + (g + 1))
                        for j in range(R):
                            nc.vector.tensor_scalar(hot[:, j, :], places[:], m.dst_f[:, ds(g * R + j, 1)], None,
                                                    ALU.is_equal).then_inc(hot_ready, 1)
                    dve.wait_ge(summed, w + 1)
                    tile = m.agg[:, :, ds(w * P, P)]
                    nc.vector.tensor_tensor(tile, tile, m.ps[:, 0:DK, 0:P], ALU.add).then_inc(tile_free, 1)
                    nc.vector.tensor_scalar(places[:], places[:], float(P), None, ALU.add).then_inc(moved, 1)

            branch(dve, in_windows, anywhere)

        @block.tensor
        def _(pe):
            def in_windows():
                def multiply(c, j, round_):
                    pe.wait_ge(landed[j], round_ * 16)
                    pe.wait_ge(hot_ready, c + 1)
                    for k in range(DK):
                        last = nc.tensor.matmul(part_ps(j)[:, k, :], rows[:, j, k * P:(k + 1) * P], hot[:, j, :],
                                                start=True, stop=True)
                    last.then_inc(summed, 1)

                for j in range(R):
                    if j >= B:
                        pe.wait_ge(added, j + 1 - B)
                    multiply(j, j, 1)
                with pe.Fori(1, loops) as g:
                    for j in range(R):
                        pe.wait_ge(added, g * R + (j + 1 - B))
                        multiply(g * R + j, j, g + 1)

            def anywhere():
                def group(w, g, first, last):
                    pe.wait_ge(hot_ready, (w * loops + g) * R + R)
                    for j in range(R):
                        pe.wait_ge(landed[j], (w * loops + (g + 1)) * 16)
                        for k in range(DK):
                            mm = nc.tensor.matmul(m.ps[:, k, 0:P], rows[:, j, k * P:(k + 1) * P], hot[:, j, :],
                                                  start=first and j == 0, stop=last and j == R - 1,
                                                  skip_group_check=True)
                    mm.then_inc(group_free, 1)
                    return mm

                nc.tensor.nop().then_inc(group_free, 1)
                with pe.Fori(0, m.tiles) as w:
                    pe.wait_ge(tile_free, w + 1)
                    group(w, 0, True, False)
                    with pe.Fori(1, loops - 1) as g:
                        group(w, g, False, False)
                    group(w, loops - 1, False, True)
                    nc.tensor.drain().then_inc(summed, 1)

            branch(pe, in_windows, anywhere)


def update_nodes(nc, m, tag, w, bias, table):
    R = TILE_RING
    with Stage(nc) as ctx:
        sem = lambda name: ctx.sem(f"{tag}_{name}")
        cols = ctx.enter_context(nc.sbuf_tensor(f"{tag}_cols", [P, R, DK, P], F32))
        biased = ctx.enter_context(nc.sbuf_tensor(f"{tag}_biased", [P, R, D], F32))
        rows = ctx.enter_context(nc.sbuf_tensor(f"{tag}_rows", [P, R, D], F32))
        cols_ready, multiplied, biased_ready, rows_ready = sem("cols"), sem("multiplied"), sem("biased"), sem("rows")
        turned, kept = sem("turned"), sem("kept")
        stored = [sem(f"stored{j}") for j in range(R)]
        block = ctx.enter_context(nc.Block())

        def product_ps(j):
            return m.ps[:, j, 0:D]

        def turned_ps(j):
            return m.ps[:, j, D:2 * D].rearrange("p (k n) -> p k n", k=DK)

        @block.gpsimd
        def _(pool):
            def fetch(t, j, again, round_):
                if again:
                    pool.wait_ge(multiplied, t + (1 - R))
                    nc.gpsimd.nop(nofuse=True)
                nc.gpsimd.tensor_copy(cols[:, j, :, :], m.agg[:, :, ds(t * P, P)]).then_inc(cols_ready, 1)
            tile_loop(pool, m.tiles, [(0, fetch)])

        @block.tensor
        def _(pe):
            def multiply(t, j, again, round_):
                pe.wait_ge(cols_ready, t + 1)
                if again:
                    pe.wait_ge(kept, t + (1 - R))
                for k in range(DK):
                    last = nc.tensor.matmul(product_ps(j), cols[:, j, k, :], w[:, k, :], start=(k == 0),
                                            stop=(k == DK - 1))
                last.then_inc(multiplied, 1)

            def turn(t, j, again, round_):
                pe.wait_ge(rows_ready, t + 1)
                for k in range(DK):
                    last = nc.tensor.transpose(turned_ps(j)[:, k, :], rows[:, j, k * P:(k + 1) * P], m.ident[:])
                last.then_inc(turned, 1)
            tile_loop(pe, m.tiles, [(0, multiply), (3, turn)])

        @block.vector
        def _(dve):
            def add_bias(t, j, again, round_):
                dve.wait_ge(multiplied, t + 1)
                if again:
                    dve.wait_ge(rows_ready, t + (1 - R))
                nc.vector.scalar_tensor_tensor(biased[:, j, :], product_ps(j), m.dinv[:, ds(t, 1)], bias[:],
                                               ALU.mult, ALU.add).then_inc(biased_ready, 1)

            def keep(t, j, again, round_):
                dve.wait_ge(turned, t + 1)
                nc.vector.tensor_copy(m.agg[:, :, ds(t * P, P)], turned_ps(j)).then_inc(kept, 1)
            tile_loop(dve, m.tiles, [(0, add_bias), (4, keep)])

        @block.scalar
        def _(act):
            def rectify(t, j, again, round_):
                act.wait_ge(biased_ready, t + 1)
                if again:
                    act.wait_ge(turned, t + (1 - R))
                    act.wait_ge(stored[j], round_ * 16)
                nc.scalar.activation(rows[:, j, :], biased[:, j, :], ACT.Relu,
                                     scale=m.dinv[:, ds(t, 1)]).then_inc(rows_ready, 1)
            tile_loop(act, m.tiles, [(0, rectify)])

        @block.sync
        def _(sp):
            def store(t, j, again, round_):
                sp.wait_ge(rows_ready, t + 1)
                sp.dma_start(table[ds(t * P, P), :], rows[:, j, :]).then_inc(stored[j], 16)
            tile_loop(sp, m.tiles, [(0, store)])
            for j in range(R):
                sp.wait_ge(stored[j], m.tiles // R * 16)


def finish_gcn(nc, m, tag):
    R = TILE_RING
    with Stage(nc) as ctx:
        sem = lambda name: ctx.sem(f"{tag}_{name}")
        cols = ctx.enter_context(nc.sbuf_tensor(f"{tag}_cols", [P, R, DK, P], F32))
        biased = ctx.enter_context(nc.sbuf_tensor(f"{tag}_biased", [P, R, P], F32))
        rows = ctx.enter_context(nc.sbuf_tensor(f"{tag}_rows", [P, R, P], F32))
        turned = ctx.enter_context(nc.sbuf_tensor(f"{tag}_turned", [P, R, P], F32))
        cols_ready, multiplied, biased_ready, rows_ready = sem("cols"), sem("multiplied"), sem("biased"), sem("rows")
        turn_done, turned_ready, projected, x_biased, added = (sem("turn_done"), sem("turned"), sem("projected"),
                                                               sem("x_biased"), sem("added"))
        block = ctx.enter_context(nc.Block())

        @block.gpsimd
        def _(pool):
            def fetch(t, j, again, round_):
                if again:
                    pool.wait_ge(multiplied, t + (1 - R))
                    nc.gpsimd.nop(nofuse=True)
                nc.gpsimd.tensor_copy(cols[:, j, :, :], m.agg[:, :, ds(t * P, P)]).then_inc(cols_ready, 1)
            tile_loop(pool, m.tiles, [(0, fetch)])

        @block.tensor
        def _(pe):
            def multiply(t, j, again, round_):
                pe.wait_ge(cols_ready, t + 1)
                if again:
                    pe.wait_ge(added, t + (1 - R))
                for k in range(DK):
                    last = nc.tensor.matmul(m.ps[:, j, 0:P], cols[:, j, k, :], m.w3[:, k, :], start=(k == 0),
                                            stop=(k == DK - 1))
                last.then_inc(multiplied, 1)

            def turn(t, j, again, round_):
                pe.wait_ge(rows_ready, t + 1)
                nc.tensor.transpose(m.ps[:, j, P:2 * P], rows[:, j, :], m.ident[:]).then_inc(turn_done, 1)

            def project(t, j, again, round_):
                pe.wait_ge(turned_ready, t + 1)
                nc.tensor.matmul(m.ps[:, j, D:2 * D], turned[:, j, :], m.wp[:], start=True,
                                 stop=True).then_inc(projected, 1)
            tile_loop(pe, m.tiles, [(0, multiply), (2, turn), (4, project)])

        @block.vector
        def _(dve):
            def add_bias(t, j, again, round_):
                dve.wait_ge(multiplied, t + 1)
                if again:
                    dve.wait_ge(rows_ready, t + (1 - R))
                nc.vector.scalar_tensor_tensor(biased[:, j, :], m.ps[:, j, 0:P], m.dinv[:, ds(t, 1)], m.b3[:],
                                               ALU.mult, ALU.add).then_inc(biased_ready, 1)
                nc.vector.tensor_tensor(tile_of(m.x, t), tile_of(m.x, t), m.bp[:], ALU.add).then_inc(x_biased, 1)

            def add(t, j, again, round_):
                dve.wait_ge(projected, t + 1)
                dve.wait_ge(x_biased, t + 1)
                nc.vector.tensor_tensor(tile_of(m.x, t), tile_of(m.x, t), m.ps[:, j, D:2 * D],
                                        ALU.add).then_inc(added, 1)
            tile_loop(dve, m.tiles, [(0, add_bias), (5, add)])

        @block.scalar
        def _(act):
            def rectify(t, j, again, round_):
                act.wait_ge(biased_ready, t + 1)
                if again:
                    act.wait_ge(turn_done, t + (1 - R))
                nc.scalar.activation(rows[:, j, :], biased[:, j, :], ACT.Relu).then_inc(rows_ready, 1)

            def keep(t, j, again, round_):
                act.wait_ge(turn_done, t + 1)
                if again:
                    act.wait_ge(projected, t + (1 - R))
                nc.scalar.copy(turned[:, j, :], m.ps[:, j, P:2 * P]).then_inc(turned_ready, 1)
            tile_loop(act, m.tiles, [(0, rectify), (2, keep)])


def mask_pads(nc, m, tag):
    with Stage(nc) as ctx:
        block = ctx.enter_context(nc.Block())

        @block.gpsimd
        def _(pool):
            nc.gpsimd.affine_select(out=m.x[:, m.full_tiles, :], in_=m.x[:, m.full_tiles, :], compare_op=ALU.is_ge,
                                    fill=0.0, base=m.tail_nodes - 1, pattern=[[0, D]], channel_multiplier=-1)


def route_all(nc, m, a):
    E = m.experts
    capacity = float(ceil_div(m.nodes * 5, 4 * E))
    with Stage(nc) as ctx:
        sem = lambda name: ctx.sem(f"route_{name}")
        buf = lambda name, shape, dt=F32: ctx.enter_context(nc.sbuf_tensor(f"route_{name}", shape, dt))
        wr, br, mean_col = buf("wr", [P, DK, E]), buf("br", [1, E]), buf("mean_col", [P, DK])
        row, tmp, prob = buf("row", [1, E]), buf("tmp", [1, E]), buf("prob", [1, E])
        over, ratio, expd = buf("over", [1, E]), buf("ratio", [1, E]), buf("expd", [1, E])
        rev_i, rev = buf("rev_i", [1, E], I32), buf("rev", [1, E])
        peak, total, inv = buf("peak", [1, 4]), buf("total", [1, 2]), buf("inv", [1, 2])
        top, code = buf("top", [1, 2]), buf("code", [1, 2])
        choice_f, choice, share = buf("choice_f", [1, 2]), buf("choice", [1, 2], I32), buf("share", [1, 4])
        shares, b2_rows = buf("shares", [P, 2]), buf("b2_rows", [P, 2, D])
        loaded, turned, col_ready, scored = sem("loaded"), sem("turned"), sem("col_ready"), sem("scored")
        chain, exp_asked, exp_done, rev_made = sem("chain"), sem("exp_asked"), sem("exp_done"), sem("rev_made")
        chosen, share_ready, spread, fetched = sem("chosen"), sem("share_ready"), sem("spread"), sem("fetched")
        block = ctx.enter_context(nc.Block())

        @block.sync
        def _(sp):
            sp.dma_start(wr[:], a["ffn0_wr"].rearrange("(k p) e -> p k e", p=P)).then_inc(loaded, 16)
            sp.dma_start(br[:], a["ffn0_br"].rearrange("(o e) -> o e", o=1)).then_inc(loaded, 16)
            sp.wait_ge(chosen, 1)
            for n in range(2):
                e = sp.value_load(choice[0:1, n:n + 1], min_val=0, max_val=E - 1)
                sp.dma_start(m.f0_w1[:, n, :, :], a["ffn0_w1"][ds(e, 1), :, :]
                             .rearrange("o (k p) f -> p (o k) f", p=P)).then_inc(fetched, 16)
                sp.dma_start(m.f0_w2[:, n, :, :], a["ffn0_w2"][ds(e, 1), :, :]
                             .rearrange("o (k p) f -> p (o k) f", p=P)).then_inc(fetched, 16)
                sp.dma_start(m.f0_b1[:, n, :], a["ffn0_b1"][ds(e, 1), :, :]
                             .rearrange("o p f -> p (o f)")).then_inc(fetched, 16)
                sp.dma_start(b2_rows[:, n, :], a["ffn0_b2"][ds(e, 1), :]
                             .rearrange("o d -> (o d)").partition_broadcast(P)).then_inc(fetched, 16)
            sp.dma_start(m.gamma[:], a["ffn0_gamma"].partition_broadcast(P)).then_inc(fetched, 16)
            sp.dma_start(m.beta[:], a["ffn0_beta"].partition_broadcast(P)).then_inc(fetched, 16)
            sp.wait_ge(fetched, 16 * 10)

        @block.gpsimd
        def _(pool):
            nc.gpsimd.iota(rev_i[:], pattern=[[-1, E]], base=E, channel_multiplier=0).then_inc(rev_made, 1)

        @block.tensor
        def _(pe):
            for k in range(DK):
                last = nc.tensor.matmul(m.ps[:, 0, k:k + 1], m.mean_row[0:1, k * P:(k + 1) * P], m.ones[0:1, 0:1],
                                        start=True, stop=True)
            last.then_inc(turned, 1)
            pe.wait_ge(col_ready, 1)
            pe.wait_ge(loaded, 32)
            for k in range(DK):
                last = nc.tensor.matmul(m.ps[0:1, 1, 0:E], mean_col[:, k:k + 1], wr[:, k, :], start=(k == 0),
                                        stop=(k == DK - 1))
            last.then_inc(scored, 1)
            pe.wait_ge(share_ready, 1)
            nc.tensor.matmul(m.ps[:, 2, 0:2], m.ones[0:1, :], share[0:1, 2:4], start=True, stop=True).then_inc(spread, 1)

        @block.scalar
        def _(act):
            for n in range(2):
                act.wait_ge(exp_asked, n + 1)
                nc.scalar.activation(expd[:], row[:], ACT.Exp, bias=peak[0:1, n:n + 1],
                                     accum_out=total[0:1, n:n + 1]).then_inc(exp_done, 1)
            act.wait_ge(exp_asked, 3)
            nc.scalar.activation(share[0:1, 1:2], share[0:1, 0:1], ACT.Exp).then_inc(exp_done, 1)

        @block.vector
        def _(dve):
            links = [0]

            def link(ins):
                links[0] += 1
                ins.then_inc(chain, 1)
                dve.wait_ge(chain, links[0])

            def softmax(n, out):
                link(nc.vector.reduce_max(peak[0:1, 2:3], row[:], AX.X))
                nc.vector.tensor_scalar(peak[0:1, n:n + 1], peak[0:1, 2:3], -1.0, None, ALU.mult).then_inc(exp_asked, 1)
                dve.wait_ge(exp_done, n + 1)
                link(nc.vector.reciprocal(inv[0:1, n:n + 1], total[0:1, n:n + 1]))
                link(nc.vector.tensor_scalar(out, expd[:], inv[0:1, n:n + 1], None, ALU.mult))

            dve.wait_ge(turned, 1)
            nc.vector.tensor_copy(mean_col[:], m.ps[:, 0, 0:DK]).then_inc(col_ready, 1)
            dve.wait_ge(rev_made, 1)
            nc.vector.tensor_copy(rev[:], rev_i[:])
            dve.wait_ge(scored, 1)
            link(nc.vector.tensor_tensor(row[:], m.ps[0:1, 1, 0:E], br[:], ALU.add))
            softmax(0, prob[:])
            link(nc.vector.tensor_scalar(tmp[:], prob[:], float(m.nodes), None, ALU.mult))
            link(nc.vector.tensor_scalar(over[:], tmp[:], capacity, None, ALU.is_gt))
            link(nc.vector.tensor_scalar(tmp[:], tmp[:], capacity, None, ALU.max))
            link(nc.vector.reciprocal(ratio[:], tmp[:]))
            link(nc.vector.scalar_tensor_tensor(ratio[:], ratio[:], capacity, over[:], ALU.mult, ALU.mult))
            link(nc.vector.tensor_scalar(over[:], over[:], -1.0, 1.0, ALU.mult, ALU.add))
            link(nc.vector.tensor_tensor(ratio[:], ratio[:], over[:], ALU.add))
            link(nc.vector.tensor_tensor(row[:], prob[:], ratio[:], ALU.mult))
            softmax(1, prob[:])
            for n in range(2):
                link(nc.vector.reduce_max(top[0:1, n:n + 1], prob[:], AX.X))
                link(nc.vector.tensor_scalar(tmp[:], prob[:], top[0:1, n:n + 1], None, ALU.is_equal))
                link(nc.vector.tensor_tensor(tmp[:], tmp[:], rev[:], ALU.mult))
                link(nc.vector.reduce_max(code[0:1, n:n + 1], tmp[:], AX.X))
                if n == 0:
                    link(nc.vector.tensor_scalar(tmp[:], rev[:], code[0:1, 0:1], -2.0, ALU.is_equal, ALU.mult))
                    link(nc.vector.tensor_tensor(prob[:], prob[:], tmp[:], ALU.add))
            link(nc.vector.tensor_scalar(choice_f[:], code[:], -1.0, float(E), ALU.mult, ALU.add))
            nc.vector.tensor_copy(choice[:], choice_f[:]).then_inc(chosen, 1)
            nc.vector.tensor_tensor(share[0:1, 0:1], top[0:1, 1:2], top[0:1, 0:1], ALU.subtract).then_inc(exp_asked, 1)
            dve.wait_ge(exp_done, 3)
            link(nc.vector.tensor_scalar(inv[0:1, 0:1], share[0:1, 1:2], 1.0, None, ALU.add))
            link(nc.vector.reciprocal(share[0:1, 2:3], inv[0:1, 0:1]))
            nc.vector.tensor_tensor(share[0:1, 3:4], share[0:1, 1:2], share[0:1, 2:3], ALU.mult).then_inc(share_ready, 1)
            dve.wait_ge(spread, 1)
            link(nc.vector.tensor_copy(shares[:], m.ps[:, 2, 0:2]))
            dve.wait_ge(fetched, 16 * 10)
            for n in range(2):
                w2 = m.f0_w2[:, n, :, :]
                nc.vector.tensor_scalar(w2, w2, shares[:, n:n + 1], None, ALU.mult)
            link(nc.vector.tensor_scalar(m.f0_b2[:], b2_rows[:, 0, :], shares[:, 0:1], None, ALU.mult))
            nc.vector.scalar_tensor_tensor(m.f0_b2[:], b2_rows[:, 1, :], shares[:, 1:2], m.f0_b2[:],
                                           ALU.mult, ALU.add)


def two_experts(nc, m):
    T = 4
    F = 2 * m.hidden0 // P
    chunks = m.tiles // T
    assert m.tiles % T == 1 and chunks % 2 == 0
    with Stage(nc) as ctx:
        sem = lambda name: ctx.sem(f"two_{name}")
        hid = ctx.enter_context(nc.sbuf_tensor("two_hid", [P, 2, F, T * P], F32))
        own = ctx.enter_context(nc.sbuf_tensor("two_own", [P, T, D], F32))
        up_done, gelu_done, down_done = sem("up"), sem("gelu"), sem("down")
        own_made, own_biased, added = sem("own_made"), sem("own_biased"), sem("added")
        block = ctx.enter_context(nc.Block())

        @block.tensor
        def _(pe):
            def up(c, half, first, width):
                for f in range(F):
                    if not first or f >= 4:
                        pe.wait_ge(gelu_done, c * F + (f - 3))
                    for k in range(DK):
                        last = nc.tensor.matmul(m.ps[:, f % 4, 0:width],
                                                m.f0_w1[:, f // (F // 2), k, (f % (F // 2)) * P:(f % (F // 2) + 1) * P],
                                                m.agg[:, k, ds(c * T * P, width)], start=(k == 0), stop=(k == DK - 1))
                    last.then_inc(up_done, 1)

            def down(c, half, first, tiles):
                pe.wait_ge(gelu_done, (c + 1) * F)
                for i in range(tiles):
                    if not first:
                        pe.wait_ge(added, c * T + (i + 1 - T))
                    for f in range(F):
                        last = nc.tensor.matmul(m.ps[:, 4 + i, 0:D], hid[:, half, f, i * P:(i + 1) * P],
                                                m.f0_w2[:, f // (F // 2), f % (F // 2), :], start=(f == 0),
                                                stop=(f == F - 1))
                    last.then_inc(down_done, 1)

            up(0, 0, True, T * P)
            up(1, 1, False, T * P)
            down(0, 0, True, T)
            with pe.Fori(1, chunks // 2) as g:
                up(g * 2, 0, False, T * P)
                down(g * 2 - 1, 1, False, T)
                up(g * 2 + 1, 1, False, T * P)
                down(g * 2, 0, False, T)
            up(chunks, 0, False, P)
            down(chunks - 1, 1, False, T)
            down(chunks, 0, False, 1)

        @block.scalar
        def _(act):
            def gelu(c, half, first, width):
                if not first:
                    act.wait_ge(down_done, (c - 1) * T)
                for f in range(F):
                    act.wait_ge(up_done, c * F + (f + 1))
                    nc.scalar.activation(hid[:, half, f, 0:width], m.ps[:, f % 4, 0:width], ACT.Gelu,
                                         bias=m.f0_b1[:, f // (F // 2), f % (F // 2):f % (F // 2) + 1])\
                        .then_inc(gelu_done, 1)
            gelu(0, 0, True, T * P)
            gelu(1, 1, True, T * P)
            with act.Fori(1, chunks // 2) as g:
                gelu(g * 2, 0, False, T * P)
                gelu(g * 2 + 1, 1, False, T * P)
            gelu(chunks, 0, False, P)

        @block.vector
        def _(dve):
            def combine(c, tiles, first=False):
                for i in range(tiles):
                    t = c * T + i
                    if not first:
                        dve.wait_ge(added, t + (1 - T))
                    nc.vector.tensor_scalar(own[:, i, :], tile_of(m.x, t), m.mv[:, ds(t, 1), 0], m.scale[:, ds(t, 1)],
                                            ALU.subtract, ALU.mult).then_inc(own_made, 1)
                for i in range(tiles):
                    t = c * T + i
                    dve.wait_ge(own_made, t + 1)
                    nc.vector.tensor_tensor(own[:, i, :], own[:, i, :], m.f0_b2[:], ALU.add).then_inc(own_biased, 1)
                for i in range(tiles):
                    t = c * T + i
                    dve.wait_ge(own_biased, t + 1)
                    dve.wait_ge(down_done, t + 1)
                    nc.vector.tensor_tensor(m.agg[:, :, ds(t * P, P)],
                                            own[:, i, :].rearrange("p (k n) -> p k n", k=DK),
                                            m.ps[:, 4 + i, 0:D].rearrange("p (k n) -> p k n", k=DK),
                                            ALU.add).then_inc(added, 1)
            combine(0, T, first=True)
            with dve.Fori(1, chunks) as c:
                combine(c, T)
            combine(chunks, 1)


def add_normalized(nc, m):
    R = TILE_RING
    with Stage(nc) as ctx:
        sem = lambda name: ctx.sem(f"addn_{name}")
        scaled = ctx.enter_context(nc.sbuf_tensor("addn_scaled", [P, R, D], F32))
        x_shifted, scaled_made, x_done = sem("x_shifted"), sem("scaled"), sem("x_done")
        block = ctx.enter_context(nc.Block())

        @block.gpsimd
        def _(pool):
            def shift(t, j, again, round_):
                nc.gpsimd.tensor_tensor(tile_of(m.x, t), tile_of(m.x, t), m.beta[:], ALU.add).then_inc(x_shifted, 1)
            tile_loop(pool, m.tiles, [(0, shift)])

        @block.vector
        def _(dve):
            def scale(t, j, again, round_):
                if again:
                    dve.wait_ge(x_done, t + (1 - R))
                nc.vector.scalar_tensor_tensor(scaled[:, j, :].rearrange("p (k n) -> p k n", k=DK),
                                               m.agg[:, :, ds(t * P, P)], m.mv[:, ds(t, 1), 0],
                                               m.gamma[:].rearrange("p (k n) -> p k n", k=DK),
                                               ALU.subtract, ALU.mult).then_inc(scaled_made, 1)

            def add(t, j, again, round_):
                dve.wait_ge(scaled_made, t + 1)
                dve.wait_ge(x_shifted, t + 1)
                nc.vector.scalar_tensor_tensor(tile_of(m.x, t), scaled[:, j, :], m.scale[:, ds(t, 1)],
                                               tile_of(m.x, t), ALU.mult, ALU.add).then_inc(x_done, 1)
            tile_loop(dve, m.tiles, [(0, scale), (1, add)])


def project_heads(nc, m, a, heads_table, left_table):
    R = TILE_RING
    H = m.heads
    with Stage(nc) as ctx:
        sem = lambda name: ctx.sem(f"proj_{name}")
        buf = lambda name, shape, dt=F32: ctx.enter_context(nc.sbuf_tensor(f"proj_{name}", shape, dt))
        w, attn, prod = buf("w", [P, DK, D + 2 * H]), buf("attn", [P, 2, D]), buf("prod", [P, D])
        ring, cols, out = buf("ring", [P, R, D]), buf("cols", [P, R, DK, P]), buf("out", [P, R, D + 2 * H])
        loaded, prod_made, wa_made = sem("loaded"), sem("prod_made"), sem("wa_made")
        rows_ready, turned, cols_ready, multiplied = sem("rows"), sem("turned"), sem("cols"), sem("multiplied")
        heads_kept = sem("heads_kept")
        stored = [sem(f"stored{j}") for j in range(R)]
        block = ctx.enter_context(nc.Block())

        @block.sync
        def _(sp):
            sp.dma_start(w[:, :, 0:D], a["gat_w"].rearrange("(k p) n -> p k n", p=P)).then_inc(loaded, 16)
            sp.dma_start(attn[:, 0, :], a["gat_l"].rearrange("h d -> (h d)").partition_broadcast(P)).then_inc(loaded, 16)
            sp.dma_start(attn[:, 1, :], a["gat_r"].rearrange("h d -> (h d)").partition_broadcast(P)).then_inc(loaded, 16)

            def store(t, j, again, round_):
                sp.wait_ge(heads_kept, t + 1)
                sp.dma_start(heads_table[ds(t * P, P), :], out[:, j, 0:D + H]).then_inc(stored[j], 16)
                sp.dma_start(left_table[ds(t * P, P), :], out[:, j, D + H:D + 2 * H]).then_inc(stored[j], 16)
            tile_loop(sp, m.tiles, [(0, store)])
            for j in range(R):
                sp.wait_ge(stored[j], m.tiles // R * 32)

        @block.vector
        def _(dve):
            dve.wait_ge(loaded, 48)
            for n, side in enumerate((1, 0)):
                for k in range(DK):
                    s = n * DK + k
                    if s:
                        dve.wait_ge(wa_made, s)
                    nc.vector.tensor_tensor(prod[:], w[:, k, 0:D], attn[:, side, :], ALU.mult).then_inc(prod_made, 1)
                    dve.wait_ge(prod_made, s + 1)
                    nc.vector.reduce_sum(w[:, k, D + n * H:D + (n + 1) * H], prod[:].rearrange("p (h d) -> p h d", h=H),
                                         AX.X).then_inc(wa_made, 1)

            def rows(t, j, again, round_):
                if again:
                    dve.wait_ge(turned, t + (1 - R))
                nc.vector.tensor_scalar(ring[:, j, :], tile_of(m.x, t), m.mv[:, ds(t, 1), 0], m.scale[:, ds(t, 1)],
                                        ALU.subtract, ALU.mult).then_inc(rows_ready, 1)

            tile_loop(dve, m.tiles, [(0, rows)])

        @block.scalar
        def _(act):
            def keep_cols(t, j, again, round_):
                act.wait_ge(turned, t + 1)
                if again:
                    act.wait_ge(multiplied, t + (1 - R))
                nc.scalar.copy(cols[:, j, :, :],
                               m.ps[:, j, 0:D].rearrange("p (k n) -> p k n", k=DK)).then_inc(cols_ready, 1)

            def keep_heads(t, j, again, round_):
                act.wait_ge(multiplied, t + 1)
                if again:
                    act.wait_ge(stored[j], round_ * 32)
                nc.scalar.copy(out[:, j, :], m.ps[:, j, 0:D + 2 * H]).then_inc(heads_kept, 1)
            tile_loop(act, m.tiles, [(0, keep_cols), (2, keep_heads)])

        @block.tensor
        def _(pe):
            def turn(t, j, again, round_):
                pe.wait_ge(rows_ready, t + 1)
                if again:
                    pe.wait_ge(heads_kept, t + (1 - R))
                for k in range(DK):
                    last = nc.tensor.transpose(m.ps[:, j, k * P:(k + 1) * P], ring[:, j, k * P:(k + 1) * P], m.ident[:])
                last.then_inc(turned, 1)

            def multiply(t, j, again, round_):
                pe.wait_ge(cols_ready, t + 1)
                for k in range(DK):
                    last = nc.tensor.matmul(m.ps[:, j, 0:D + 2 * H], cols[:, j, k, :], w[:, k, :], start=(k == 0),
                                            stop=(k == DK - 1))
                last.then_inc(multiplied, 1)

            pe.wait_ge(wa_made, 2 * DK)
            tile_loop(pe, m.tiles, [(0, turn), (2, multiply)])


def attend(nc, m, heads_table, left_table):
    R = TILE_RING
    H = m.heads
    with Stage(nc) as ctx:
        sem = lambda name: ctx.sem(f"att_{name}")
        buf = lambda name, shape, dt=F32: ctx.enter_context(nc.sbuf_tensor(f"att_{name}", shape, dt))
        src_col, dst_col = buf("src_col", [P, R], I32), buf("dst_col", [P, R], I32)
        rows, left = buf("rows", [P, R, D + H]), buf("left", [P, R, H])
        score, flat, peak = buf("score", [P, R, H]), buf("flat", [P, R, H]), buf("peak", [P, R])
        weight, total, inv = buf("weight", [P, R, H]), buf("total", [P, R]), buf("inv", [P, R])
        prod, head_sum = buf("prod", [P, R, D]), buf("head_sum", [P, R, D // H])
        index_ready, chain, scores_ready, exp_done, used = (sem("index_ready"), sem("chain"), sem("scores_ready"),
                                                            sem("exp_done"), sem("used"))
        landed = [sem(f"landed{j}") for j in range(R)]
        block = ctx.enter_context(nc.Block())

        @block.scalar
        def _(act):
            def put_index(t, j, again, round_):
                if again:
                    act.wait_ge(landed[j], round_ * 32)
                nc.scalar.copy(src_col[:, j:j + 1], m.src[:, ds(t, 1)]).then_inc(index_ready, 1)
                nc.scalar.copy(dst_col[:, j:j + 1], m.dst[:, ds(t, 1)]).then_inc(index_ready, 1)

            def exps(t, j, again, round_):
                act.wait_ge(scores_ready, t + 1)
                if again:
                    act.wait_ge(used, t + (1 - R))
                nc.scalar.activation(weight[:, j, :], score[:, j, :], ACT.Exp, bias=peak[:, j:j + 1],
                                     accum_out=total[:, j:j + 1]).then_inc(exp_done, 1)
            tile_loop(act, m.tiles, [(0, put_index), (5, exps)])

        @block.gpsimd
        def _(pool):
            def gather(t, j, again, round_):
                pool.wait_ge(index_ready, t * 2 + 2)
                if again:
                    pool.wait_ge(used, t + (1 - R))
                nc.gpsimd.nop(nofuse=True)
                nc.gpsimd.indirect_dma_start(
                    out=rows[:, j, :], out_offset=None, in_=heads_table[:, :],
                    in_offset=bass.IndirectOffsetOnAxis(ap=dst_col[:, j:j + 1], axis=0)).then_inc(landed[j], 16)
                nc.gpsimd.indirect_dma_start(
                    out=left[:, j, :], out_offset=None, in_=left_table[:, :],
                    in_offset=bass.IndirectOffsetOnAxis(ap=src_col[:, j:j + 1], axis=0)).then_inc(landed[j], 16)
            tile_loop(pool, m.tiles, [(0, gather)])

        @block.vector
        def _(dve):
            STEPS = 7

            def scores(t, j, again, round_):
                dve.wait_ge(landed[j], (round_ + 1) * 32)
                nc.vector.tensor_tensor(flat[:, j, :], left[:, j, :], rows[:, j, D:D + H], ALU.add).then_inc(chain, 1)

            def leak(t, j, again, round_):
                dve.wait_ge(chain, 1 + t)
                nc.vector.scalar_tensor_tensor(score[:, j, :], flat[:, j, :], 0.01, flat[:, j, :], ALU.mult,
                                               ALU.max).then_inc(leaked, 1)

            def peaks(t, j, again, round_):
                dve.wait_ge(leaked, 1 + t)
                nc.vector.tensor_reduce(peak[:, j:j + 1], score[:, j, :], AX.X, ALU.max,
                                        negate=True).then_inc(scores_ready, 1)

            def weigh(t, j, again, round_):
                dve.wait_ge(exp_done, t + 1)
                nc.vector.reciprocal(inv[:, j:j + 1], total[:, j:j + 1]).then_inc(inverted, 1)
                nc.vector.tensor_tensor(prod[:, j, :].rearrange("p (h d) -> p h d", h=H),
                                        rows[:, j, 0:D].rearrange("p (h d) -> p h d", h=H),
                                        weight[:, j, :].unsqueeze(2).to_broadcast([P, H, D // H]),
                                        ALU.mult).then_inc(weighed, 1)

            def sum_heads(t, j, again, round_):
                dve.wait_ge(weighed, t + 1)
                nc.vector.reduce_sum(head_sum[:, j, :], prod[:, j, :].rearrange("p (h d) -> p d h", h=H),
                                     AX.X).then_inc(head_summed, 1)

            def add(t, j, again, round_):
                dve.wait_ge(head_summed, t + 1)
                dve.wait_ge(inverted, t + 1)
                xt = tile_of(m.x, t).rearrange("p (h d) -> p h d", h=H)
                nc.vector.scalar_tensor_tensor(xt, head_sum[:, j, :].unsqueeze(1).to_broadcast([P, H, D // H]),
                                               inv[:, j:j + 1], xt, ALU.mult, ALU.add).then_inc(used, 1)

            leaked, inverted, weighed, head_summed = sem("leaked"), sem("inverted"), sem("weighed"), sem("head_summed")
            tile_loop(dve, m.tiles, [(0, scores), (0, leak), (0, peaks), (1, weigh), (1, sum_heads), (1, add)])


def score_experts(nc, m, a):
    R = TILE_RING
    E = m.experts
    with Stage(nc) as ctx:
        sem = lambda name: ctx.sem(f"gate_{name}")
        buf = lambda name, shape, dt=F32: ctx.enter_context(nc.sbuf_tensor(f"gate_{name}", shape, dt))
        w, b = buf("w", [P, DK, E]), buf("b", [P, E])
        ring, cols = buf("ring", [P, R, D]), buf("cols", [P, R, DK, P])
        loaded, rows_ready, turned, cols_ready = sem("loaded"), sem("rows"), sem("turned"), sem("cols")
        multiplied, kept = sem("multiplied"), sem("kept")
        block = ctx.enter_context(nc.Block())

        @block.sync
        def _(sp):
            sp.dma_start(w[:], a["gate_w"].rearrange("(k p) n -> p k n", p=P)).then_inc(loaded, 16)
            sp.dma_start(b[:], a["gate_b"].partition_broadcast(P)).then_inc(loaded, 16)

        @block.vector
        def _(dve):
            def rows(t, j, again, round_):
                if again:
                    dve.wait_ge(turned, t + (1 - R))
                nc.vector.tensor_scalar(ring[:, j, :], tile_of(m.x, t), m.mv[:, ds(t, 1), 0], m.scale[:, ds(t, 1)],
                                        ALU.subtract, ALU.mult).then_inc(rows_ready, 1)

            def keep(t, j, again, round_):
                dve.wait_ge(multiplied, t + 1)
                nc.vector.tensor_tensor(tile_of(m.gates, t), m.ps[:, j, D:D + E], b[:],
                                        ALU.add).then_inc(kept, 1)
            dve.wait_ge(loaded, 32)
            tile_loop(dve, m.tiles, [(0, rows), (4, keep)])

        @block.scalar
        def _(act):
            def keep_cols(t, j, again, round_):
                act.wait_ge(turned, t + 1)
                if again:
                    act.wait_ge(multiplied, t + (1 - R))
                nc.scalar.copy(cols[:, j, :, :],
                               m.ps[:, j, 0:D].rearrange("p (k n) -> p k n", k=DK)).then_inc(cols_ready, 1)
            tile_loop(act, m.tiles, [(0, keep_cols)])

        @block.tensor
        def _(pe):
            def turn(t, j, again, round_):
                pe.wait_ge(rows_ready, t + 1)
                if again:
                    pe.wait_ge(kept, t + (1 - R))
                for k in range(DK):
                    last = nc.tensor.transpose(m.ps[:, j, k * P:(k + 1) * P], ring[:, j, k * P:(k + 1) * P], m.ident[:])
                last.then_inc(turned, 1)

            def multiply(t, j, again, round_):
                pe.wait_ge(cols_ready, t + 1)
                for k in range(DK):
                    last = nc.tensor.matmul(m.ps[:, j, D:D + E], cols[:, j, k, :], w[:, k, :],
                                            start=(k == 0), stop=(k == DK - 1))
                last.then_inc(multiplied, 1)
            pe.wait_ge(loaded, 32)
            tile_loop(pe, m.tiles, [(0, turn), (2, multiply)])


def assign_slots(nc, m):
    E, T, C = m.experts, m.tiles, m.capacity
    with Stage(nc) as ctx:
        sem = lambda name: ctx.sem(f"slot_{name}")
        buf = lambda name, shape, dt=F32: ctx.enter_context(nc.sbuf_tensor(f"slot_{name}", shape, dt))
        peak, total, code = buf("peak", [P, T]), buf("total", [P, T]), buf("code", [P, T])
        low, one_hot = buf("low", [P, T, E]), buf("one_hot", [P, T, E])
        rev_i, rev = buf("rev_i", [P, E], I32), buf("rev", [P, E])
        upper = buf("upper", [P, P])
        sums = buf("sums", [P, 2, T, E])
        totals, place, kept_f = buf("totals", [P, T, E]), buf("place", [P, T]), buf("kept_f", [P, T])
        first, to, back = buf("first", [P, T]), buf("to", [P, T]), buf("back", [P, T])
        chain, rev_made, upper_made, low_ready, exp_done = (sem("chain"), sem("rev_made"), sem("upper_made"),
                                                            sem("low_ready"), sem("exp_done"))
        hot_ready, counted, to_ready, to_masked = sem("hot_ready"), sem("counted"), sem("to_ready"), sem("to_masked")
        block = ctx.enter_context(nc.Block())
        wide = lambda v: v.unsqueeze(2).to_broadcast([P, T, E])
        flat = lambda v: v.rearrange("p t e -> p (t e)")

        @block.gpsimd
        def _(pool):
            nc.gpsimd.iota(rev_i[:], pattern=[[-1, E]], base=E, channel_multiplier=0).then_inc(rev_made, 1)
            nc.gpsimd.memset(upper[:], 1.0).then_inc(rev_made, 1)
            pool.wait_ge(rev_made, 2)
            nc.gpsimd.affine_select(out=upper[:], in_=upper[:], compare_op=ALU.is_ge, fill=0.0, base=0,
                                    pattern=[[1, P]], channel_multiplier=-1).then_inc(upper_made, 1)
            pool.wait_ge(to_ready, 1)
            nc.gpsimd.affine_select(out=to[:, T - 1:T], in_=to[:, T - 1:T], compare_op=ALU.is_ge,
                                    fill=float(4 * E * C), base=m.tail_nodes - 1, pattern=[[0, 1]],
                                    channel_multiplier=-1).then_inc(to_masked, 1)

        @block.scalar
        def _(act):
            act.wait_ge(low_ready, 1)
            nc.scalar.activation(low[:], low[:], ACT.Exp).then_inc(exp_done, 1)

        @block.tensor
        def _(pe):
            pe.wait_ge(hot_ready, 1)
            pe.wait_ge(upper_made, 1)
            nc.tensor.matmul(m.ps[:, 0, 0:T * E], upper[:], flat(one_hot[:]), start=True, stop=True)
            nc.tensor.matmul(m.ps[:, 1, 0:T * E], m.ones[:], flat(one_hot[:]), start=True, stop=True).then_inc(counted, 1)

        @block.vector
        def _(dve):
            links = [0]

            def link(ins):
                links[0] += 1
                ins.then_inc(chain, 1)
                dve.wait_ge(chain, links[0])

            dve.wait_ge(rev_made, 1)
            link(nc.vector.tensor_copy(rev[:], rev_i[:]))
            revs = rev[:].unsqueeze(1).to_broadcast([P, T, E])
            link(nc.vector.reduce_max(peak[:], m.gates[:], AX.X))
            nc.vector.tensor_tensor(low[:], m.gates[:], wide(peak[:]), ALU.subtract).then_inc(low_ready, 1)
            link(nc.vector.tensor_tensor(one_hot[:], m.gates[:], wide(peak[:]), ALU.is_equal))
            link(nc.vector.tensor_tensor(one_hot[:], one_hot[:], revs, ALU.mult))
            link(nc.vector.reduce_max(code[:], one_hot[:], AX.X))
            nc.vector.tensor_tensor(one_hot[:], revs, wide(code[:]), ALU.is_equal).then_inc(hot_ready, 1)
            nc.vector.tensor_scalar(first[:], code[:], -float(C), float(E * C), ALU.mult, ALU.add)
            dve.wait_ge(exp_done, 1)
            link(nc.vector.reduce_sum(total[:], low[:], AX.X))
            link(nc.vector.reciprocal(m.prob[:], total[:]))
            dve.wait_ge(counted, 1)
            link(nc.vector.tensor_copy(flat(totals[:]), m.ps[:, 1, 0:T * E]))
            link(nc.vector.tensor_copy(sums[:, 0, :, :], totals[:]))
            now, step = 0, 1
            while step < T:
                nc.vector.tensor_copy(sums[:, 1 - now, 0:step, :], sums[:, now, 0:step, :])
                link(nc.vector.tensor_tensor(sums[:, 1 - now, step:T, :], sums[:, now, step:T, :],
                                             sums[:, now, 0:T - step, :], ALU.add))
                now, step = 1 - now, 2 * step
            link(nc.vector.tensor_tensor(totals[:], sums[:, now, :, :], totals[:], ALU.subtract))
            link(nc.vector.tensor_tensor(flat(totals[:]), flat(totals[:]), m.ps[:, 0, 0:T * E], ALU.add))
            link(nc.vector.tensor_tensor(totals[:], totals[:], one_hot[:], ALU.mult))
            link(nc.vector.reduce_sum(place[:], totals[:], AX.X))
            link(nc.vector.tensor_scalar(place[:], place[:], -1.0, None, ALU.add))
            link(nc.vector.tensor_scalar(kept_f[:], place[:], float(C), None, ALU.is_lt))
            link(nc.vector.tensor_tensor(first[:], first[:], place[:], ALU.add))
            link(nc.vector.tensor_scalar(place[:], kept_f[:], -4.0 * E * C, 4.0 * E * C, ALU.mult, ALU.add))
            nc.vector.tensor_tensor(to[:], first[:], place[:], ALU.add).then_inc(to_ready, 1)
            link(nc.vector.tensor_scalar(first[:], first[:], -float(E * C), None, ALU.add))
            link(nc.vector.tensor_tensor(first[:], first[:], kept_f[:], ALU.mult))
            link(nc.vector.tensor_scalar(back[:], first[:], float(E * C), None, ALU.add))
            nc.vector.tensor_copy(m.back[:], back[:])
            dve.wait_ge(to_masked, 1)
            nc.vector.tensor_copy(m.to[:], to[:])


def dispatch(nc, m, slots):
    R = TILE_RING
    with Stage(nc) as ctx:
        sem = lambda name: ctx.sem(f"disp_{name}")
        ring = ctx.enter_context(nc.sbuf_tensor("disp_ring", [P, R, D + 1], F32))
        index = ctx.enter_context(nc.sbuf_tensor("disp_index", [P, R], I32))
        rows_ready, index_ready, prob_ready = sem("rows"), sem("index"), sem("prob")
        landed = [sem(f"landed{j}") for j in range(R)]
        block = ctx.enter_context(nc.Block())

        @block.vector
        def _(dve):
            def rows(t, j, again, round_):
                if again:
                    dve.wait_ge(landed[j], round_ * 16)
                nc.vector.tensor_scalar(ring[:, j, 0:D], tile_of(m.x, t), m.mv[:, ds(t, 1), 0], m.scale[:, ds(t, 1)],
                                        ALU.subtract, ALU.mult).then_inc(rows_ready, 1)
            tile_loop(dve, m.tiles, [(0, rows)])

        @block.scalar
        def _(act):
            def fill(t, j, again, round_):
                if again:
                    act.wait_ge(landed[j], round_ * 16)
                nc.scalar.copy(ring[:, j, D:D + 1], m.prob[:, ds(t, 1)]).then_inc(prob_ready, 1)
                nc.scalar.copy(index[:, j:j + 1], m.to[:, ds(t, 1)]).then_inc(index_ready, 1)
            tile_loop(act, m.tiles, [(0, fill)])

        @block.gpsimd
        def _(pool):
            pool.wait_ge(m.slots_zeroed, 48)

            def scatter(t, j, again, round_):
                pool.wait_ge(rows_ready, t + 1)
                pool.wait_ge(prob_ready, t + 1)
                pool.wait_ge(index_ready, t + 1)
                nc.gpsimd.nop(nofuse=True)
                nc.gpsimd.indirect_dma_start(
                    out=slots[:, :], out_offset=bass.IndirectOffsetOnAxis(ap=index[:, j:j + 1], axis=0),
                    in_=ring[:, j, :], in_offset=None, bounds_check=m.experts * m.capacity - 1,
                    oob_is_err=False).then_inc(landed[j], 16)
            tile_loop(pool, m.tiles, [(0, scatter)])
            for j in range(R):
                pool.wait_ge(landed[j], m.tiles // R * 16)


def expert_slots(nc, m, a, slots, results):
    E, C = m.experts, m.capacity
    F = m.hidden1 // P
    TE = ceil_div(C, P)
    starts = [i * P for i in range(TE - 1)] + [C - P]
    fresh = [i * P for i in range(TE)]
    halves = [(0, 4 * P), (4 * P, C)]
    assert TE == 8 and C - 4 * P <= 512
    with Stage(nc) as ctx:
        sem = lambda name: ctx.sem(f"exp_{name}")
        buf = lambda name, shape, dt=F32: ctx.enter_context(nc.sbuf_tensor(f"exp_{name}", shape, dt))
        w1, w2 = buf("w1", [P, DK, F * P]), buf("w2", [P, F, D])
        b1, b2 = buf("b1", [P, 2, F]), buf("b2", [P, 2, D])
        rows = buf("rows", [P, TE, D + 1])
        prob = buf("prob", [P, 2, TE])
        cols = m.agg_flat[:, 0:DK * C].rearrange("p (k c) -> p k c", k=DK)
        hid = m.agg_flat[:, DK * C:DK * C + F * C].rearrange("p (f c) -> p f c", f=F)
        RY = 4
        y, mask, clamp = buf("y", [P, RY, D]), buf("mask", [P, RY, D], I32), buf("clamp", [P, RY, D])
        good, res, zero = buf("good", [P, RY, D], I32), buf("res", [P, RY, D]), buf("zero", [P, D])
        rows_landed, w1_landed, w2_landed = [sem(f"rows_landed{i}") for i in range(TE)], sem("w1_landed"), sem("w2_landed")
        turned, cols_kept, up_done, relu_done, down_done = (sem("turned"), sem("cols_kept"), sem("up"), sem("relu"),
                                                            sem("down"))
        prob_kept, biased, scaled, clamped, masked, merged, res_zeroed, res_done, freed = (
            sem("prob_kept"), sem("biased"), sem("scaled"), sem("clamped"), sem("masked"), sem("merged"),
            sem("res_zeroed"), sem("res_done"), sem("freed"))
        stored = [sem(f"stored{i}") for i in range(RY)]
        block = ctx.enter_context(nc.Block())

        def turned_ps(i):
            return m.ps[:, 4 + i % 2, 0:D].rearrange("p (k n) -> p k n", k=DK)

        def down_ps(i):
            return m.ps[:, 6 + i % 2, 0:D]

        @block.sync
        def _(sp):
            def load_rows(e, first):
                for i in range(TE):
                    if not first:
                        sp.wait_ge(turned, e * TE + (i + 1 - TE))
                        sp.wait_ge(prob_kept, e * TE + (i + 1 - TE))
                    sp.dma_start(rows[:, i, :], slots[ds(e * C + starts[i], P), :]).then_inc(rows_landed[i], 16)

            def load_w1(e, first):
                if not first:
                    sp.wait_ge(up_done, e * 2 * F)
                    sp.wait_ge(relu_done, e * 2 * F)
                sp.dma_start(w1[:], a["ffn1_w1"][ds(e, 1), :, :].rearrange("o (k p) f -> p (o k) f", p=P))\
                    .then_inc(w1_landed, 16)
                sp.dma_start(b1[:, 0, :], a["ffn1_b1"][ds(e, 1), :, :].rearrange("o p f -> p (o f)"))\
                    .then_inc(w1_landed, 16)

            def load_w2(e, first):
                if not first:
                    sp.wait_ge(down_done, e * TE)
                    sp.wait_ge(biased, e * TE)
                sp.dma_start(w2[:], a["ffn1_w2"][ds(e, 1), :, :].rearrange("o (k p) f -> p (o k) f", p=P))\
                    .then_inc(w2_landed, 16)
                sp.dma_start(b2[:, 0, :], a["ffn1_b2"][ds(e, 1), :].rearrange("o d -> (o d)").partition_broadcast(P))\
                    .then_inc(w2_landed, 16)

            load_rows(0, True)
            load_w1(0, True)
            load_w2(0, True)
            with sp.Fori(1, E) as e:
                load_rows(e, False)
                load_w1(e, False)
                load_w2(e, False)

        @block.tensor
        def _(pe):
            def turn(e, first):
                for i in range(TE):
                    pe.wait_ge(rows_landed[i], (e + 1) * 16)
                    if not first or i >= 2:
                        pe.wait_ge(cols_kept, e * TE + (i - 1))
                    for k in range(DK):
                        last = nc.tensor.transpose(turned_ps(i)[:, k, :], rows[:, i, k * P:(k + 1) * P], m.ident[:])
                    last.then_inc(turned, 1)

            def up(e, first):
                pe.wait_ge(w1_landed, (e + 1) * 32)
                pe.wait_ge(cols_kept, (e + 1) * TE)
                for h, (lo, hi) in enumerate(halves):
                    for f in range(F):
                        if not first or h or f >= 4:
                            pe.wait_ge(relu_done, e * 2 * F + (h * F + f - 3))
                        for k in range(DK):
                            last = nc.tensor.matmul(m.ps[:, f % 4, 0:hi - lo], w1[:, k, f * P:(f + 1) * P],
                                                    cols[:, k, lo:hi], start=(k == 0), stop=(k == DK - 1))
                        last.then_inc(up_done, 1)

            def down(e, first):
                pe.wait_ge(w2_landed, (e + 1) * 32)
                for i in range(TE):
                    if i == 0:
                        pe.wait_ge(relu_done, e * 2 * F + F)
                    if i == 4:
                        pe.wait_ge(relu_done, e * 2 * F + 2 * F)
                    if not first or i >= 2:
                        pe.wait_ge(biased, e * TE + (i - 1))
                    for f in range(F):
                        last = nc.tensor.matmul(down_ps(i), hid[:, f, starts[i]:starts[i] + P], w2[:, f, :],
                                                start=(f == 0), stop=(f == F - 1))
                    last.then_inc(down_done, 1)

            turn(0, True)
            up(0, True)
            turn(1, False)
            down(0, True)
            with pe.Fori(1, E - 1) as e:
                up(e, False)
                turn(e + 1, False)
                down(e, False)
            up(E - 1, False)
            down(E - 1, False)

        @block.scalar
        def _(act):
            def keep_cols(e, first):
                if not first:
                    act.wait_ge(up_done, e * 2 * F)
                for i in range(TE):
                    act.wait_ge(turned, e * TE + (i + 1))
                    skip = fresh[i] - starts[i]
                    nc.scalar.copy(cols[:, :, fresh[i]:starts[i] + P], turned_ps(i)[:, :, skip:P]).then_inc(cols_kept, 1)

            def relu(e, first):
                act.wait_ge(w1_landed, (e + 1) * 32)
                for h, (lo, hi) in enumerate(halves):
                    if not first:
                        act.wait_ge(down_done, e * TE + (4 * (h + 1) - TE))
                        if h:
                            act.wait_ge(down_done, e * TE)
                    for f in range(F):
                        act.wait_ge(up_done, e * 2 * F + (h * F + f + 1))
                        nc.scalar.activation(hid[:, f, lo:hi], m.ps[:, f % 4, 0:hi - lo], ACT.Relu,
                                             bias=b1[:, 0, f:f + 1]).then_inc(relu_done, 1)

            keep_cols(0, True)
            relu(0, True)
            with act.Fori(1, E) as e:
                keep_cols(e, False)
                relu(e, False)

        @block.vector
        def _(dve):
            nc.vector.memset(zero[:], 0.0).then_inc(freed, 1)

            def save_probs(e, parity):
                for i in range(TE):
                    dve.wait_ge(rows_landed[i], (e + 1) * 16)
                    nc.vector.tensor_copy(prob[:, parity, i:i + 1], rows[:, i, D:D + 1]).then_inc(prob_kept, 1)

            def finish(e, parity, first):
                dve.wait_ge(w2_landed, (e + 1) * 32)
                for i in range(TE):
                    s = i % RY
                    n = e * TE + i
                    again = not first or i >= RY
                    if again:
                        dve.wait_ge(stored[s], e * 16 * (TE // RY) + 16 * (i // RY))
                    dve.wait_ge(down_done, n + 1)
                    nc.vector.tensor_tensor(y[:, s, :], down_ps(i), b2[:, 0, :], ALU.add).then_inc(biased, 1)
                    nc.vector.memset(res[:, s, :], 0.0).then_inc(res_zeroed, 1)
                    dve.wait_ge(biased, n + 1)
                    dve.wait_ge(prob_kept, n + 1)
                    nc.vector.tensor_scalar(y[:, s, :], y[:, s, :], prob[:, parity, i:i + 1], None,
                                            ALU.mult).then_inc(scaled, 1)
                    dve.wait_ge(scaled, n + 1)
                    nc.vector.tensor_scalar(clamp[:, s, :], y[:, s, :], 1e4, -1e4, ALU.min, ALU.max).then_inc(clamped, 1)
                    nc.vector.tensor_scalar(mask[:, s, :], y[:, s, :], 0.0, 0.0, ALU.mult,
                                            ALU.is_equal).then_inc(masked, 1)
                    nc.vector.tensor_tensor(good[:, s, :], y[:, s, :], y[:, s, :], ALU.is_equal).then_inc(masked, 1)
                    dve.wait_ge(clamped, n + 1)
                    dve.wait_ge(masked, n * 2 + 2)
                    nc.vector.nop(nofuse=True)
                    nc.vector.copy_predicated(clamp[:, s, :], mask[:, s, :], y[:, s, :]).then_inc(merged, 1)
                    dve.wait_ge(merged, n + 1)
                    dve.wait_ge(res_zeroed, n + 1)
                    nc.vector.nop(nofuse=True)
                    nc.vector.copy_predicated(res[:, s, :], good[:, s, :], clamp[:, s, :]).then_inc(res_done, 1)

            save_probs(0, 0)
            save_probs(1, 1)
            finish(0, 0, True)
            with dve.Fori(1, E // 2) as g:
                save_probs(g * 2, 0)
                finish(g * 2 - 1, 1, False)
                save_probs(g * 2 + 1, 1)
                finish(g * 2, 0, False)
            finish(E - 1, 1, False)

        @block.gpsimd
        def _(pool):
            pool.wait_ge(freed, 1)
            pool.dma_start(results[E * C:E * C + 1, :], zero[0:1, :]).then_inc(m.zero_row, 16)

            def store(e):
                for i in range(TE):
                    s = i % RY
                    skip = fresh[i] - starts[i]
                    pool.wait_ge(res_done, e * TE + (i + 1))
                    nc.gpsimd.nop(nofuse=True)
                    pool.dma_start(results[ds(e * C + fresh[i], P - skip), :], res[skip:P, s, :])\
                        .then_inc(stored[s], 16)
            with pool.Fori(0, E) as e:
                store(e)
            pool.wait_ge(m.zero_row, 16)
            for s in range(RY):
                pool.wait_ge(stored[s], E * 16 * (TE // RY))


def collect(nc, m, results, out):
    R = TILE_RING
    with Stage(nc) as ctx:
        sem = lambda name: ctx.sem(f"coll_{name}")
        rows = ctx.enter_context(nc.sbuf_tensor("coll_rows", [P, R, D], F32))
        index = ctx.enter_context(nc.sbuf_tensor("coll_index", [P, R], I32))
        index_ready, added, stored = sem("index"), sem("added"), sem("stored")
        landed = [sem(f"landed{j}") for j in range(R)]
        block = ctx.enter_context(nc.Block())

        @block.scalar
        def _(act):
            def put_index(t, j, again, round_):
                if again:
                    act.wait_ge(landed[j], round_ * 16)
                nc.scalar.copy(index[:, j:j + 1], m.back[:, ds(t, 1)]).then_inc(index_ready, 1)
            tile_loop(act, m.tiles, [(0, put_index)])

        @block.gpsimd
        def _(pool):
            def gather(t, j, again, round_):
                pool.wait_ge(index_ready, t + 1)
                if again:
                    pool.wait_ge(added, t + (1 - R))
                nc.gpsimd.nop(nofuse=True)
                nc.gpsimd.indirect_dma_start(
                    out=rows[:, j, :], out_offset=None, in_=results[:, :],
                    in_offset=bass.IndirectOffsetOnAxis(ap=index[:, j:j + 1], axis=0)).then_inc(landed[j], 16)
            tile_loop(pool, m.tiles, [(0, gather)])

        @block.vector
        def _(dve):
            def add(t, j, again, round_):
                dve.wait_ge(landed[j], (round_ + 1) * 16)
                nc.vector.tensor_tensor(tile_of(m.x, t), tile_of(m.x, t), rows[:, j, :], ALU.add).then_inc(added, 1)
            tile_loop(dve, m.tiles, [(0, add)])

        @block.sync
        def _(sp):
            with sp.Fori(0, m.full_tiles // 4) as g:
                sp.wait_ge(added, g * 4 + 4)
                sp.dma_start(out[ds(g * 4 * P, 4 * P), :].rearrange("(t p) d -> p t d", p=P),
                             m.x[:, ds(g * 4, 4), :]).then_inc(stored, 16)
            sp.wait_ge(added, m.tiles)
            sp.dma_start(out[m.full_tiles * P:m.nodes, :], m.x[0:m.tail_nodes, m.full_tiles, :]).then_inc(stored, 16)
            sp.wait_ge(stored, 16 * (m.full_tiles // 4 + 1))


def graph_network(nc, a, out):
    nodes, width = a["x"].shape
    full_chunks, tail_edges = a["src_main"].shape[1], a["src_tail"].shape[0]
    m = Shared()
    m.nodes, m.tiles, m.full_tiles, m.tail_nodes = nodes, ceil_div(nodes, P), nodes // P, nodes % P
    m.full_chunks, m.tail_edges = full_chunks, tail_edges
    m.chunks = ceil_div(full_chunks + 1, 2 * CHUNK_RING) * 2 * CHUNK_RING
    m.experts = a["gate_w"].shape[1]
    m.capacity = ceil_div(nodes * 5, 4 * m.experts)
    m.hidden0, m.hidden1, m.heads = a["ffn0_w1"].shape[2], a["ffn1_w1"].shape[2], a["gat_l"].shape[0]
    table = [nc.dram_tensor(f"table{i}", [m.tiles * P, D], F32, kind="Internal").ap() for i in range(2)]
    heads_table = nc.dram_tensor("heads_table", [m.tiles * P, D + m.heads], F32, kind="Internal").ap()
    left_table = nc.dram_tensor("left_table", [m.tiles * P, m.heads], F32, kind="Internal").ap()
    slots = nc.dram_tensor("slots", [m.experts * m.capacity, D + 1], F32, kind="Internal").ap()
    results = nc.dram_tensor("results", [m.experts * m.capacity + 1, D], F32, kind="Internal").ap()
    with ExitStack() as ctx:
        def sb(name, shape, dt=F32):
            return ctx.enter_context(nc.sbuf_tensor(name, shape, dt))
        m.x = sb("x", [P, m.tiles, D])
        m.agg_flat = sb("agg", [P, DK * (m.tiles * P + P)])
        m.agg = m.agg_flat[:].rearrange("p (k n) -> p k n", k=DK)
        m.mean_row = sb("mean_row", [1, D])
        m.slots_zeroed = ctx.enter_context(nc.semaphore("slots_zeroed"))
        m.zero_made = ctx.enter_context(nc.semaphore("zero_made"))
        m.zero = sb("zero", [P, D + 1])
        m.zero_row = ctx.enter_context(nc.semaphore("zero_row"))
        m.ones = sb("ones", [P, P])
        m.iota_i = sb("iota_i", [P, P], I32)
        m.part_i = sb("part_i", [P, 1], I32)
        m.iota, m.iota_b, m.part = sb("iota", [P, P]), sb("iota_b", [P, P], BF16), sb("part", [P, 1])
        m.mv, m.scale = sb("mv", [P, m.tiles, 2]), sb("scale", [P, m.tiles])
        m.ident, m.first_row = sb("ident", [P, P]), sb("first_row", [P, P])
        m.src, m.dst = sb("src", [P, m.chunks], I32), sb("dst", [P, m.chunks], I32)
        m.ps = ctx.enter_context(nc.psum_tensor("ps", [P, 8, 512], F32))
        with ExitStack() as gcn:
            def gb(name, shape, dt=F32):
                return gcn.enter_context(nc.sbuf_tensor(name, shape, dt))
            m.dloc = gb("dloc", [P, m.chunks])
            m.dinv = gb("dinv", [P, m.tiles])
            m.dst_f = gb("dst_f", [P, m.chunks])
            m.astray = gb("astray_flag", [1, 1], I32)
            m.w1, m.w2, m.w3, m.wp = gb("w1", [P, DK, D]), gb("w2", [P, DK, D]), gb("w3", [P, DK, P]), gb("wp", [P, D])
            m.b1, m.b2, m.b3, m.bp = gb("b1", [P, D]), gb("b2", [P, D]), gb("b3", [P, P]), gb("bp", [P, D])
            load_inputs(nc, m, a, slots)
            degrees(nc, m)
            row_stats(nc, m, "stats0", lambda t: tile_of(m.x, t), with_degree=True)
            normalize(nc, m, "norm0", table=table[0])
            sum_edges(nc, m, "e1", table[0])
            update_nodes(nc, m, "n1", m.w1, m.b1, table[1])
            sum_edges(nc, m, "e2", table[1])
            update_nodes(nc, m, "n2", m.w2, m.b2, table[0])
            sum_edges(nc, m, "e3", table[0])
            finish_gcn(nc, m, "n3")
        mask_pads(nc, m, "pads1")
        row_stats(nc, m, "stats1", lambda t: tile_of(m.x, t))
        normalize(nc, m, "norm1", column_sums=True)
        with ExitStack() as ffn:
            def fb(name, shape, dt=F32):
                return ffn.enter_context(nc.sbuf_tensor(name, shape, dt))
            m.f0_w1, m.f0_w2 = fb("f0_w1", [P, 2, DK, m.hidden0]), fb("f0_w2", [P, 2, m.hidden0 // P, D])
            m.f0_b1, m.f0_b2 = fb("f0_b1", [P, 2, m.hidden0 // P]), fb("f0_b2", [P, D])
            m.gamma, m.beta = fb("gamma", [P, D]), fb("beta", [P, D])
            route_all(nc, m, a)
            two_experts(nc, m)
            row_stats(nc, m, "stats2", lambda t: m.agg[:, :, ds(t * P, P)])
            add_normalized(nc, m)
        row_stats(nc, m, "stats3", lambda t: tile_of(m.x, t))
        project_heads(nc, m, a, heads_table, left_table)
        attend(nc, m, heads_table, left_table)
        row_stats(nc, m, "stats4", lambda t: tile_of(m.x, t))
        m.gates, m.prob = sb("gates", [P, m.tiles, m.experts]), sb("prob", [P, m.tiles])
        m.to, m.back = sb("to", [P, m.tiles], I32), sb("back", [P, m.tiles], I32)
        score_experts(nc, m, a)
        assign_slots(nc, m)
        dispatch(nc, m, slots)
        expert_slots(nc, m, a, slots, results)
        collect(nc, m, results, out)


def kernel(**inputs):
    import numpy as np
    import concourse.bacc as bacc
    from concourse.bass_utils import run_bass_kernel_spmd

    nc = bacc.Bacc("TRN2", target_bir_lowering=False, num_devices=1)
    src, dst = np.asarray(inputs["src"]), np.asarray(inputs["dst"])
    main = src.shape[0] // P * P

    def by_partition(b):
        b = np.asarray(b)
        return b.reshape(b.shape[0], -1, P).transpose(0, 2, 1)

    data = {
        "x": inputs["x"],
        "src_main": src[:main].reshape(-1, P).T, "src_tail": src[main:].reshape(-1, 1),
        "dst_main": dst[:main].reshape(-1, P).T, "dst_tail": dst[main:].reshape(-1, 1),
        "gnn_w1": inputs["L0_gnn_W1"], "gnn_b1": inputs["L0_gnn_b1"],
        "gnn_w2": inputs["L0_gnn_W2"], "gnn_b2": inputs["L0_gnn_b2"],
        "gnn_w3": inputs["L0_gnn_W3"], "gnn_b3": inputs["L0_gnn_b3"],
        "gnn_wp": inputs["L0_gnn_Wp"], "gnn_bp": inputs["L0_gnn_bp"],
        "ffn0_wr": inputs["L0_ffn_Wr"], "ffn0_br": inputs["L0_ffn_br"],
        "ffn0_w1": inputs["L0_ffn_W1"], "ffn0_b1": by_partition(inputs["L0_ffn_b1"]),
        "ffn0_w2": inputs["L0_ffn_W2"], "ffn0_b2": inputs["L0_ffn_b2"],
        "ffn0_gamma": inputs["L0_ffn_gamma"], "ffn0_beta": inputs["L0_ffn_beta"],
        "gat_w": inputs["L1_gnn_weight"], "gat_l": inputs["L1_gnn_attn_l"], "gat_r": inputs["L1_gnn_attn_r"],
        "gate_w": inputs["L1_ffn_gate_w"], "gate_b": inputs["L1_ffn_gate_b"],
        "ffn1_w1": inputs["L1_ffn_w1"], "ffn1_b1": by_partition(inputs["L1_ffn_b1"]),
        "ffn1_w2": inputs["L1_ffn_w2"], "ffn1_b2": inputs["L1_ffn_b2"],
    }
    arrays, a = {}, {}
    for name, value in data.items():
        value = np.ascontiguousarray(value)
        arrays[f"in_{name}"] = value
        a[name] = nc.dram_tensor(f"in_{name}", value.shape, mybir.dt.from_np(value.dtype),
                                 kind="ExternalInput").ap()
    out = nc.dram_tensor("out", inputs["x"].shape, F32, kind="ExternalOutput").ap()
    graph_network(nc, a, out)
    return run_bass_kernel_spmd(nc, [arrays], core_ids=[0]).results[0]["out"]
```

```python
from contextlib import ExitStack

import concourse.bass as bass
from concourse import mybir

ALU = mybir.AluOpType
ACT = mybir.ActivationFunctionType
AX = mybir.AxisListType
F32 = mybir.dt.float32
BF16 = mybir.dt.bfloat16
F32R = mybir.dt.float32r
I32 = mybir.dt.int32
U32 = mybir.dt.uint32
ds = bass.ds

P = 128
D = 256
DK = D // P
EPS = 1e-5
TILE_RING = 7
CHUNK_RING = 8
HOT_RING = 4
WINDOW = P


def ceil_div(a, b):
    return (a + b - 1) // b


class Shared:
    pass


class Stage(ExitStack):

    def __init__(self, nc):
        super().__init__()
        self.nc, self.sems = nc, []

    def sem(self, name):
        self.sems.append(self.nc.alloc_semaphore(name))
        return self.sems[-1]

    def __exit__(self, *error):
        super().__exit__(*error)
        if self.sems and error[0] is None:
            self.nc.clear_and_free_semaphores(self.sems)
            self.nc.all_engine_barrier(sem_only=True)


def load_inputs(nc, m, a, slots):
    n_main = m.full_tiles * P
    with Stage(nc) as ctx:
        pads_zero = ctx.sem("pads_zero")
        edges_landed = ctx.sem("edges_landed")
        iota_made = ctx.sem("iota_made")
        zeroed = ctx.sem("zeroed")
        block = ctx.enter_context(nc.Block())

        @block.sync
        def _(sp):
            sp.wait_ge(pads_zero, 3)
            sp.dma_start(m.src[:, 0:m.full_chunks], a["src_main"]).then_inc(edges_landed, 16)
            sp.dma_start(m.dst[:, 0:m.full_chunks], a["dst_main"]).then_inc(edges_landed, 16)
            sp.dma_start(m.src[0:m.tail_edges, m.full_chunks:m.full_chunks + 1], a["src_tail"]).then_inc(edges_landed, 16)
            sp.dma_start(m.dst[0:m.tail_edges, m.full_chunks:m.full_chunks + 1], a["dst_tail"]).then_inc(edges_landed, 16)
            sp.dma_start(m.x[:, 0:m.full_tiles, :],
                         a["x"][0:n_main, :].rearrange("(t p) d -> p t d", p=P)).then_inc(m.x_landed, 16)
            sp.dma_start(m.x[0:m.tail_nodes, m.full_tiles, :], a["x"][n_main:m.nodes, :]).then_inc(m.x_landed, 16)
            sp.wait_ge(edges_landed, 64)

        @block.scalar
        def _(act):
            act.dma_start(m.w1[:], a["gnn_w1"].rearrange("(k p) n -> p k n", p=P)).then_inc(m.w_landed, 16)
            act.dma_start(m.w2[:], a["gnn_w2"].rearrange("(k p) n -> p k n", p=P)).then_inc(m.w_landed, 16)
            act.dma_start(m.w3[:], a["gnn_w3"].rearrange("(k p) n -> p k n", p=P)).then_inc(m.w_landed, 16)
            act.dma_start(m.wp[:], a["gnn_wp"]).then_inc(m.w_landed, 16)
            act.dma_start(m.b1[:], a["gnn_b1"].partition_broadcast(P)).then_inc(m.w_landed, 16)
            act.dma_start(m.b2[:], a["gnn_b2"].partition_broadcast(P)).then_inc(m.w_landed, 16)
            act.dma_start(m.b3[:], a["gnn_b3"].partition_broadcast(P)).then_inc(m.w_landed, 16)
            act.dma_start(m.bp[:], a["gnn_bp"].partition_broadcast(P)).then_inc(m.w_landed, 16)
            act.wait_ge(m.zero_made, 1)
            full = slots.shape[0] // P
            half = full // 2
            for lo, hi in ((0, half), (half, full)):
                act.dma_start(slots[lo * P:hi * P, :].rearrange("(t p) w -> p t w", p=P),
                              m.zero[:].unsqueeze(1).to_broadcast([P, hi - lo, D + 1])).then_inc(m.slots_zeroed, 16)
            act.dma_start(slots[full * P:, :], m.zero[0:slots.shape[0] - full * P, :]).then_inc(m.slots_zeroed, 16)

        @block.vector
        def _(dve):
            nc.vector.memset(m.x[:, m.full_tiles, :], 0.0).then_inc(pads_zero, 1)
            nc.vector.memset(m.src[:, m.full_chunks:m.chunks], 0).then_inc(pads_zero, 1)
            nc.vector.memset(m.dst[:, m.full_chunks:m.chunks], 0).then_inc(pads_zero, 1)
            nc.vector.memset(m.agg[:, :, m.tiles * P:], 0.0)
            nc.vector.memset(m.ones[:], 1.0)
            nc.vector.memset(m.zero[:], 0.0).then_inc(m.zero_made, 1)

        @block.gpsimd
        def _(pool):
            nc.gpsimd.iota(m.iota_i[:], pattern=[[1, P]], base=0, channel_multiplier=0).then_inc(iota_made, 1)
            nc.gpsimd.iota(m.part_i[:], pattern=[[1, 1]], base=0, channel_multiplier=1).then_inc(iota_made, 1)
            nc.gpsimd.memset(m.ident[:], 0.0).then_inc(zeroed, 1)
            nc.gpsimd.memset(m.first_row[:], 1.0).then_inc(zeroed, 1)
            pool.wait_ge(iota_made, 2)
            nc.gpsimd.tensor_copy(m.iota[:], m.iota_i[:])
            nc.gpsimd.tensor_copy(m.iota_b[:], m.iota_i[:])
            nc.gpsimd.tensor_copy(m.part[:], m.part_i[:])
            pool.wait_ge(zeroed, 2)
            nc.gpsimd.affine_select(out=m.ident[:], in_=m.ident[:], compare_op=ALU.not_equal, fill=1.0, base=0,
                                    pattern=[[-1, P]], channel_multiplier=1)
            nc.gpsimd.affine_select(out=m.first_row[:], in_=m.first_row[:], compare_op=ALU.is_ge, fill=0.0, base=0,
                                    pattern=[[0, P]], channel_multiplier=-1)


def degrees(nc, m):
    half = m.chunks // 2
    groups = m.chunks // CHUNK_RING
    with Stage(nc) as ctx:
        dst_f = m.dst_f
        ends = ctx.enter_context(nc.sbuf_tensor("ends", [P, 2], F32))
        astray = ctx.enter_context(nc.sbuf_tensor("astray", [P, 4], F32))
        ends_done, astray_done, counted = ctx.sem("ends_done"), ctx.sem("astray_done"), ctx.sem("counted")
        hi_i = ctx.enter_context(nc.sbuf_tensor("hi_i", [P, m.chunks], I32))
        lo_i = ctx.enter_context(nc.sbuf_tensor("lo_i", [P, m.chunks], I32))
        hi = ctx.enter_context(nc.sbuf_tensor("hi", [P, m.chunks], F32))
        lo = ctx.enter_context(nc.sbuf_tensor("lo", [P, m.chunks], F32))
        hot_lo = ctx.enter_context(nc.sbuf_tensor("hot_lo", [P, 2, CHUNK_RING, P], BF16))
        hot_hi = ctx.enter_context(nc.sbuf_tensor("hot_hi", [P, 2, CHUNK_RING, m.tiles], BF16))
        deg = ctx.enter_context(nc.sbuf_tensor("deg", [P, m.tiles], F32))
        root = ctx.enter_context(nc.sbuf_tensor("root", [P, m.tiles], F32))
        ints_done = ctx.sem("ints_done")
        floats_done = ctx.sem("floats_done")
        base_spread = ctx.sem("base_spread")
        dloc_made = ctx.sem("dloc_made")
        pads_marked = ctx.sem("pads_marked")
        hot_ready = ctx.sem("hot_ready")
        group_used = ctx.sem("group_used")
        deg_done = ctx.sem("deg_done")
        root_done = ctx.sem("root_done")
        block = ctx.enter_context(nc.Block())
        base_ps = m.ps[:, 0:2, 0:half]
        deg_ps = m.ps[:, 2, 0:m.tiles]

        @block.vector
        def _(dve):
            nc.vector.tensor_copy(dst_f[:], m.dst[:]).then_inc(floats_done, 1)
            nc.vector.tensor_scalar(hi_i[:], m.dst[:], 7, None, ALU.logical_shift_right).then_inc(ints_done, 1)
            nc.vector.tensor_scalar(lo_i[:], m.dst[:], P - 1, None, ALU.bitwise_and).then_inc(ints_done, 1)
            dve.wait_ge(ints_done, 2)
            nc.vector.tensor_copy(hi[:], hi_i[:]).then_inc(floats_done, 1)
            nc.vector.tensor_copy(lo[:], lo_i[:])
            dve.wait_ge(base_spread, 1)
            dve.wait_ge(floats_done, 2)
            nc.vector.tensor_tensor(m.dloc[:].rearrange("p (h c) -> p h c", h=2),
                                    dst_f[:].rearrange("p (h c) -> p h c", h=2), base_ps,
                                    ALU.subtract).then_inc(dloc_made, 1)
            dve.wait_ge(pads_marked, 5)
            nc.vector.reduce_max(ends[:, 0:1], m.dloc[:], AX.X).then_inc(ends_done, 1)
            nc.vector.tensor_reduce(ends[:, 1:2], m.dloc[:], AX.X, ALU.min).then_inc(ends_done, 1)
            dve.wait_ge(ends_done, 2)
            nc.vector.tensor_scalar(astray[:, 0:1], ends[:, 0:1], float(WINDOW - 1), None, ALU.is_gt).then_inc(astray_done, 1)
            nc.vector.tensor_scalar(astray[:, 1:2], ends[:, 1:2], 0.0, None, ALU.is_lt).then_inc(astray_done, 1)

            def put(g, h):
                for j in range(CHUNK_RING):
                    hot = nc.vector.tensor_scalar(hot_lo[:, h, j, :], m.iota_b[:],
                                                  lo[:, ds(g * CHUNK_RING + j, 1)], None, ALU.is_equal)
                nc.vector.tensor_tensor(hot_hi[:, h, :, :],
                                        hi[:, ds(g * CHUNK_RING, CHUNK_RING)].unsqueeze(2)
                                        .to_broadcast([P, CHUNK_RING, m.tiles]),
                                        m.iota[:, 0:m.tiles].unsqueeze(1).to_broadcast([P, CHUNK_RING, m.tiles]),
                                        ALU.is_equal).then_inc(hot_ready, 1)

            put(0, 0)
            put(1, 1)
            with dve.Fori(0, (groups - 2) // 2) as g:
                for h in range(2):
                    dve.wait_ge(group_used, g * 2 + (1 + h))
                    put(g * 2 + (2 + h), h)
            dve.wait_ge(counted, 1)
            nc.vector.reduce_max(astray[0:1, 2:3], m.ps[0:1, 3, 0:2], AX.X).then_inc(astray_done, 1)
            dve.wait_ge(astray_done, 3)
            nc.vector.tensor_scalar(m.astray[0:1, :], astray[0:1, 2:3], 0.0, None, ALU.is_gt)
            dve.wait_ge(group_used, groups)
            nc.vector.tensor_scalar(deg[:], deg_ps, 1.0, None, ALU.add).then_inc(deg_done, 1)
            dve.wait_ge(root_done, 1)
            nc.vector.reciprocal(m.dinv[:], root[:])

        @block.gpsimd
        def _(pool):
            c = m.full_chunks
            pool.wait_ge(dloc_made, 1)
            for targets in (m.dloc, dst_f):
                nc.gpsimd.affine_select(out=targets[:, c:c + 1], in_=targets[:, c:c + 1], compare_op=ALU.is_ge,
                                        fill=0.5, base=m.tail_edges - 1, pattern=[[0, 1]],
                                        channel_multiplier=-1).then_inc(pads_marked, 1)
            nc.gpsimd.memset(m.dloc[:, c + 1:m.chunks], 0.5)
            nc.gpsimd.memset(dst_f[:, c + 1:m.chunks], 0.5).then_inc(pads_marked, 1)
            nc.gpsimd.affine_select(out=hi[:, c:c + 1], in_=hi[:, c:c + 1], compare_op=ALU.is_ge, fill=-1.0,
                                    base=m.tail_edges - 1, pattern=[[0, 1]],
                                    channel_multiplier=-1).then_inc(pads_marked, 1)
            nc.gpsimd.memset(hi[:, c + 1:m.chunks], -1.0).then_inc(pads_marked, 1)

        @block.tensor
        def _(pe):
            pe.wait_ge(floats_done, 1)
            for h in range(2):
                last = nc.tensor.matmul(base_ps[:, h, :], m.first_row[:], dst_f[:, h * half:(h + 1) * half],
                                        start=True, stop=True)
            last.then_inc(base_spread, 1)
            pe.wait_ge(astray_done, 2)
            nc.tensor.matmul(m.ps[0:1, 3, 0:2], m.ones[:, 0:1], astray[:, 0:2], start=True, stop=True).then_inc(counted, 1)
            pe.wait_ge(hot_ready, 1)
            for j in range(CHUNK_RING):
                mm = nc.tensor.matmul(deg_ps, hot_lo[:, 0, j, :], hot_hi[:, 0, j, :], start=(j == 0), stop=False,
                                      skip_group_check=True)
            mm.then_inc(group_used, 1)
            with pe.Fori(0, (groups - 2) // 2) as g:
                for h in range(2):
                    pe.wait_ge(hot_ready, g * 2 + (2 + h))
                    for j in range(CHUNK_RING):
                        mm = nc.tensor.matmul(deg_ps, hot_lo[:, 1 - h, j, :], hot_hi[:, 1 - h, j, :], start=False,
                                              stop=False, skip_group_check=True)
                    mm.then_inc(group_used, 1)
            pe.wait_ge(hot_ready, groups)
            for j in range(CHUNK_RING):
                mm = nc.tensor.matmul(deg_ps, hot_lo[:, 1, j, :], hot_hi[:, 1, j, :], start=False,
                                      stop=(j == CHUNK_RING - 1), skip_group_check=True)
            mm.then_inc(group_used, 1)

        @block.scalar
        def _(act):
            act.wait_ge(deg_done, 1)
            nc.scalar.activation(root[:], deg[:], ACT.Sqrt).then_inc(root_done, 1)


def tile_loop(eng, tiles, steps):
    R = TILE_RING
    lags = max(lag for lag, _ in steps)
    assert tiles % R == 0 and lags < R
    for s in range(2 * R):
        for lag, body in steps:
            if s >= lag:
                body(s - lag, (s - lag) % R, s - lag >= R, (s - lag) // R)
    with eng.Fori(2, tiles // R) as g:
        for j in range(R):
            for lag, body in steps:
                body(g * R + (j - lag), (j - lag) % R, True, g + (j - lag) // R)
    for s in range(tiles, tiles + lags):
        for lag, body in steps:
            if s - lag < tiles:
                body(s - lag, (s - lag) % R, True, (s - lag) // R)


def tile_of(buf, t):
    return buf[:, ds(t, 1), :].rearrange("p t d -> p (t d)")


class RowStats:

    def __init__(self, nc, m, ctx, tag, with_degree=False):
        sem = lambda name: ctx.sem(f"{tag}_{name}")
        buf = lambda name: ctx.enter_context(nc.sbuf_tensor(f"{tag}_{name}", [P, m.tiles], F32))
        self.nc, self.m, self.with_degree = nc, m, with_degree
        self.done, self.chain, self.veps_done, self.std_done = sem("tile_stats"), sem("chain"), sem("veps"), sem("std")
        self.spread, self.veps, self.std = buf("spread"), buf("veps"), buf("std")

    def of_tile(self, t, rows):
        self.nc.vector.nop(nofuse=True)
        self.nc.vector.bn_stats(tile_of(self.m.stats, t), rows).then_inc(self.done, 1)

    def on_vector(self, dve, tiles):
        nc, m = self.nc, self.m
        links = [0]

        def link(ins):
            links[0] += 1
            ins.then_inc(self.chain, 1)
            dve.wait_ge(self.chain, links[0])

        dve.wait_ge(self.done, tiles)
        mean, var = (m.stats[:, :, 1], m.stats[:, :, 4]), (m.stats[:, :, 2], m.stats[:, :, 5])
        nc.vector.tensor_tensor(m.mean[:], mean[0], mean[1], ALU.add)
        link(nc.vector.tensor_tensor(self.spread[:], mean[0], mean[1], ALU.subtract))
        link(nc.vector.tensor_tensor(self.spread[:], self.spread[:], self.spread[:], ALU.mult))
        link(nc.vector.tensor_scalar(self.spread[:], self.spread[:], 0.25, EPS, ALU.mult, ALU.add))
        nc.vector.tensor_scalar(m.mean[:], m.mean[:], 0.5, None, ALU.mult)
        link(nc.vector.tensor_tensor(self.veps[:], var[0], var[1], ALU.add))
        nc.vector.scalar_tensor_tensor(self.veps[:], self.veps[:], 1.0 / D, self.spread[:], ALU.mult,
                                       ALU.add).then_inc(self.veps_done, 1)
        dve.wait_ge(self.std_done, 1)
        if self.with_degree:
            link(nc.vector.reciprocal(self.std[:], self.std[:]))
            nc.vector.tensor_tensor(m.scale[:], self.std[:], m.dinv[:], ALU.mult)
        else:
            nc.vector.reciprocal(m.scale[:], self.std[:])

    def on_scalar(self, act):
        act.wait_ge(self.veps_done, 1)
        self.nc.scalar.activation(self.std[:], self.veps[:], ACT.Sqrt).then_inc(self.std_done, 1)


def row_stats(nc, m):
    with Stage(nc) as ctx:
        stats = RowStats(nc, m, ctx, "stats0", with_degree=True)
        block = ctx.enter_context(nc.Block())

        @block.vector
        def _(dve):
            dve.wait_ge(m.x_landed, 32)
            dve.wait_ge(m.w_landed, 16 * 8)
            tile_loop(dve, m.tiles, [(0, lambda t, j, again, round_: stats.of_tile(t, tile_of(m.x, t)))])
            stats.on_vector(dve, m.tiles)

        @block.scalar
        def _(act):
            stats.on_scalar(act)


def normalize(nc, m, tag, table=None, column_sums=False):
    R = TILE_RING
    with Stage(nc) as ctx:
        sem = lambda name: ctx.sem(f"{tag}_{name}")
        ring = ctx.enter_context(nc.sbuf_tensor(f"{tag}_ring", [P, R, D], F32))
        rows_ready, turned, turned_kept, sums_done = sem("rows"), sem("turned"), sem("turned_kept"), sem("sums")
        stored = [sem(f"stored{j}") for j in range(R)]
        block = ctx.enter_context(nc.Block())

        def turned_ps(j):
            return m.ps[:, j, 0:D].rearrange("p (k n) -> p k n", k=DK)

        @block.vector
        def _(dve):
            def rows(t, j, again, round_):
                if again:
                    dve.wait_ge(turned, t + (1 - R))
                    if table is not None:
                        dve.wait_ge(stored[j], round_ * 16)
                nc.vector.tensor_scalar(ring[:, j, :], tile_of(m.x, t), m.mean[:, ds(t, 1)], m.scale[:, ds(t, 1)],
                                        ALU.subtract, ALU.mult).then_inc(rows_ready, 1)
            tile_loop(dve, m.tiles, [(0, rows)])
            if column_sums:
                dve.wait_ge(turned, m.tiles)
                nc.vector.tensor_scalar(m.mean_row[0:1, :], m.ps[0:1, R, 0:D], 1.0 / m.nodes, None, ALU.mult)

        @block.scalar
        def _(act):
            def keep(t, j, again, round_):
                act.wait_ge(turned, t + 1)
                nc.scalar.copy(m.agg[:, :, ds(t * P, P)], turned_ps(j)).then_inc(turned_kept, 1)
            tile_loop(act, m.tiles, [(0, keep)])

        @block.tensor
        def _(pe):
            def turn(t, j, again, round_):
                pe.wait_ge(rows_ready, t + 1)
                if again:
                    pe.wait_ge(turned_kept, t + (1 - R))
                if column_sums:
                    nc.tensor.matmul(m.ps[0:1, R, 0:D], m.ones[:, 0:1], ring[:, j, :], start=not again and j == 0,
                                     stop=False, skip_group_check=True)
                for k in range(DK):
                    last = nc.tensor.transpose(turned_ps(j)[:, k, :], ring[:, j, k * P:(k + 1) * P], m.ident[:])
                last.then_inc(turned, 1)
            tile_loop(pe, m.tiles, [(0, turn)])

        if table is not None:
            @block.sync
            def _(sp):
                def store(t, j, again, round_):
                    sp.wait_ge(rows_ready, t + 1)
                    sp.dma_start(table[ds(t * P, P), :], ring[:, j, :]).then_inc(stored[j], 16)
                tile_loop(sp, m.tiles, [(0, store)])
                for j in range(R):
                    sp.wait_ge(stored[j], m.tiles // R * 16)


def sum_edges(nc, m, tag, table):
    R = 2 * CHUNK_RING
    B = 8
    H = CHUNK_RING
    loops = m.chunks // R
    with Stage(nc) as ctx:
        sem = lambda name: ctx.sem(f"{tag}_{name}")
        rows = ctx.enter_context(nc.sbuf_tensor(f"{tag}_rows", [P, R, D], F32))
        hot = ctx.enter_context(nc.sbuf_tensor(f"{tag}_hot", [P, R, P], F32))
        index = ctx.enter_context(nc.sbuf_tensor(f"{tag}_index", [P, R], I32))
        landed = [sem(f"landed{j}") for j in range(R)]
        group_free, tile_free, moved = sem("group_free"), sem("tile_free"), sem("moved")
        index_ready, hot_ready, summed, added = sem("index_ready"), sem("hot_ready"), sem("summed"), sem("added")
        places = ctx.enter_context(nc.sbuf_tensor(f"{tag}_places", [P, P], F32))
        block = ctx.enter_context(nc.Block())

        def branch(eng, in_windows, anywhere):
            astray = eng.value_load(m.astray[0:1, 0:1], min_val=0, max_val=1)
            with eng.If(astray == 0):
                in_windows()
            with eng.Else():
                anywhere()

        def part_ps(j):
            return m.ps[:, j % B, 0:DK * P].rearrange("p (k n) -> p k n", k=DK)

        @block.scalar
        def _(act):
            def in_windows():
                def put(g, h):
                    nc.scalar.copy(index[:, h * H:(h + 1) * H], m.src[:, ds(g * R + h * H, H)]).then_inc(index_ready, 1)
                for h in range(2):
                    put(0, h)
                with act.Fori(1, loops) as g:
                    for h in range(2):
                        for j in range(h * H, (h + 1) * H):
                            act.wait_ge(landed[j], g * 16)
                        put(g, h)

            def anywhere():
                with act.Fori(0, m.tiles) as w:
                    with act.Fori(0, loops) as g:
                        act.wait_ge(group_free, w * loops + (g + 1))
                        nc.scalar.copy(index[:], m.src[:, ds(g * R, R)]).then_inc(index_ready, 1)

            branch(act, in_windows, anywhere)

        @block.gpsimd
        def _(pool):
            def in_windows():
                def gather_half(g, h):
                    pool.wait_ge(index_ready, g * 2 + (1 + h))
                    nc.gpsimd.nop(nofuse=True)
                    for j in range(h * H, (h + 1) * H):
                        nc.gpsimd.indirect_dma_start(
                            out=rows[:, j, :], out_offset=None, in_=table[:, :],
                            in_offset=bass.IndirectOffsetOnAxis(ap=index[:, j:j + 1], axis=0)).then_inc(landed[j], 16)

                for h in range(2):
                    gather_half(0, h)
                with pool.Fori(1, loops) as g:
                    for h in range(2):
                        pool.wait_ge(summed, g * R + ((h + 1) * H - R))
                        gather_half(g, h)

            def anywhere():
                with pool.Fori(0, m.tiles) as w:
                    with pool.Fori(0, loops) as g:
                        pool.wait_ge(index_ready, w * loops + (g + 1))
                        nc.gpsimd.nop(nofuse=True)
                        for j in range(R):
                            nc.gpsimd.indirect_dma_start(
                                out=rows[:, j, :], out_offset=None, in_=table[:, :],
                                in_offset=bass.IndirectOffsetOnAxis(ap=index[:, j:j + 1], axis=0)).then_inc(landed[j], 16)

            branch(pool, in_windows, anywhere)

        @block.vector
        def _(dve):
            def in_windows():
                def make_hot(c, j):
                    nc.vector.tensor_scalar(hot[:, j, :], m.iota[:], m.dloc[:, ds(c, 1)], None,
                                            ALU.is_equal).then_inc(hot_ready, 1)

                for j in range(R):
                    make_hot(j, j)

                def add(c, j, base, first=False):
                    dve.wait_ge(summed, c + 1)
                    if not first:
                        dve.wait_ge(added, c)
                    window = m.agg[:, :, ds(base, WINDOW)]
                    nc.vector.tensor_tensor(window, window, part_ps(j), ALU.add).then_inc(added, 1)

                def bases(c):
                    _, values = nc.values_load_multi_w_load_instructions(
                        m.dst[0:1, ds(c, H)], engines=(dve.engine,), min_val=0, max_val=m.nodes - 1,
                        skip_runtime_bounds_check_because="targets are node numbers")
                    return values

                for h in range(2):
                    for j, base in enumerate(bases(h * H), h * H):
                        add(j, j, base, first=(j == 0))
                        make_hot(R + j, j)
                with dve.Fori(1, loops - 1) as g:
                    for h in range(2):
                        for j, base in enumerate(bases(g * R + h * H), h * H):
                            add(g * R + j, j, base)
                            make_hot((g + 1) * R + j, j)
                for h in range(2):
                    for j, base in enumerate(bases((loops - 1) * R + h * H), h * H):
                        add((loops - 1) * R + j, j, base)

            def anywhere():
                nc.vector.tensor_copy(places[:], m.iota[:]).then_inc(moved, 1)
                nc.vector.nop().then_inc(tile_free, 1)
                with dve.Fori(0, m.tiles) as w:
                    dve.wait_ge(moved, w + 1)
                    nc.vector.nop(nofuse=True)
                    with dve.Fori(0, loops) as g:
                        dve.wait_ge(group_free, w * loops + (g + 1))
                        for j in range(R):
                            nc.vector.tensor_scalar(hot[:, j, :], places[:], m.dst_f[:, ds(g * R + j, 1)], None,
                                                    ALU.is_equal).then_inc(hot_ready, 1)
                    dve.wait_ge(summed, w + 1)
                    tile = m.agg[:, :, ds(w * P, P)]
                    nc.vector.tensor_tensor(tile, tile, m.ps[:, 0:DK, 0:P], ALU.add).then_inc(tile_free, 1)
                    nc.vector.tensor_scalar(places[:], places[:], float(P), None, ALU.add).then_inc(moved, 1)

            branch(dve, in_windows, anywhere)

        @block.tensor
        def _(pe):
            def in_windows():
                def multiply(c, j, round_):
                    pe.wait_ge(landed[j], round_ * 16)
                    pe.wait_ge(hot_ready, c + 1)
                    for k in range(DK):
                        last = nc.tensor.matmul(part_ps(j)[:, k, :], rows[:, j, k * P:(k + 1) * P], hot[:, j, :],
                                                start=True, stop=True)
                    last.then_inc(summed, 1)

                for j in range(R):
                    if j >= B:
                        pe.wait_ge(added, j + 1 - B)
                    multiply(j, j, 1)
                with pe.Fori(1, loops) as g:
                    for j in range(R):
                        pe.wait_ge(added, g * R + (j + 1 - B))
                        multiply(g * R + j, j, g + 1)

            def anywhere():
                def group(w, g, first, last):
                    pe.wait_ge(hot_ready, (w * loops + g) * R + R)
                    for j in range(R):
                        pe.wait_ge(landed[j], (w * loops + (g + 1)) * 16)
                        for k in range(DK):
                            mm = nc.tensor.matmul(m.ps[:, k, 0:P], rows[:, j, k * P:(k + 1) * P], hot[:, j, :],
                                                  start=first and j == 0, stop=last and j == R - 1,
                                                  skip_group_check=True)
                    mm.then_inc(group_free, 1)
                    return mm

                nc.tensor.nop().then_inc(group_free, 1)
                with pe.Fori(0, m.tiles) as w:
                    pe.wait_ge(tile_free, w + 1)
                    group(w, 0, True, False)
                    with pe.Fori(1, loops - 1) as g:
                        group(w, g, False, False)
                    group(w, loops - 1, False, True)
                    nc.tensor.drain().then_inc(summed, 1)

            branch(pe, in_windows, anywhere)


def update_nodes(nc, m, tag, w, bias, table):
    R = TILE_RING
    with Stage(nc) as ctx:
        sem = lambda name: ctx.sem(f"{tag}_{name}")
        cols = ctx.enter_context(nc.sbuf_tensor(f"{tag}_cols", [P, R, DK, P], F32))
        biased = ctx.enter_context(nc.sbuf_tensor(f"{tag}_biased", [P, R, D], F32))
        rows = ctx.enter_context(nc.sbuf_tensor(f"{tag}_rows", [P, R, D], F32))
        cols_ready, multiplied, biased_ready, rows_ready = sem("cols"), sem("multiplied"), sem("biased"), sem("rows")
        turned, kept = sem("turned"), sem("kept")
        stored = [sem(f"stored{j}") for j in range(R)]
        block = ctx.enter_context(nc.Block())

        def product_ps(j):
            return m.ps[:, j, 0:D]

        def turned_ps(j):
            return m.ps[:, j, D:2 * D].rearrange("p (k n) -> p k n", k=DK)

        @block.gpsimd
        def _(pool):
            def fetch(t, j, again, round_):
                if again:
                    pool.wait_ge(multiplied, t + (1 - R))
                    nc.gpsimd.nop(nofuse=True)
                nc.gpsimd.tensor_copy(cols[:, j, :, :], m.agg[:, :, ds(t * P, P)]).then_inc(cols_ready, 1)
            tile_loop(pool, m.tiles, [(0, fetch)])

        @block.tensor
        def _(pe):
            def multiply(t, j, again, round_):
                pe.wait_ge(cols_ready, t + 1)
                if again:
                    pe.wait_ge(kept, t + (1 - R))
                for k in range(DK):
                    last = nc.tensor.matmul(product_ps(j), cols[:, j, k, :], w[:, k, :], start=(k == 0),
                                            stop=(k == DK - 1))
                last.then_inc(multiplied, 1)

            def turn(t, j, again, round_):
                pe.wait_ge(rows_ready, t + 1)
                for k in range(DK):
                    last = nc.tensor.transpose(turned_ps(j)[:, k, :], rows[:, j, k * P:(k + 1) * P], m.ident[:])
                last.then_inc(turned, 1)
            tile_loop(pe, m.tiles, [(0, multiply), (3, turn)])

        @block.vector
        def _(dve):
            def add_bias(t, j, again, round_):
                dve.wait_ge(multiplied, t + 1)
                if again:
                    dve.wait_ge(rows_ready, t + (1 - R))
                nc.vector.scalar_tensor_tensor(biased[:, j, :], product_ps(j), m.dinv[:, ds(t, 1)], bias[:],
                                               ALU.mult, ALU.add).then_inc(biased_ready, 1)

            def keep(t, j, again, round_):
                dve.wait_ge(turned, t + 1)
                nc.vector.tensor_copy(m.agg[:, :, ds(t * P, P)], turned_ps(j)).then_inc(kept, 1)
            tile_loop(dve, m.tiles, [(0, add_bias), (4, keep)])

        @block.scalar
        def _(act):
            def rectify(t, j, again, round_):
                act.wait_ge(biased_ready, t + 1)
                if again:
                    act.wait_ge(turned, t + (1 - R))
                    act.wait_ge(stored[j], round_ * 16)
                nc.scalar.activation(rows[:, j, :], biased[:, j, :], ACT.Relu,
                                     scale=m.dinv[:, ds(t, 1)]).then_inc(rows_ready, 1)
            tile_loop(act, m.tiles, [(0, rectify)])

        @block.sync
        def _(sp):
            def store(t, j, again, round_):
                sp.wait_ge(rows_ready, t + 1)
                sp.dma_start(table[ds(t * P, P), :], rows[:, j, :]).then_inc(stored[j], 16)
            tile_loop(sp, m.tiles, [(0, store)])
            for j in range(R):
                sp.wait_ge(stored[j], m.tiles // R * 16)


def finish_gcn(nc, m, tag):
    R = TILE_RING
    with Stage(nc) as ctx:
        sem = lambda name: ctx.sem(f"{tag}_{name}")
        cols = ctx.enter_context(nc.sbuf_tensor(f"{tag}_cols", [P, R, DK, P], F32))
        biased = ctx.enter_context(nc.sbuf_tensor(f"{tag}_biased", [P, R, P], F32))
        rows = ctx.enter_context(nc.sbuf_tensor(f"{tag}_rows", [P, R, P], F32))
        turned = ctx.enter_context(nc.sbuf_tensor(f"{tag}_turned", [P, R, P], F32))
        cols_ready, multiplied, biased_ready, rows_ready = sem("cols"), sem("multiplied"), sem("biased"), sem("rows")
        turn_done, turned_ready, projected, x_biased, added = (sem("turn_done"), sem("turned"), sem("projected"),
                                                               sem("x_biased"), sem("added"))
        stats, pads_zero = RowStats(nc, m, ctx, "stats1"), sem("pads_zero")
        block = ctx.enter_context(nc.Block())

        @block.gpsimd
        def _(pool):
            def add_bias(t, j, again, round_):
                nc.gpsimd.tensor_tensor(tile_of(m.x, t), tile_of(m.x, t), m.bp[:], ALU.add).then_inc(x_biased, 1)
            tile_loop(pool, m.tiles, [(0, add_bias)])
            pool.wait_ge(stats.done, m.tiles)
            nc.gpsimd.affine_select(out=m.x[:, m.full_tiles, :], in_=m.x[:, m.full_tiles, :], compare_op=ALU.is_ge,
                                    fill=0.0, base=m.tail_nodes - 1, pattern=[[0, D]],
                                    channel_multiplier=-1).then_inc(pads_zero, 1)

        @block.tensor
        def _(pe):
            def multiply(t, j, again, round_):
                pe.wait_ge(cols_ready, t + 1)
                if again:
                    pe.wait_ge(added, t + (1 - R))
                for k in range(DK):
                    last = nc.tensor.matmul(m.ps[:, j, 0:P], cols[:, j, k, :], m.w3[:, k, :], start=(k == 0),
                                            stop=(k == DK - 1))
                last.then_inc(multiplied, 1)

            def turn(t, j, again, round_):
                pe.wait_ge(rows_ready, t + 1)
                nc.tensor.transpose(m.ps[:, j, P:2 * P], rows[:, j, :], m.ident[:]).then_inc(turn_done, 1)

            def project(t, j, again, round_):
                pe.wait_ge(turned_ready, t + 1)
                nc.tensor.matmul(m.ps[:, j, D:2 * D], turned[:, j, :], m.wp[:], start=True,
                                 stop=True).then_inc(projected, 1)
            tile_loop(pe, m.tiles, [(0, multiply), (2, turn), (4, project)])

        @block.vector
        def _(dve):
            def add_bias(t, j, again, round_):
                dve.wait_ge(multiplied, t + 1)
                if again:
                    dve.wait_ge(rows_ready, t + (1 - R))
                nc.vector.scalar_tensor_tensor(biased[:, j, :], m.ps[:, j, 0:P], m.dinv[:, ds(t, 1)], m.b3[:],
                                               ALU.mult, ALU.add).then_inc(biased_ready, 1)

            def add(t, j, again, round_):
                dve.wait_ge(projected, t + 1)
                dve.wait_ge(x_biased, t + 1)
                nc.vector.tensor_tensor(tile_of(m.x, t), tile_of(m.x, t), m.ps[:, j, D:2 * D],
                                        ALU.add).then_inc(added, 1)

            def measure(t, j, again, round_):
                dve.wait_ge(added, t + 1)
                stats.of_tile(t, tile_of(m.x, t))
            tile_loop(dve, m.tiles, [(0, add_bias), (5, add), (6, measure)])
            dve.wait_ge(pads_zero, 1)
            stats.of_tile(m.full_tiles, m.x[:, m.full_tiles, :])
            stats.on_vector(dve, m.tiles + 1)

        @block.scalar
        def _(act):
            def fetch(t, j, again, round_):
                if again:
                    act.wait_ge(multiplied, t + (1 - R))
                nc.scalar.copy(cols[:, j, :, :], m.agg[:, :, ds(t * P, P)]).then_inc(cols_ready, 1)

            def rectify(t, j, again, round_):
                act.wait_ge(biased_ready, t + 1)
                if again:
                    act.wait_ge(turn_done, t + (1 - R))
                nc.scalar.activation(rows[:, j, :], biased[:, j, :], ACT.Relu).then_inc(rows_ready, 1)

            def keep(t, j, again, round_):
                act.wait_ge(turn_done, t + 1)
                if again:
                    act.wait_ge(projected, t + (1 - R))
                nc.scalar.copy(turned[:, j, :], m.ps[:, j, P:2 * P]).then_inc(turned_ready, 1)
            tile_loop(act, m.tiles, [(0, fetch), (2, rectify), (4, keep)])
            stats.on_scalar(act)


def route_all(nc, m, a):
    E = m.experts
    capacity = float(ceil_div(m.nodes * 5, 4 * E))
    with Stage(nc) as ctx:
        sem = lambda name: ctx.sem(f"route_{name}")
        buf = lambda name, shape, dt=F32: ctx.enter_context(nc.sbuf_tensor(f"route_{name}", shape, dt))
        wr, br, mean_col = buf("wr", [P, DK, E]), buf("br", [1, E]), buf("mean_col", [P, DK])
        row, tmp, prob = buf("row", [1, E]), buf("tmp", [1, E]), buf("prob", [1, E])
        over, ratio, expd = buf("over", [1, E]), buf("ratio", [1, E]), buf("expd", [1, E])
        rev_i, rev = buf("rev_i", [1, E], I32), buf("rev", [1, E])
        peak, total, inv = buf("peak", [1, 4]), buf("total", [1, 2]), buf("inv", [1, 2])
        top, code = buf("top", [1, 2]), buf("code", [1, 2])
        choice_f, choice, share = buf("choice_f", [1, 2]), buf("choice", [1, 2], I32), buf("share", [1, 4])
        shares, b2_rows = buf("shares", [P, 2]), buf("b2_rows", [P, 2, D])
        w1, w2 = buf("w1", [P, 2, DK, m.hidden0]), buf("w2", [P, 2, m.hidden0 // P, D])
        rounded, w2_scaled = sem("rounded"), sem("w2_scaled")
        loaded, turned, col_ready, scored = sem("loaded"), sem("turned"), sem("col_ready"), sem("scored")
        chain, exp_asked, exp_done, rev_made = sem("chain"), sem("exp_asked"), sem("exp_done"), sem("rev_made")
        chosen, share_ready, spread, fetched = sem("chosen"), sem("share_ready"), sem("spread"), sem("fetched")
        block = ctx.enter_context(nc.Block())

        @block.sync
        def _(sp):
            sp.dma_start(wr[:], a["ffn0_wr"].rearrange("(k p) e -> p k e", p=P)).then_inc(loaded, 16)
            sp.dma_start(br[:], a["ffn0_br"].rearrange("(o e) -> o e", o=1)).then_inc(loaded, 16)
            sp.wait_ge(chosen, 1)
            for n in range(2):
                e = sp.value_load(choice[0:1, n:n + 1], min_val=0, max_val=E - 1)
                sp.dma_start(w1[:, n, :, :], a["ffn0_w1"][ds(e, 1), :, :]
                             .rearrange("o (k p) f -> p (o k) f", p=P)).then_inc(fetched, 16)
                sp.dma_start(w2[:, n, :, :], a["ffn0_w2"][ds(e, 1), :, :]
                             .rearrange("o (k p) f -> p (o k) f", p=P)).then_inc(fetched, 16)
                sp.dma_start(m.f0_b1[:, n, :], a["ffn0_b1"][ds(e, 1), :, :]
                             .rearrange("o p f -> p (o f)")).then_inc(fetched, 16)
                sp.dma_start(b2_rows[:, n, :], a["ffn0_b2"][ds(e, 1), :]
                             .rearrange("o d -> (o d)").partition_broadcast(P)).then_inc(fetched, 16)
            sp.dma_start(m.gamma[:], a["ffn0_gamma"].partition_broadcast(P)).then_inc(fetched, 16)
            sp.dma_start(m.beta[:], a["ffn0_beta"].partition_broadcast(P)).then_inc(fetched, 16)
            sp.wait_ge(fetched, 16 * 10)

        @block.gpsimd
        def _(pool):
            nc.gpsimd.iota(rev_i[:], pattern=[[-1, E]], base=E, channel_multiplier=0).then_inc(rev_made, 1)

        @block.tensor
        def _(pe):
            for k in range(DK):
                last = nc.tensor.matmul(m.ps[:, 0, k:k + 1], m.mean_row[0:1, k * P:(k + 1) * P], m.ones[0:1, 0:1],
                                        start=True, stop=True)
            last.then_inc(turned, 1)
            pe.wait_ge(col_ready, 1)
            pe.wait_ge(loaded, 32)
            for k in range(DK):
                last = nc.tensor.matmul(m.ps[0:1, 1, 0:E], mean_col[:, k:k + 1], wr[:, k, :], start=(k == 0),
                                        stop=(k == DK - 1))
            last.then_inc(scored, 1)
            pe.wait_ge(share_ready, 1)
            nc.tensor.matmul(m.ps[:, 2, 0:2], m.ones[0:1, :], share[0:1, 2:4], start=True, stop=True).then_inc(spread, 1)

        @block.scalar
        def _(act):
            for n in range(2):
                act.wait_ge(exp_asked, n + 1)
                nc.scalar.activation(expd[:], row[:], ACT.Exp, bias=peak[0:1, n:n + 1],
                                     accum_out=total[0:1, n:n + 1]).then_inc(exp_done, 1)
            act.wait_ge(exp_asked, 3)
            nc.scalar.activation(share[0:1, 1:2], share[0:1, 0:1], ACT.Exp).then_inc(exp_done, 1)
            act.wait_ge(fetched, 16 * 10)
            nc.scalar.copy(m.f0_w1_hi[:], w1[:]).then_inc(rounded, 1)
            for n in range(2):
                act.wait_ge(w2_scaled, n + 1)
                nc.scalar.copy(m.f0_w2_hi[:, n, :, :], w2[:, n, :, :]).then_inc(rounded, 1)

        @block.vector
        def _(dve):
            links = [0]

            def link(ins):
                links[0] += 1
                ins.then_inc(chain, 1)
                dve.wait_ge(chain, links[0])

            def softmax(n, out):
                link(nc.vector.reduce_max(peak[0:1, 2:3], row[:], AX.X))
                nc.vector.tensor_scalar(peak[0:1, n:n + 1], peak[0:1, 2:3], -1.0, None, ALU.mult).then_inc(exp_asked, 1)
                dve.wait_ge(exp_done, n + 1)
                link(nc.vector.reciprocal(inv[0:1, n:n + 1], total[0:1, n:n + 1]))
                link(nc.vector.tensor_scalar(out, expd[:], inv[0:1, n:n + 1], None, ALU.mult))

            dve.wait_ge(turned, 1)
            nc.vector.tensor_copy(mean_col[:], m.ps[:, 0, 0:DK]).then_inc(col_ready, 1)
            dve.wait_ge(rev_made, 1)
            nc.vector.tensor_copy(rev[:], rev_i[:])
            dve.wait_ge(scored, 1)
            link(nc.vector.tensor_tensor(row[:], m.ps[0:1, 1, 0:E], br[:], ALU.add))
            softmax(0, prob[:])
            link(nc.vector.tensor_scalar(tmp[:], prob[:], float(m.nodes), None, ALU.mult))
            link(nc.vector.tensor_scalar(over[:], tmp[:], capacity, None, ALU.is_gt))
            link(nc.vector.tensor_scalar(tmp[:], tmp[:], capacity, None, ALU.max))
            link(nc.vector.reciprocal(ratio[:], tmp[:]))
            link(nc.vector.scalar_tensor_tensor(ratio[:], ratio[:], capacity, over[:], ALU.mult, ALU.mult))
            link(nc.vector.tensor_scalar(over[:], over[:], -1.0, 1.0, ALU.mult, ALU.add))
            link(nc.vector.tensor_tensor(ratio[:], ratio[:], over[:], ALU.add))
            link(nc.vector.tensor_tensor(row[:], prob[:], ratio[:], ALU.mult))
            softmax(1, prob[:])
            for n in range(2):
                link(nc.vector.reduce_max(top[0:1, n:n + 1], prob[:], AX.X))
                link(nc.vector.tensor_scalar(tmp[:], prob[:], top[0:1, n:n + 1], None, ALU.is_equal))
                link(nc.vector.tensor_tensor(tmp[:], tmp[:], rev[:], ALU.mult))
                link(nc.vector.reduce_max(code[0:1, n:n + 1], tmp[:], AX.X))
                if n == 0:
                    link(nc.vector.tensor_scalar(tmp[:], rev[:], code[0:1, 0:1], -2.0, ALU.is_equal, ALU.mult))
                    link(nc.vector.tensor_tensor(prob[:], prob[:], tmp[:], ALU.add))
            link(nc.vector.tensor_scalar(choice_f[:], code[:], -1.0, float(E), ALU.mult, ALU.add))
            nc.vector.tensor_copy(choice[:], choice_f[:]).then_inc(chosen, 1)
            nc.vector.tensor_tensor(share[0:1, 0:1], top[0:1, 1:2], top[0:1, 0:1], ALU.subtract).then_inc(exp_asked, 1)
            dve.wait_ge(exp_done, 3)
            link(nc.vector.tensor_scalar(inv[0:1, 0:1], share[0:1, 1:2], 1.0, None, ALU.add))
            link(nc.vector.reciprocal(share[0:1, 2:3], inv[0:1, 0:1]))
            nc.vector.tensor_tensor(share[0:1, 3:4], share[0:1, 1:2], share[0:1, 2:3], ALU.mult).then_inc(share_ready, 1)
            dve.wait_ge(spread, 1)
            link(nc.vector.tensor_copy(shares[:], m.ps[:, 2, 0:2]))
            dve.wait_ge(fetched, 16 * 10)
            for n in range(2):
                nc.vector.tensor_scalar(w2[:, n, :, :], w2[:, n, :, :], shares[:, n:n + 1], None,
                                        ALU.mult).then_inc(w2_scaled, 1)
            link(nc.vector.tensor_scalar(m.f0_b2[:], b2_rows[:, 0, :], shares[:, 0:1], None, ALU.mult))
            nc.vector.scalar_tensor_tensor(m.f0_b2[:], b2_rows[:, 1, :], shares[:, 1:2], m.f0_b2[:],
                                           ALU.mult, ALU.add)
            dve.wait_ge(rounded, 1)
            nc.vector.tensor_tensor(m.f0_w1_lo[:], w1[:], m.f0_w1_hi[:].bitcast(F32), ALU.subtract)
            for n in range(2):
                dve.wait_ge(rounded, n + 2)
                nc.vector.tensor_tensor(m.f0_w2_lo[:, n, :, :], w2[:, n, :, :], m.f0_w2_hi[:, n, :, :].bitcast(F32),
                                        ALU.subtract)


def multiply_halves(nc, out, left, right, start, stop):
    for n, (i, j) in enumerate(((1, 0), (0, 1), (0, 0))):
        last = nc.tensor.matmul(out, left[i], right[j], start=start and n == 0, stop=stop and n == 2,
                                skip_group_check=True)
    return last


def two_experts(nc, m):
    T = 4
    F = 2 * m.hidden0 // P
    LAG, HID_RING = 4, 2
    chunks = m.tiles // T
    assert m.tiles % T == 1
    with Stage(nc) as ctx:
        sem = lambda name: ctx.sem(f"two_{name}")
        cols_hi, cols_lo = (ctx.enter_context(nc.sbuf_tensor(f"two_cols_{half}", [P, DK, T * P], F32R))
                            for half in ("hi", "lo"))
        hid = ctx.enter_context(nc.sbuf_tensor("two_hid", [P, HID_RING, T * P], F32))
        hid_hi, hid_lo = (ctx.enter_context(nc.sbuf_tensor(f"two_hid_{half}", [P, F, T * P], F32R))
                          for half in ("hi", "lo"))
        up_done, gelu_done, down_done = sem("up"), sem("gelu"), sem("down")
        own_made, own_biased, added = sem("own_made"), sem("own_biased"), sem("added")
        stats = RowStats(nc, m, ctx, "stats2")
        cols_rounded, cols_split, hid_rounded, hid_split = (sem("cols_rounded"), sem("cols_split"),
                                                            sem("hid_rounded"), sem("hid_split"))
        block = ctx.enter_context(nc.Block())

        def cols_of(c, width):
            return m.agg[:, :, ds(c * T * P, width)]

        def down_ps(i):
            return m.ps[:, 4 + i // 2, i % 2 * D:(i % 2 + 1) * D]

        @block.tensor
        def _(pe):
            def up(c, f, width, first):
                if not first or f >= 4:
                    pe.wait_ge(gelu_done, c * F + (f - 3))
                e, at = f // (F // 2), ds(f % (F // 2) * P, P)
                for k in range(DK):
                    last = multiply_halves(nc, m.ps[:, f % 4, 0:width], (m.f0_w1_hi[:, e, k, at], m.f0_w1_lo[:, e, k, at]),
                                           (cols_hi[:, k, 0:width], cols_lo[:, k, 0:width]), k == 0, k == DK - 1)
                last.then_inc(up_done, 1)

            def down(c, f, tiles, first):
                pe.wait_ge(hid_split, c * F + (f + 1))
                if f == 0 and not first:
                    pe.wait_ge(added, c * T)
                e, s = f // (F // 2), f % (F // 2)
                for i in range(tiles):
                    at = slice(i * P, (i + 1) * P)
                    last = multiply_halves(nc, down_ps(i), (hid_hi[:, f, at], hid_lo[:, f, at]),
                                           (m.f0_w2_hi[:, e, s, :], m.f0_w2_lo[:, e, s, :]),
                                           f == 0 and i % 2 == 0, f == F - 1)
                last.then_inc(down_done, 1)

            def both(c, first=False, width=T * P, tiles=T):
                pe.wait_ge(cols_split, c + 1)
                for f in range(F):
                    up(c, f, width, first)
                    if f >= LAG:
                        down(c, f - LAG, tiles, first)
                for f in range(F - LAG, F):
                    down(c, f, tiles, first)

            both(0, first=True)
            with pe.Fori(1, chunks) as c:
                both(c)
            both(chunks, width=P, tiles=1)

        @block.scalar
        def _(act):
            def gelu(c, width, first=False):
                nc.scalar.copy(cols_hi[:, :, 0:width], cols_of(c, width)).then_inc(cols_rounded, 1)
                for f in range(F):
                    if not first or f >= HID_RING:
                        act.wait_ge(hid_split, c * F + (f + 1 - HID_RING))
                    act.wait_ge(up_done, c * F + (f + 1))
                    nc.scalar.activation(hid[:, f % HID_RING, 0:width], m.ps[:, f % 4, 0:width], ACT.Gelu,
                                         bias=m.f0_b1[:, f // (F // 2), f % (F // 2):f % (F // 2) + 1])\
                        .then_inc(gelu_done, 1)
                    act.wait_ge(gelu_done, c * F + (f + 1))
                    if not first:
                        act.wait_ge(down_done, c * F + (f + 1 - F))
                    nc.scalar.copy(hid_hi[:, f, 0:width], hid[:, f % HID_RING, 0:width]).then_inc(hid_rounded, 1)

            gelu(0, T * P, first=True)
            with act.Fori(1, chunks) as c:
                act.wait_ge(up_done, c * F)
                gelu(c, T * P)
            act.wait_ge(up_done, chunks * F)
            gelu(chunks, P)
            stats.on_scalar(act)

        @block.vector
        def _(dve):
            def split_cols(c, width):
                dve.wait_ge(cols_rounded, c + 1)
                nc.vector.tensor_tensor(cols_lo[:, :, 0:width], cols_of(c, width),
                                        cols_hi[:, :, 0:width].bitcast(F32), ALU.subtract).then_inc(cols_split, 1)

            def split_hid(c, fs, width):
                for f in fs:
                    dve.wait_ge(hid_rounded, c * F + (f + 1))
                    nc.vector.tensor_tensor(hid_lo[:, f, 0:width], hid[:, f % HID_RING, 0:width],
                                            hid_hi[:, f, 0:width].bitcast(F32), ALU.subtract).then_inc(hid_split, 1)

            def rows_of(c, i):
                return m.agg[:, :, ds((c * T + i) * P, P)]

            def make_own(c, tiles):
                dve.wait_ge(cols_split, c + 1)
                for i in range(tiles):
                    t = c * T + i
                    nc.vector.tensor_scalar(rows_of(c, i), m.x[:, ds(t, 1), :].rearrange("p t (k n) -> p (t k) n", k=DK),
                                            m.mean[:, ds(t, 1)], m.scale[:, ds(t, 1)],
                                            ALU.subtract, ALU.mult).then_inc(own_made, 1)
                for i in range(tiles):
                    dve.wait_ge(own_made, c * T + (i + 1))
                    nc.vector.tensor_tensor(rows_of(c, i), rows_of(c, i), m.f0_b2[:].rearrange("p (k n) -> p k n", k=DK),
                                            ALU.add).then_inc(own_biased, 1)

            def combine(c, tiles):
                dve.wait_ge(down_done, c * F + F)
                for i in range(tiles):
                    dve.wait_ge(own_biased, c * T + (i + 1))
                    nc.vector.tensor_tensor(rows_of(c, i), rows_of(c, i),
                                            down_ps(i).rearrange("p (k n) -> p k n", k=DK), ALU.add).then_inc(added, 1)
                for i in range(tiles):
                    dve.wait_ge(added, c * T + (i + 1))
                    stats.of_tile(c * T + i, rows_of(c, i))

            def hidden_and_own(c, width, tiles):
                split_hid(c, range(LAG), width)
                make_own(c, tiles)
                split_hid(c, range(LAG, F), width)

            split_cols(0, T * P)
            with dve.Fori(0, chunks - 1) as c:
                hidden_and_own(c, T * P, T)
                dve.wait_ge(up_done, c * F + F)
                split_cols(c + 1, T * P)
                combine(c, T)
            hidden_and_own(chunks - 1, T * P, T)
            split_cols(chunks, P)
            combine(chunks - 1, T)
            hidden_and_own(chunks, P, 1)
            combine(chunks, 1)
            stats.on_vector(dve, m.tiles)


def add_normalized(nc, m):
    R = TILE_RING
    with Stage(nc) as ctx:
        sem = lambda name: ctx.sem(f"addn_{name}")
        scaled = ctx.enter_context(nc.sbuf_tensor("addn_scaled", [P, R, D], F32))
        x_shifted, scaled_made, x_done = sem("x_shifted"), sem("scaled"), sem("x_done")
        stats = RowStats(nc, m, ctx, "stats3")
        block = ctx.enter_context(nc.Block())

        @block.gpsimd
        def _(pool):
            def shift(t, j, again, round_):
                nc.gpsimd.tensor_tensor(tile_of(m.x, t), tile_of(m.x, t), m.beta[:], ALU.add).then_inc(x_shifted, 1)
            tile_loop(pool, m.tiles, [(0, shift)])

        @block.vector
        def _(dve):
            def scale(t, j, again, round_):
                if again:
                    dve.wait_ge(x_done, t + (1 - R))
                nc.vector.scalar_tensor_tensor(scaled[:, j, :].rearrange("p (k n) -> p k n", k=DK),
                                               m.agg[:, :, ds(t * P, P)], m.mean[:, ds(t, 1)],
                                               m.gamma[:].rearrange("p (k n) -> p k n", k=DK),
                                               ALU.subtract, ALU.mult).then_inc(scaled_made, 1)

            def add(t, j, again, round_):
                dve.wait_ge(scaled_made, t + 1)
                dve.wait_ge(x_shifted, t + 1)
                nc.vector.scalar_tensor_tensor(tile_of(m.x, t), scaled[:, j, :], m.scale[:, ds(t, 1)],
                                               tile_of(m.x, t), ALU.mult, ALU.add).then_inc(x_done, 1)

            def measure(t, j, again, round_):
                dve.wait_ge(x_done, t + 1)
                stats.of_tile(t, tile_of(m.x, t))
            tile_loop(dve, m.tiles, [(0, scale), (1, add), (2, measure)])
            stats.on_vector(dve, m.tiles)

        @block.scalar
        def _(act):
            stats.on_scalar(act)


def project_heads(nc, m, a, heads_table, left_table):
    R = TILE_RING
    H = m.heads
    with Stage(nc) as ctx:
        sem = lambda name: ctx.sem(f"proj_{name}")
        buf = lambda name, shape, dt=F32: ctx.enter_context(nc.sbuf_tensor(f"proj_{name}", shape, dt))
        w, attn, prod = buf("w", [P, DK, D + 2 * H]), buf("attn", [P, 2, D]), buf("prod", [P, D])
        ring, cols, out = buf("ring", [P, R, D]), buf("cols", [P, R, DK, P]), buf("out", [P, R, D + 2 * H])
        loaded, prod_made, wa_made = sem("loaded"), sem("prod_made"), sem("wa_made")
        rows_ready, turned, cols_ready, multiplied = sem("rows"), sem("turned"), sem("cols"), sem("multiplied")
        heads_kept = sem("heads_kept")
        stored = [sem(f"stored{j}") for j in range(R)]
        block = ctx.enter_context(nc.Block())

        @block.sync
        def _(sp):
            sp.dma_start(w[:, :, 0:D], a["gat_w"].rearrange("(k p) n -> p k n", p=P)).then_inc(loaded, 16)
            sp.dma_start(attn[:, 0, :], a["gat_l"].rearrange("h d -> (h d)").partition_broadcast(P)).then_inc(loaded, 16)
            sp.dma_start(attn[:, 1, :], a["gat_r"].rearrange("h d -> (h d)").partition_broadcast(P)).then_inc(loaded, 16)

            def store(t, j, again, round_):
                sp.wait_ge(heads_kept, t + 1)
                sp.dma_start(heads_table[ds(t * P, P), :], out[:, j, 0:D + H]).then_inc(stored[j], 16)
                sp.dma_start(left_table[ds(t * P, P), :], out[:, j, D + H:D + 2 * H]).then_inc(stored[j], 16)
            tile_loop(sp, m.tiles, [(0, store)])
            for j in range(R):
                sp.wait_ge(stored[j], m.tiles // R * 32)

        @block.vector
        def _(dve):
            dve.wait_ge(loaded, 48)
            for n, side in enumerate((1, 0)):
                for k in range(DK):
                    s = n * DK + k
                    if s:
                        dve.wait_ge(wa_made, s)
                    nc.vector.tensor_tensor(prod[:], w[:, k, 0:D], attn[:, side, :], ALU.mult).then_inc(prod_made, 1)
                    dve.wait_ge(prod_made, s + 1)
                    nc.vector.reduce_sum(w[:, k, D + n * H:D + (n + 1) * H], prod[:].rearrange("p (h d) -> p h d", h=H),
                                         AX.X).then_inc(wa_made, 1)

            def rows(t, j, again, round_):
                if again:
                    dve.wait_ge(turned, t + (1 - R))
                nc.vector.tensor_scalar(ring[:, j, :], tile_of(m.x, t), m.mean[:, ds(t, 1)], m.scale[:, ds(t, 1)],
                                        ALU.subtract, ALU.mult).then_inc(rows_ready, 1)

            tile_loop(dve, m.tiles, [(0, rows)])

        @block.scalar
        def _(act):
            def keep_cols(t, j, again, round_):
                act.wait_ge(turned, t + 1)
                if again:
                    act.wait_ge(multiplied, t + (1 - R))
                nc.scalar.copy(cols[:, j, :, :],
                               m.ps[:, j, 0:D].rearrange("p (k n) -> p k n", k=DK)).then_inc(cols_ready, 1)

            def keep_heads(t, j, again, round_):
                act.wait_ge(multiplied, t + 1)
                if again:
                    act.wait_ge(stored[j], round_ * 32)
                nc.scalar.copy(out[:, j, :], m.ps[:, j, 0:D + 2 * H]).then_inc(heads_kept, 1)
            tile_loop(act, m.tiles, [(0, keep_cols), (2, keep_heads)])

        @block.tensor
        def _(pe):
            def turn(t, j, again, round_):
                pe.wait_ge(rows_ready, t + 1)
                if again:
                    pe.wait_ge(heads_kept, t + (1 - R))
                for k in range(DK):
                    last = nc.tensor.transpose(m.ps[:, j, k * P:(k + 1) * P], ring[:, j, k * P:(k + 1) * P], m.ident[:])
                last.then_inc(turned, 1)

            def multiply(t, j, again, round_):
                pe.wait_ge(cols_ready, t + 1)
                for k in range(DK):
                    last = nc.tensor.matmul(m.ps[:, j, 0:D + 2 * H], cols[:, j, k, :], w[:, k, :], start=(k == 0),
                                            stop=(k == DK - 1))
                last.then_inc(multiplied, 1)

            pe.wait_ge(wa_made, 2 * DK)
            tile_loop(pe, m.tiles, [(0, turn), (2, multiply)])


def attend(nc, m, heads_table, left_table):
    R = TILE_RING
    H = m.heads
    with Stage(nc) as ctx:
        sem = lambda name: ctx.sem(f"att_{name}")
        buf = lambda name, shape, dt=F32: ctx.enter_context(nc.sbuf_tensor(f"att_{name}", shape, dt))
        src_col, dst_col = buf("src_col", [P, R], I32), buf("dst_col", [P, R], I32)
        rows, left = buf("rows", [P, R, D + H]), buf("left", [P, R, H])
        score, flat, peak = buf("score", [P, R, H]), buf("flat", [P, R, H]), buf("peak", [P, R])
        weight, total, inv = buf("weight", [P, R, H]), buf("total", [P, R]), buf("inv", [P, R])
        prod, head_sum = buf("prod", [P, R, D]), buf("head_sum", [P, R, D // H])
        index_ready, chain, scores_ready, exp_done, used = (sem("index_ready"), sem("chain"), sem("scores_ready"),
                                                            sem("exp_done"), sem("used"))
        landed = [sem(f"landed{j}") for j in range(R)]
        stats = RowStats(nc, m, ctx, "stats4")
        block = ctx.enter_context(nc.Block())

        @block.scalar
        def _(act):
            def put_index(t, j, again, round_):
                if again:
                    act.wait_ge(landed[j], round_ * 32)
                nc.scalar.copy(src_col[:, j:j + 1], m.src[:, ds(t, 1)]).then_inc(index_ready, 1)
                nc.scalar.copy(dst_col[:, j:j + 1], m.dst[:, ds(t, 1)]).then_inc(index_ready, 1)

            def exps(t, j, again, round_):
                act.wait_ge(scores_ready, t + 1)
                if again:
                    act.wait_ge(used, t + (1 - R))
                nc.scalar.activation(weight[:, j, :], score[:, j, :], ACT.Exp, bias=peak[:, j:j + 1],
                                     accum_out=total[:, j:j + 1]).then_inc(exp_done, 1)
            tile_loop(act, m.tiles, [(0, put_index), (5, exps)])
            stats.on_scalar(act)

        @block.gpsimd
        def _(pool):
            def gather(t, j, again, round_):
                pool.wait_ge(index_ready, t * 2 + 2)
                if again:
                    pool.wait_ge(used, t + (1 - R))
                nc.gpsimd.nop(nofuse=True)
                nc.gpsimd.indirect_dma_start(
                    out=rows[:, j, :], out_offset=None, in_=heads_table[:, :],
                    in_offset=bass.IndirectOffsetOnAxis(ap=dst_col[:, j:j + 1], axis=0)).then_inc(landed[j], 16)
                nc.gpsimd.indirect_dma_start(
                    out=left[:, j, :], out_offset=None, in_=left_table[:, :],
                    in_offset=bass.IndirectOffsetOnAxis(ap=src_col[:, j:j + 1], axis=0)).then_inc(landed[j], 16)
            tile_loop(pool, m.tiles, [(0, gather)])

        @block.vector
        def _(dve):
            STEPS = 7

            def scores(t, j, again, round_):
                dve.wait_ge(landed[j], (round_ + 1) * 32)
                nc.vector.tensor_tensor(flat[:, j, :], left[:, j, :], rows[:, j, D:D + H], ALU.add).then_inc(chain, 1)

            def leak(t, j, again, round_):
                dve.wait_ge(chain, 1 + t)
                nc.vector.scalar_tensor_tensor(score[:, j, :], flat[:, j, :], 0.01, flat[:, j, :], ALU.mult,
                                               ALU.max).then_inc(leaked, 1)

            def peaks(t, j, again, round_):
                dve.wait_ge(leaked, 1 + t)
                nc.vector.tensor_reduce(peak[:, j:j + 1], score[:, j, :], AX.X, ALU.max,
                                        negate=True).then_inc(scores_ready, 1)

            def weigh(t, j, again, round_):
                dve.wait_ge(exp_done, t + 1)
                nc.vector.reciprocal(inv[:, j:j + 1], total[:, j:j + 1]).then_inc(inverted, 1)
                nc.vector.tensor_tensor(prod[:, j, :].rearrange("p (h d) -> p h d", h=H),
                                        rows[:, j, 0:D].rearrange("p (h d) -> p h d", h=H),
                                        weight[:, j, :].unsqueeze(2).to_broadcast([P, H, D // H]),
                                        ALU.mult).then_inc(weighed, 1)

            def sum_heads(t, j, again, round_):
                dve.wait_ge(weighed, t + 1)
                nc.vector.reduce_sum(head_sum[:, j, :], prod[:, j, :].rearrange("p (h d) -> p d h", h=H),
                                     AX.X).then_inc(head_summed, 1)

            def add(t, j, again, round_):
                dve.wait_ge(head_summed, t + 1)
                dve.wait_ge(inverted, t + 1)
                xt = tile_of(m.x, t).rearrange("p (h d) -> p h d", h=H)
                nc.vector.scalar_tensor_tensor(xt, head_sum[:, j, :].unsqueeze(1).to_broadcast([P, H, D // H]),
                                               inv[:, j:j + 1], xt, ALU.mult, ALU.add).then_inc(used, 1)

            leaked, inverted, weighed, head_summed = sem("leaked"), sem("inverted"), sem("weighed"), sem("head_summed")
            def measure(t, j, again, round_):
                dve.wait_ge(used, t + 1)
                stats.of_tile(t, tile_of(m.x, t))
            tile_loop(dve, m.tiles, [(0, scores), (0, leak), (0, peaks), (1, weigh), (1, sum_heads), (1, add), (2, measure)])
            stats.on_vector(dve, m.tiles)


def score_experts(nc, m, a):
    R = TILE_RING
    E = m.experts
    with Stage(nc) as ctx:
        sem = lambda name: ctx.sem(f"gate_{name}")
        buf = lambda name, shape, dt=F32: ctx.enter_context(nc.sbuf_tensor(f"gate_{name}", shape, dt))
        w, b = buf("w", [P, DK, E]), buf("b", [P, E])
        ring, cols = buf("ring", [P, R, D]), buf("cols", [P, R, DK, P])
        loaded, rows_ready, turned, cols_ready = sem("loaded"), sem("rows"), sem("turned"), sem("cols")
        multiplied, kept = sem("multiplied"), sem("kept")
        block = ctx.enter_context(nc.Block())

        @block.sync
        def _(sp):
            sp.dma_start(w[:], a["gate_w"].rearrange("(k p) n -> p k n", p=P)).then_inc(loaded, 16)
            sp.dma_start(b[:], a["gate_b"].partition_broadcast(P)).then_inc(loaded, 16)

        @block.vector
        def _(dve):
            def rows(t, j, again, round_):
                if again:
                    dve.wait_ge(turned, t + (1 - R))
                nc.vector.tensor_scalar(ring[:, j, :], tile_of(m.x, t), m.mean[:, ds(t, 1)], m.scale[:, ds(t, 1)],
                                        ALU.subtract, ALU.mult).then_inc(rows_ready, 1)

            def keep(t, j, again, round_):
                dve.wait_ge(multiplied, t + 1)
                nc.vector.tensor_tensor(tile_of(m.gates, t), m.ps[:, j, D:D + E], b[:],
                                        ALU.add).then_inc(kept, 1)
            dve.wait_ge(loaded, 32)
            tile_loop(dve, m.tiles, [(0, rows), (4, keep)])

        @block.scalar
        def _(act):
            def keep_cols(t, j, again, round_):
                act.wait_ge(turned, t + 1)
                if again:
                    act.wait_ge(multiplied, t + (1 - R))
                nc.scalar.copy(cols[:, j, :, :],
                               m.ps[:, j, 0:D].rearrange("p (k n) -> p k n", k=DK)).then_inc(cols_ready, 1)
            tile_loop(act, m.tiles, [(0, keep_cols)])

        @block.tensor
        def _(pe):
            def turn(t, j, again, round_):
                pe.wait_ge(rows_ready, t + 1)
                if again:
                    pe.wait_ge(kept, t + (1 - R))
                for k in range(DK):
                    last = nc.tensor.transpose(m.ps[:, j, k * P:(k + 1) * P], ring[:, j, k * P:(k + 1) * P], m.ident[:])
                last.then_inc(turned, 1)

            def multiply(t, j, again, round_):
                pe.wait_ge(cols_ready, t + 1)
                for k in range(DK):
                    last = nc.tensor.matmul(m.ps[:, j, D:D + E], cols[:, j, k, :], w[:, k, :],
                                            start=(k == 0), stop=(k == DK - 1))
                last.then_inc(multiplied, 1)
            pe.wait_ge(loaded, 32)
            tile_loop(pe, m.tiles, [(0, turn), (2, multiply)])


def assign_slots(nc, m):
    E, T, C = m.experts, m.tiles, m.capacity
    with Stage(nc) as ctx:
        sem = lambda name: ctx.sem(f"slot_{name}")
        buf = lambda name, shape, dt=F32: ctx.enter_context(nc.sbuf_tensor(f"slot_{name}", shape, dt))
        peak, total, code = buf("peak", [P, T]), buf("total", [P, T]), buf("code", [P, T])
        low, one_hot = buf("low", [P, T, E]), buf("one_hot", [P, T, E])
        rev_i, rev = buf("rev_i", [P, E], I32), buf("rev", [P, E])
        upper = buf("upper", [P, P])
        sums = buf("sums", [P, 2, T, E])
        totals, place, kept_f = buf("totals", [P, T, E]), buf("place", [P, T]), buf("kept_f", [P, T])
        first, to, back = buf("first", [P, T]), buf("to", [P, T]), buf("back", [P, T])
        chain, rev_made, upper_made, low_ready, exp_done = (sem("chain"), sem("rev_made"), sem("upper_made"),
                                                            sem("low_ready"), sem("exp_done"))
        hot_ready, counted, to_ready, to_masked = sem("hot_ready"), sem("counted"), sem("to_ready"), sem("to_masked")
        block = ctx.enter_context(nc.Block())
        wide = lambda v: v.unsqueeze(2).to_broadcast([P, T, E])
        flat = lambda v: v.rearrange("p t e -> p (t e)")

        @block.gpsimd
        def _(pool):
            nc.gpsimd.iota(rev_i[:], pattern=[[-1, E]], base=E, channel_multiplier=0).then_inc(rev_made, 1)
            nc.gpsimd.memset(upper[:], 1.0).then_inc(rev_made, 1)
            pool.wait_ge(rev_made, 2)
            nc.gpsimd.affine_select(out=upper[:], in_=upper[:], compare_op=ALU.is_ge, fill=0.0, base=0,
                                    pattern=[[1, P]], channel_multiplier=-1).then_inc(upper_made, 1)
            pool.wait_ge(to_ready, 1)
            nc.gpsimd.affine_select(out=to[:, T - 1:T], in_=to[:, T - 1:T], compare_op=ALU.is_ge,
                                    fill=float(4 * E * C), base=m.tail_nodes - 1, pattern=[[0, 1]],
                                    channel_multiplier=-1).then_inc(to_masked, 1)

        @block.scalar
        def _(act):
            act.wait_ge(low_ready, 1)
            nc.scalar.activation(low[:], low[:], ACT.Exp).then_inc(exp_done, 1)

        @block.tensor
        def _(pe):
            pe.wait_ge(hot_ready, 1)
            pe.wait_ge(upper_made, 1)
            nc.tensor.matmul(m.ps[:, 0, 0:T * E], upper[:], flat(one_hot[:]), start=True, stop=True)
            nc.tensor.matmul(m.ps[:, 1, 0:T * E], m.ones[:], flat(one_hot[:]), start=True, stop=True).then_inc(counted, 1)

        @block.vector
        def _(dve):
            links = [0]

            def link(ins):
                links[0] += 1
                ins.then_inc(chain, 1)
                dve.wait_ge(chain, links[0])

            dve.wait_ge(rev_made, 1)
            link(nc.vector.tensor_copy(rev[:], rev_i[:]))
            revs = rev[:].unsqueeze(1).to_broadcast([P, T, E])
            link(nc.vector.reduce_max(peak[:], m.gates[:], AX.X))
            nc.vector.tensor_tensor(low[:], m.gates[:], wide(peak[:]), ALU.subtract).then_inc(low_ready, 1)
            link(nc.vector.tensor_tensor(one_hot[:], m.gates[:], wide(peak[:]), ALU.is_equal))
            link(nc.vector.tensor_tensor(one_hot[:], one_hot[:], revs, ALU.mult))
            link(nc.vector.reduce_max(code[:], one_hot[:], AX.X))
            nc.vector.tensor_tensor(one_hot[:], revs, wide(code[:]), ALU.is_equal).then_inc(hot_ready, 1)
            nc.vector.tensor_scalar(first[:], code[:], -float(C), float(E * C), ALU.mult, ALU.add)
            dve.wait_ge(exp_done, 1)
            link(nc.vector.reduce_sum(total[:], low[:], AX.X))
            link(nc.vector.reciprocal(m.prob[:], total[:]))
            dve.wait_ge(counted, 1)
            link(nc.vector.tensor_copy(flat(totals[:]), m.ps[:, 1, 0:T * E]))
            link(nc.vector.tensor_copy(sums[:, 0, :, :], totals[:]))
            now, step = 0, 1
            while step < T:
                nc.vector.tensor_copy(sums[:, 1 - now, 0:step, :], sums[:, now, 0:step, :])
                link(nc.vector.tensor_tensor(sums[:, 1 - now, step:T, :], sums[:, now, step:T, :],
                                             sums[:, now, 0:T - step, :], ALU.add))
                now, step = 1 - now, 2 * step
            link(nc.vector.tensor_tensor(totals[:], sums[:, now, :, :], totals[:], ALU.subtract))
            link(nc.vector.tensor_tensor(flat(totals[:]), flat(totals[:]), m.ps[:, 0, 0:T * E], ALU.add))
            link(nc.vector.tensor_tensor(totals[:], totals[:], one_hot[:], ALU.mult))
            link(nc.vector.reduce_sum(place[:], totals[:], AX.X))
            link(nc.vector.tensor_scalar(place[:], place[:], -1.0, None, ALU.add))
            link(nc.vector.tensor_scalar(kept_f[:], place[:], float(C), None, ALU.is_lt))
            link(nc.vector.tensor_tensor(first[:], first[:], place[:], ALU.add))
            link(nc.vector.tensor_scalar(place[:], kept_f[:], -4.0 * E * C, 4.0 * E * C, ALU.mult, ALU.add))
            nc.vector.tensor_tensor(to[:], first[:], place[:], ALU.add).then_inc(to_ready, 1)
            link(nc.vector.tensor_scalar(first[:], first[:], -float(E * C), None, ALU.add))
            link(nc.vector.tensor_tensor(first[:], first[:], kept_f[:], ALU.mult))
            link(nc.vector.tensor_scalar(back[:], first[:], float(E * C), None, ALU.add))
            nc.vector.tensor_copy(m.back[:], back[:])
            dve.wait_ge(to_masked, 1)
            nc.vector.tensor_copy(m.to[:], to[:])


def dispatch(nc, m, slots):
    R = TILE_RING
    with Stage(nc) as ctx:
        sem = lambda name: ctx.sem(f"disp_{name}")
        ring = ctx.enter_context(nc.sbuf_tensor("disp_ring", [P, R, D + 1], F32))
        index = ctx.enter_context(nc.sbuf_tensor("disp_index", [P, R], I32))
        rows_ready, index_ready, prob_ready = sem("rows"), sem("index"), sem("prob")
        landed = [sem(f"landed{j}") for j in range(R)]
        block = ctx.enter_context(nc.Block())

        @block.vector
        def _(dve):
            def rows(t, j, again, round_):
                if again:
                    dve.wait_ge(landed[j], round_ * 16)
                nc.vector.tensor_scalar(ring[:, j, 0:D], tile_of(m.x, t), m.mean[:, ds(t, 1)], m.scale[:, ds(t, 1)],
                                        ALU.subtract, ALU.mult).then_inc(rows_ready, 1)
            tile_loop(dve, m.tiles, [(0, rows)])

        @block.scalar
        def _(act):
            def fill(t, j, again, round_):
                if again:
                    act.wait_ge(landed[j], round_ * 16)
                nc.scalar.copy(ring[:, j, D:D + 1], m.prob[:, ds(t, 1)]).then_inc(prob_ready, 1)
                nc.scalar.copy(index[:, j:j + 1], m.to[:, ds(t, 1)]).then_inc(index_ready, 1)
            tile_loop(act, m.tiles, [(0, fill)])

        @block.gpsimd
        def _(pool):
            pool.wait_ge(m.slots_zeroed, 48)

            def scatter(t, j, again, round_):
                pool.wait_ge(rows_ready, t + 1)
                pool.wait_ge(prob_ready, t + 1)
                pool.wait_ge(index_ready, t + 1)
                nc.gpsimd.nop(nofuse=True)
                nc.gpsimd.indirect_dma_start(
                    out=slots[:, :], out_offset=bass.IndirectOffsetOnAxis(ap=index[:, j:j + 1], axis=0),
                    in_=ring[:, j, :], in_offset=None, bounds_check=m.experts * m.capacity - 1,
                    oob_is_err=False).then_inc(landed[j], 16)
            tile_loop(pool, m.tiles, [(0, scatter)])
            for j in range(R):
                pool.wait_ge(landed[j], m.tiles // R * 16)


def expert_slots(nc, m, a, slots, results):
    E, C = m.experts, m.capacity
    F = m.hidden1 // P
    TE = ceil_div(C, P)
    starts = [i * P for i in range(TE - 1)] + [C - P]
    fresh = [i * P for i in range(TE)]
    halves = [(0, 4 * P), (4 * P, C)]
    assert TE == 8 and C - 4 * P <= 512
    with Stage(nc) as ctx:
        sem = lambda name: ctx.sem(f"exp_{name}")
        buf = lambda name, shape, dt=F32: ctx.enter_context(nc.sbuf_tensor(f"exp_{name}", shape, dt))
        w1, w2 = buf("w1", [P, DK, F * P]), buf("w2", [P, F, D])
        b1, b2 = buf("b1", [P, 2, F]), buf("b2", [P, 2, D])
        rows = buf("rows", [P, TE, D + 1])
        prob = buf("prob", [P, 2, TE])
        cols = m.agg_flat[:, 0:DK * C].rearrange("p (k c) -> p k c", k=DK)
        hid = m.agg_flat[:, DK * C:DK * C + F * C].rearrange("p (f c) -> p f c", f=F)
        RY = 4
        y, mask, clamp = buf("y", [P, RY, D]), buf("mask", [P, RY, D], I32), buf("clamp", [P, RY, D])
        good, res, zero = buf("good", [P, RY, D], I32), buf("res", [P, RY, D]), buf("zero", [P, D])
        rows_landed, w1_landed, w2_landed = [sem(f"rows_landed{i}") for i in range(TE)], sem("w1_landed"), sem("w2_landed")
        turned, cols_kept, up_done, relu_done, down_done = (sem("turned"), sem("cols_kept"), sem("up"), sem("relu"),
                                                            sem("down"))
        prob_kept, biased, scaled, clamped, masked, merged, res_zeroed, res_done, freed = (
            sem("prob_kept"), sem("biased"), sem("scaled"), sem("clamped"), sem("masked"), sem("merged"),
            sem("res_zeroed"), sem("res_done"), sem("freed"))
        stored = [sem(f"stored{i}") for i in range(RY)]
        block = ctx.enter_context(nc.Block())

        def turned_ps(i):
            return m.ps[:, 4 + i % 2, 0:D].rearrange("p (k n) -> p k n", k=DK)

        def down_ps(i):
            return m.ps[:, 6 + i % 2, 0:D]

        @block.sync
        def _(sp):
            def load_rows(e, first):
                for i in range(TE):
                    if not first:
                        sp.wait_ge(turned, e * TE + (i + 1 - TE))
                        sp.wait_ge(prob_kept, e * TE + (i + 1 - TE))
                    sp.dma_start(rows[:, i, :], slots[ds(e * C + starts[i], P), :]).then_inc(rows_landed[i], 16)

            def load_w1(e, first):
                if not first:
                    sp.wait_ge(up_done, e * 2 * F)
                    sp.wait_ge(relu_done, e * 2 * F)
                sp.dma_start(w1[:], a["ffn1_w1"][ds(e, 1), :, :].rearrange("o (k p) f -> p (o k) f", p=P))\
                    .then_inc(w1_landed, 16)
                sp.dma_start(b1[:, 0, :], a["ffn1_b1"][ds(e, 1), :, :].rearrange("o p f -> p (o f)"))\
                    .then_inc(w1_landed, 16)

            def load_w2(e, first):
                if not first:
                    sp.wait_ge(down_done, e * TE)
                    sp.wait_ge(biased, e * TE)
                sp.dma_start(w2[:], a["ffn1_w2"][ds(e, 1), :, :].rearrange("o (k p) f -> p (o k) f", p=P))\
                    .then_inc(w2_landed, 16)
                sp.dma_start(b2[:, 0, :], a["ffn1_b2"][ds(e, 1), :].rearrange("o d -> (o d)").partition_broadcast(P))\
                    .then_inc(w2_landed, 16)

            load_rows(0, True)
            load_w1(0, True)
            load_w2(0, True)
            with sp.Fori(1, E) as e:
                load_rows(e, False)
                load_w1(e, False)
                load_w2(e, False)

        @block.tensor
        def _(pe):
            def turn(e, first):
                for i in range(TE):
                    pe.wait_ge(rows_landed[i], (e + 1) * 16)
                    if not first or i >= 2:
                        pe.wait_ge(cols_kept, e * TE + (i - 1))
                    for k in range(DK):
                        last = nc.tensor.transpose(turned_ps(i)[:, k, :], rows[:, i, k * P:(k + 1) * P], m.ident[:])
                    last.then_inc(turned, 1)

            def up(e, first):
                pe.wait_ge(w1_landed, (e + 1) * 32)
                pe.wait_ge(cols_kept, (e + 1) * TE)
                for h, (lo, hi) in enumerate(halves):
                    for f in range(F):
                        if not first or h or f >= 4:
                            pe.wait_ge(relu_done, e * 2 * F + (h * F + f - 3))
                        for k in range(DK):
                            last = nc.tensor.matmul(m.ps[:, f % 4, 0:hi - lo], w1[:, k, f * P:(f + 1) * P],
                                                    cols[:, k, lo:hi], start=(k == 0), stop=(k == DK - 1))
                        last.then_inc(up_done, 1)

            def down(e, first):
                pe.wait_ge(w2_landed, (e + 1) * 32)
                for i in range(TE):
                    if i == 0:
                        pe.wait_ge(relu_done, e * 2 * F + F)
                    if i == 4:
                        pe.wait_ge(relu_done, e * 2 * F + 2 * F)
                    if not first or i >= 2:
                        pe.wait_ge(biased, e * TE + (i - 1))
                    for f in range(F):
                        last = nc.tensor.matmul(down_ps(i), hid[:, f, starts[i]:starts[i] + P], w2[:, f, :],
                                                start=(f == 0), stop=(f == F - 1))
                    last.then_inc(down_done, 1)

            turn(0, True)
            up(0, True)
            turn(1, False)
            down(0, True)
            with pe.Fori(1, E - 1) as e:
                up(e, False)
                turn(e + 1, False)
                down(e, False)
            up(E - 1, False)
            down(E - 1, False)

        @block.scalar
        def _(act):
            def keep_cols(e, first):
                if not first:
                    act.wait_ge(up_done, e * 2 * F)
                for i in range(TE):
                    act.wait_ge(turned, e * TE + (i + 1))
                    skip = fresh[i] - starts[i]
                    nc.scalar.copy(cols[:, :, fresh[i]:starts[i] + P], turned_ps(i)[:, :, skip:P]).then_inc(cols_kept, 1)

            def relu(e, first):
                act.wait_ge(w1_landed, (e + 1) * 32)
                for h, (lo, hi) in enumerate(halves):
                    if not first:
                        act.wait_ge(down_done, e * TE + (4 * (h + 1) - TE))
                        if h:
                            act.wait_ge(down_done, e * TE)
                    for f in range(F):
                        act.wait_ge(up_done, e * 2 * F + (h * F + f + 1))
                        nc.scalar.activation(hid[:, f, lo:hi], m.ps[:, f % 4, 0:hi - lo], ACT.Relu,
                                             bias=b1[:, 0, f:f + 1]).then_inc(relu_done, 1)

            keep_cols(0, True)
            relu(0, True)
            with act.Fori(1, E) as e:
                keep_cols(e, False)
                relu(e, False)

        @block.vector
        def _(dve):
            nc.vector.memset(zero[:], 0.0).then_inc(freed, 1)

            def save_probs(e, parity):
                for i in range(TE):
                    dve.wait_ge(rows_landed[i], (e + 1) * 16)
                    nc.vector.tensor_copy(prob[:, parity, i:i + 1], rows[:, i, D:D + 1]).then_inc(prob_kept, 1)

            def finish(e, parity, first):
                dve.wait_ge(w2_landed, (e + 1) * 32)
                for i in range(TE):
                    s = i % RY
                    n = e * TE + i
                    again = not first or i >= RY
                    if again:
                        dve.wait_ge(stored[s], e * 16 * (TE // RY) + 16 * (i // RY))
                    dve.wait_ge(down_done, n + 1)
                    nc.vector.tensor_tensor(y[:, s, :], down_ps(i), b2[:, 0, :], ALU.add).then_inc(biased, 1)
                    nc.vector.memset(res[:, s, :], 0.0).then_inc(res_zeroed, 1)
                    dve.wait_ge(biased, n + 1)
                    dve.wait_ge(prob_kept, n + 1)
                    nc.vector.tensor_scalar(y[:, s, :], y[:, s, :], prob[:, parity, i:i + 1], None,
                                            ALU.mult).then_inc(scaled, 1)
                    dve.wait_ge(scaled, n + 1)
                    nc.vector.tensor_scalar(clamp[:, s, :], y[:, s, :], 1e4, -1e4, ALU.min, ALU.max).then_inc(clamped, 1)
                    nc.vector.tensor_scalar(mask[:, s, :], y[:, s, :], 0.0, 0.0, ALU.mult,
                                            ALU.is_equal).then_inc(masked, 1)
                    nc.vector.tensor_tensor(good[:, s, :], y[:, s, :], y[:, s, :], ALU.is_equal).then_inc(masked, 1)
                    dve.wait_ge(clamped, n + 1)
                    dve.wait_ge(masked, n * 2 + 2)
                    nc.vector.nop(nofuse=True)
                    nc.vector.copy_predicated(clamp[:, s, :], mask[:, s, :], y[:, s, :]).then_inc(merged, 1)
                    dve.wait_ge(merged, n + 1)
                    dve.wait_ge(res_zeroed, n + 1)
                    nc.vector.nop(nofuse=True)
                    nc.vector.copy_predicated(res[:, s, :], good[:, s, :], clamp[:, s, :]).then_inc(res_done, 1)

            save_probs(0, 0)
            save_probs(1, 1)
            finish(0, 0, True)
            with dve.Fori(1, E // 2) as g:
                save_probs(g * 2, 0)
                finish(g * 2 - 1, 1, False)
                save_probs(g * 2 + 1, 1)
                finish(g * 2, 0, False)
            finish(E - 1, 1, False)

        @block.gpsimd
        def _(pool):
            pool.wait_ge(freed, 1)
            pool.dma_start(results[E * C:E * C + 1, :], zero[0:1, :]).then_inc(m.zero_row, 16)

            def store(e):
                for i in range(TE):
                    s = i % RY
                    skip = fresh[i] - starts[i]
                    pool.wait_ge(res_done, e * TE + (i + 1))
                    nc.gpsimd.nop(nofuse=True)
                    pool.dma_start(results[ds(e * C + fresh[i], P - skip), :], res[skip:P, s, :])\
                        .then_inc(stored[s], 16)
            with pool.Fori(0, E) as e:
                store(e)
            pool.wait_ge(m.zero_row, 16)
            for s in range(RY):
                pool.wait_ge(stored[s], E * 16 * (TE // RY))


def collect(nc, m, results, out):
    R = TILE_RING
    with Stage(nc) as ctx:
        sem = lambda name: ctx.sem(f"coll_{name}")
        rows = ctx.enter_context(nc.sbuf_tensor("coll_rows", [P, R, D], F32))
        index = ctx.enter_context(nc.sbuf_tensor("coll_index", [P, R], I32))
        index_ready, added, stored = sem("index"), sem("added"), sem("stored")
        landed = [sem(f"landed{j}") for j in range(R)]
        block = ctx.enter_context(nc.Block())

        @block.scalar
        def _(act):
            def put_index(t, j, again, round_):
                if again:
                    act.wait_ge(landed[j], round_ * 16)
                nc.scalar.copy(index[:, j:j + 1], m.back[:, ds(t, 1)]).then_inc(index_ready, 1)
            tile_loop(act, m.tiles, [(0, put_index)])

        @block.gpsimd
        def _(pool):
            def gather(t, j, again, round_):
                pool.wait_ge(index_ready, t + 1)
                if again:
                    pool.wait_ge(added, t + (1 - R))
                nc.gpsimd.nop(nofuse=True)
                nc.gpsimd.indirect_dma_start(
                    out=rows[:, j, :], out_offset=None, in_=results[:, :],
                    in_offset=bass.IndirectOffsetOnAxis(ap=index[:, j:j + 1], axis=0)).then_inc(landed[j], 16)
            tile_loop(pool, m.tiles, [(0, gather)])

        @block.vector
        def _(dve):
            def add(t, j, again, round_):
                dve.wait_ge(landed[j], (round_ + 1) * 16)
                nc.vector.tensor_tensor(tile_of(m.x, t), tile_of(m.x, t), rows[:, j, :], ALU.add).then_inc(added, 1)
            tile_loop(dve, m.tiles, [(0, add)])

        @block.sync
        def _(sp):
            with sp.Fori(0, m.full_tiles // 4) as g:
                sp.wait_ge(added, g * 4 + 4)
                sp.dma_start(out[ds(g * 4 * P, 4 * P), :].rearrange("(t p) d -> p t d", p=P),
                             m.x[:, ds(g * 4, 4), :]).then_inc(stored, 16)
            sp.wait_ge(added, m.tiles)
            sp.dma_start(out[m.full_tiles * P:m.nodes, :], m.x[0:m.tail_nodes, m.full_tiles, :]).then_inc(stored, 16)
            sp.wait_ge(stored, 16 * (m.full_tiles // 4 + 1))


def graph_network(nc, a, out):
    nodes, width = a["x"].shape
    full_chunks, tail_edges = a["src_main"].shape[1], a["src_tail"].shape[0]
    m = Shared()
    m.nodes, m.tiles, m.full_tiles, m.tail_nodes = nodes, ceil_div(nodes, P), nodes // P, nodes % P
    m.full_chunks, m.tail_edges = full_chunks, tail_edges
    m.chunks = ceil_div(full_chunks + 1, 2 * CHUNK_RING) * 2 * CHUNK_RING
    m.experts = a["gate_w"].shape[1]
    m.capacity = ceil_div(nodes * 5, 4 * m.experts)
    m.hidden0, m.hidden1, m.heads = a["ffn0_w1"].shape[2], a["ffn1_w1"].shape[2], a["gat_l"].shape[0]
    table = [nc.dram_tensor(f"table{i}", [m.tiles * P, D], F32, kind="Internal").ap() for i in range(2)]
    heads_table = nc.dram_tensor("heads_table", [m.tiles * P, D + m.heads], F32, kind="Internal").ap()
    left_table = nc.dram_tensor("left_table", [m.tiles * P, m.heads], F32, kind="Internal").ap()
    slots = nc.dram_tensor("slots", [m.experts * m.capacity, D + 1], F32, kind="Internal").ap()
    results = nc.dram_tensor("results", [m.experts * m.capacity + 1, D], F32, kind="Internal").ap()
    with ExitStack() as ctx:
        def sb(name, shape, dt=F32):
            return ctx.enter_context(nc.sbuf_tensor(name, shape, dt))
        m.x = sb("x", [P, m.tiles, D])
        m.agg_flat = sb("agg", [P, DK * (m.tiles * P + P)])
        m.agg = m.agg_flat[:].rearrange("p (k n) -> p k n", k=DK)
        m.mean_row = sb("mean_row", [1, D])
        m.slots_zeroed = ctx.enter_context(nc.semaphore("slots_zeroed"))
        m.x_landed, m.w_landed = (ctx.enter_context(nc.semaphore(name)) for name in ("x_landed", "w_landed"))
        m.zero_made = ctx.enter_context(nc.semaphore("zero_made"))
        m.zero = sb("zero", [P, D + 1])
        m.zero_row = ctx.enter_context(nc.semaphore("zero_row"))
        m.ones = sb("ones", [P, P])
        m.iota_i = sb("iota_i", [P, P], I32)
        m.part_i = sb("part_i", [P, 1], I32)
        m.iota, m.iota_b, m.part = sb("iota", [P, P]), sb("iota_b", [P, P], BF16), sb("part", [P, 1])
        m.stats, m.mean, m.scale = sb("stats", [P, m.tiles, 6]), sb("mean", [P, m.tiles]), sb("scale", [P, m.tiles])
        m.ident, m.first_row = sb("ident", [P, P]), sb("first_row", [P, P])
        m.src, m.dst = sb("src", [P, m.chunks], I32), sb("dst", [P, m.chunks], I32)
        m.ps = ctx.enter_context(nc.psum_tensor("ps", [P, 8, 512], F32))
        with ExitStack() as gcn:
            def gb(name, shape, dt=F32):
                return gcn.enter_context(nc.sbuf_tensor(name, shape, dt))
            m.dloc = gb("dloc", [P, m.chunks])
            m.dinv = gb("dinv", [P, m.tiles])
            m.dst_f = gb("dst_f", [P, m.chunks])
            m.astray = gb("astray_flag", [1, 1], I32)
            m.w1, m.w2, m.w3, m.wp = gb("w1", [P, DK, D]), gb("w2", [P, DK, D]), gb("w3", [P, DK, P]), gb("wp", [P, D])
            m.b1, m.b2, m.b3, m.bp = gb("b1", [P, D]), gb("b2", [P, D]), gb("b3", [P, P]), gb("bp", [P, D])
            load_inputs(nc, m, a, slots)
            degrees(nc, m)
            row_stats(nc, m)
            normalize(nc, m, "norm0", table=table[0])
            sum_edges(nc, m, "e1", table[0])
            update_nodes(nc, m, "n1", m.w1, m.b1, table[1])
            sum_edges(nc, m, "e2", table[1])
            update_nodes(nc, m, "n2", m.w2, m.b2, table[0])
            sum_edges(nc, m, "e3", table[0])
            finish_gcn(nc, m, "n3")
        normalize(nc, m, "norm1", column_sums=True)
        with ExitStack() as ffn:
            def fb(name, shape, dt=F32):
                return ffn.enter_context(nc.sbuf_tensor(name, shape, dt))
            w1_shape, w2_shape = [P, 2, DK, m.hidden0], [P, 2, m.hidden0 // P, D]
            m.f0_w1_hi, m.f0_w1_lo = fb("f0_w1_hi", w1_shape, F32R), fb("f0_w1_lo", w1_shape, F32R)
            m.f0_w2_hi, m.f0_w2_lo = fb("f0_w2_hi", w2_shape, F32R), fb("f0_w2_lo", w2_shape, F32R)
            m.f0_b1, m.f0_b2 = fb("f0_b1", [P, 2, m.hidden0 // P]), fb("f0_b2", [P, D])
            m.gamma, m.beta = fb("gamma", [P, D]), fb("beta", [P, D])
            route_all(nc, m, a)
            two_experts(nc, m)
            add_normalized(nc, m)
        project_heads(nc, m, a, heads_table, left_table)
        attend(nc, m, heads_table, left_table)
        m.gates, m.prob = sb("gates", [P, m.tiles, m.experts]), sb("prob", [P, m.tiles])
        m.to, m.back = sb("to", [P, m.tiles], I32), sb("back", [P, m.tiles], I32)
        score_experts(nc, m, a)
        assign_slots(nc, m)
        dispatch(nc, m, slots)
        expert_slots(nc, m, a, slots, results)
        collect(nc, m, results, out)


def kernel(**inputs):
    import numpy as np
    import concourse.bacc as bacc
    from concourse.bass_utils import run_bass_kernel_spmd

    nc = bacc.Bacc("TRN2", target_bir_lowering=False, num_devices=1)
    src, dst = np.asarray(inputs["src"]), np.asarray(inputs["dst"])
    main = src.shape[0] // P * P

    def by_partition(b):
        b = np.asarray(b)
        return b.reshape(b.shape[0], -1, P).transpose(0, 2, 1)

    data = {
        "x": inputs["x"],
        "src_main": src[:main].reshape(-1, P).T, "src_tail": src[main:].reshape(-1, 1),
        "dst_main": dst[:main].reshape(-1, P).T, "dst_tail": dst[main:].reshape(-1, 1),
        "gnn_w1": inputs["L0_gnn_W1"], "gnn_b1": inputs["L0_gnn_b1"],
        "gnn_w2": inputs["L0_gnn_W2"], "gnn_b2": inputs["L0_gnn_b2"],
        "gnn_w3": inputs["L0_gnn_W3"], "gnn_b3": inputs["L0_gnn_b3"],
        "gnn_wp": inputs["L0_gnn_Wp"], "gnn_bp": inputs["L0_gnn_bp"],
        "ffn0_wr": inputs["L0_ffn_Wr"], "ffn0_br": inputs["L0_ffn_br"],
        "ffn0_w1": inputs["L0_ffn_W1"], "ffn0_b1": by_partition(inputs["L0_ffn_b1"]),
        "ffn0_w2": inputs["L0_ffn_W2"], "ffn0_b2": inputs["L0_ffn_b2"],
        "ffn0_gamma": inputs["L0_ffn_gamma"], "ffn0_beta": inputs["L0_ffn_beta"],
        "gat_w": inputs["L1_gnn_weight"], "gat_l": inputs["L1_gnn_attn_l"], "gat_r": inputs["L1_gnn_attn_r"],
        "gate_w": inputs["L1_ffn_gate_w"], "gate_b": inputs["L1_ffn_gate_b"],
        "ffn1_w1": inputs["L1_ffn_w1"], "ffn1_b1": by_partition(inputs["L1_ffn_b1"]),
        "ffn1_w2": inputs["L1_ffn_w2"], "ffn1_b2": inputs["L1_ffn_b2"],
    }
    arrays, a = {}, {}
    for name, value in data.items():
        value = np.ascontiguousarray(value)
        arrays[f"in_{name}"] = value
        a[name] = nc.dram_tensor(f"in_{name}", value.shape, mybir.dt.from_np(value.dtype),
                                 kind="ExternalInput").ap()
    out = nc.dram_tensor("out", inputs["x"].shape, F32, kind="ExternalOutput").ap()
    graph_network(nc, a, out)
    return run_bass_kernel_spmd(nc, [arrays], core_ids=[0]).results[0]["out"]
```

```python
from contextlib import ExitStack

import concourse.bass as bass
from concourse import mybir

ALU = mybir.AluOpType
ACT = mybir.ActivationFunctionType
AX = mybir.AxisListType
F32 = mybir.dt.float32
BF16 = mybir.dt.bfloat16
F32R = mybir.dt.float32r
I32 = mybir.dt.int32
U32 = mybir.dt.uint32
ds = bass.ds

P = 128
D = 256
DK = D // P
EPS = 1e-5
TILE_RING = 7
CHUNK_RING = 8
HOT_RING = 4
WINDOW = P


def ceil_div(a, b):
    return (a + b - 1) // b


class Shared:
    pass


class Stage(ExitStack):

    def __init__(self, nc):
        super().__init__()
        self.nc, self.sems = nc, []

    def sem(self, name):
        self.sems.append(self.nc.alloc_semaphore(name))
        return self.sems[-1]

    def __exit__(self, *error):
        super().__exit__(*error)
        if self.sems and error[0] is None:
            self.nc.clear_and_free_semaphores(self.sems)
            self.nc.all_engine_barrier(sem_only=True)


def load_inputs(nc, m, a, slots):
    n_main = m.full_tiles * P
    with Stage(nc) as ctx:
        pads_zero = ctx.sem("pads_zero")
        edges_landed = ctx.sem("edges_landed")
        iota_made = ctx.sem("iota_made")
        zeroed = ctx.sem("zeroed")
        block = ctx.enter_context(nc.Block())

        @block.sync
        def _(sp):
            sp.wait_ge(pads_zero, 3)
            sp.dma_start(m.src[:, 0:m.full_chunks], a["src_main"]).then_inc(edges_landed, 16)
            sp.dma_start(m.dst[:, 0:m.full_chunks], a["dst_main"]).then_inc(edges_landed, 16)
            sp.dma_start(m.src[0:m.tail_edges, m.full_chunks:m.full_chunks + 1], a["src_tail"]).then_inc(edges_landed, 16)
            sp.dma_start(m.dst[0:m.tail_edges, m.full_chunks:m.full_chunks + 1], a["dst_tail"]).then_inc(edges_landed, 16)
            sp.dma_start(m.x[:, 0:m.full_tiles, :],
                         a["x"][0:n_main, :].rearrange("(t p) d -> p t d", p=P)).then_inc(m.x_landed, 16)
            sp.dma_start(m.x[0:m.tail_nodes, m.full_tiles, :], a["x"][n_main:m.nodes, :]).then_inc(m.x_landed, 16)
            sp.wait_ge(edges_landed, 64)

        @block.scalar
        def _(act):
            act.dma_start(m.w1[:], a["gnn_w1"].rearrange("(k p) n -> p k n", p=P)).then_inc(m.w_landed, 16)
            act.dma_start(m.w2[:], a["gnn_w2"].rearrange("(k p) n -> p k n", p=P)).then_inc(m.w_landed, 16)
            act.dma_start(m.w3[:], a["gnn_w3"].rearrange("(k p) n -> p k n", p=P)).then_inc(m.w_landed, 16)
            act.dma_start(m.wp[:], a["gnn_wp"]).then_inc(m.w_landed, 16)
            act.dma_start(m.b1[:], a["gnn_b1"].partition_broadcast(P)).then_inc(m.w_landed, 16)
            act.dma_start(m.b2[:], a["gnn_b2"].partition_broadcast(P)).then_inc(m.w_landed, 16)
            act.dma_start(m.b3[:], a["gnn_b3"].partition_broadcast(P)).then_inc(m.w_landed, 16)
            act.dma_start(m.bp[:], a["gnn_bp"].partition_broadcast(P)).then_inc(m.w_landed, 16)
            act.wait_ge(m.zero_made, 1)
            full = slots.shape[0] // P
            half = full // 2
            for lo, hi in ((0, half), (half, full)):
                act.dma_start(slots[lo * P:hi * P, :].rearrange("(t p) w -> p t w", p=P),
                              m.zero[:].unsqueeze(1).to_broadcast([P, hi - lo, D + 1])).then_inc(m.slots_zeroed, 16)
            act.dma_start(slots[full * P:, :], m.zero[0:slots.shape[0] - full * P, :]).then_inc(m.slots_zeroed, 16)

        @block.vector
        def _(dve):
            nc.vector.memset(m.x[:, m.full_tiles, :], 0.0).then_inc(pads_zero, 1)
            nc.vector.memset(m.src[:, m.full_chunks:m.chunks], 0).then_inc(pads_zero, 1)
            nc.vector.memset(m.dst[:, m.full_chunks:m.chunks], 0).then_inc(pads_zero, 1)
            nc.vector.memset(m.agg[:, :, m.tiles * P:], 0.0)
            nc.vector.memset(m.ones[:], 1.0)
            nc.vector.memset(m.zero[:], 0.0).then_inc(m.zero_made, 1)

        @block.gpsimd
        def _(pool):
            nc.gpsimd.iota(m.iota_i[:], pattern=[[1, P]], base=0, channel_multiplier=0).then_inc(iota_made, 1)
            nc.gpsimd.iota(m.part_i[:], pattern=[[1, 1]], base=0, channel_multiplier=1).then_inc(iota_made, 1)
            nc.gpsimd.memset(m.ident[:], 0.0).then_inc(zeroed, 1)
            nc.gpsimd.memset(m.first_row[:], 1.0).then_inc(zeroed, 1)
            pool.wait_ge(iota_made, 2)
            nc.gpsimd.tensor_copy(m.iota[:], m.iota_i[:])
            nc.gpsimd.tensor_copy(m.iota_b[:], m.iota_i[:])
            nc.gpsimd.tensor_copy(m.part[:], m.part_i[:])
            pool.wait_ge(zeroed, 2)
            nc.gpsimd.affine_select(out=m.ident[:], in_=m.ident[:], compare_op=ALU.not_equal, fill=1.0, base=0,
                                    pattern=[[-1, P]], channel_multiplier=1)
            nc.gpsimd.affine_select(out=m.first_row[:], in_=m.first_row[:], compare_op=ALU.is_ge, fill=0.0, base=0,
                                    pattern=[[0, P]], channel_multiplier=-1)


def degrees(nc, m):
    GROUP = 2 * CHUNK_RING
    half = m.chunks // 2
    groups = m.chunks // GROUP
    with Stage(nc) as ctx:
        dst_f = m.dst_f
        ends = ctx.enter_context(nc.sbuf_tensor("ends", [P, 2], F32))
        astray = ctx.enter_context(nc.sbuf_tensor("astray", [P, 4], F32))
        ends_done, astray_done, counted = ctx.sem("ends_done"), ctx.sem("astray_done"), ctx.sem("counted")
        hi_i = ctx.enter_context(nc.sbuf_tensor("hi_i", [P, m.chunks], I32))
        lo_i = ctx.enter_context(nc.sbuf_tensor("lo_i", [P, m.chunks], I32))
        hi = ctx.enter_context(nc.sbuf_tensor("hi", [P, m.chunks], BF16))
        lo = ctx.enter_context(nc.sbuf_tensor("lo", [P, m.chunks], BF16))
        hot_lo = ctx.enter_context(nc.sbuf_tensor("hot_lo", [P, 2, P, GROUP], BF16))
        hot_hi = ctx.enter_context(nc.sbuf_tensor("hot_hi", [P, 2, m.tiles, GROUP], BF16))
        number = ctx.enter_context(nc.sbuf_tensor("number", [P, P, GROUP], BF16))
        deg = ctx.enter_context(nc.sbuf_tensor("deg", [P, m.tiles], F32))
        root = ctx.enter_context(nc.sbuf_tensor("root", [P, m.tiles], F32))
        ints_done = ctx.sem("ints_done")
        floats_done = ctx.sem("floats_done")
        base_spread = ctx.sem("base_spread")
        dloc_made = ctx.sem("dloc_made")
        pads_marked = ctx.sem("pads_marked")
        hot_ready = ctx.sem("hot_ready")
        group_used = ctx.sem("group_used")
        deg_done = ctx.sem("deg_done")
        root_done = ctx.sem("root_done")
        numbers_made = ctx.sem("numbers_made")
        sums, squares, veps, std = (ctx.enter_context(nc.sbuf_tensor(f"row_{name}", [P, m.tiles], F32))
                                    for name in ("sums", "squares", "veps", "std"))
        scrap = ctx.enter_context(nc.sbuf_tensor("scrap", [P, TILE_RING, D], F32))
        minus_mean = ctx.enter_context(nc.sbuf_tensor("minus_mean", [P, TILE_RING], F32))
        summed, centred, squared = ctx.sem("summed"), ctx.sem("centred"), ctx.sem("squared")
        dinv_done, veps_done, std_done, std_inverted = (ctx.sem("dinv_done"), ctx.sem("veps_done"), ctx.sem("std_done"),
                                                        ctx.sem("std_inverted"))
        block = ctx.enter_context(nc.Block())
        base_ps = m.ps[:, 0:2, 0:half]
        deg_ps = m.ps[:, 2, 0:m.tiles]

        @block.vector
        def _(dve):
            nc.vector.tensor_copy(dst_f[:], m.dst[:]).then_inc(floats_done, 1)
            nc.vector.tensor_scalar(hi_i[:], m.dst[:], 7, None, ALU.logical_shift_right).then_inc(ints_done, 1)
            nc.vector.tensor_scalar(lo_i[:], m.dst[:], P - 1, None, ALU.bitwise_and).then_inc(ints_done, 1)
            dve.wait_ge(ints_done, 2)
            nc.vector.tensor_copy(hi[:], hi_i[:]).then_inc(floats_done, 1)
            nc.vector.tensor_copy(lo[:], lo_i[:])
            nc.vector.tensor_copy(number[:], m.iota_b[:].unsqueeze(2).to_broadcast([P, P, GROUP]))\
                .then_inc(numbers_made, 1)
            dve.wait_ge(base_spread, 1)
            dve.wait_ge(floats_done, 2)
            nc.vector.tensor_tensor(m.dloc[:].rearrange("p (h c) -> p h c", h=2),
                                    dst_f[:].rearrange("p (h c) -> p h c", h=2), base_ps,
                                    ALU.subtract).then_inc(dloc_made, 1)
            dve.wait_ge(pads_marked, 5)
            nc.vector.reduce_max(ends[:, 0:1], m.dloc[:], AX.X).then_inc(ends_done, 1)
            nc.vector.tensor_reduce(ends[:, 1:2], m.dloc[:], AX.X, ALU.min).then_inc(ends_done, 1)
            dve.wait_ge(ends_done, 2)
            nc.vector.tensor_scalar(astray[:, 0:1], ends[:, 0:1], float(WINDOW - 1), None, ALU.is_gt).then_inc(astray_done, 1)
            nc.vector.tensor_scalar(astray[:, 1:2], ends[:, 1:2], 0.0, None, ALU.is_lt).then_inc(astray_done, 1)

            def put(g, h):
                for hot, digit, width in ((hot_lo, lo, P), (hot_hi, hi, m.tiles)):
                    last = nc.vector.tensor_tensor(hot[:, h, :, :],
                                                   digit[:, ds(g * GROUP, GROUP)].unsqueeze(1)
                                                   .to_broadcast([P, width, GROUP]),
                                                   number[:, 0:width, :], ALU.is_equal)
                last.then_inc(hot_ready, 1)

            dve.wait_ge(numbers_made, 1)
            put(0, 0)
            put(1, 1)
            with dve.Fori(0, (groups - 2) // 2) as g:
                for h in range(2):
                    dve.wait_ge(group_used, g * 2 + (1 + h))
                    put(g * 2 + (2 + h), h)
            dve.wait_ge(counted, 1)
            nc.vector.reduce_max(astray[0:1, 2:3], m.ps[0:1, 3, 0:2], AX.X).then_inc(astray_done, 1)
            dve.wait_ge(astray_done, 3)
            nc.vector.tensor_scalar(m.astray[0:1, :], astray[0:1, 2:3], 0.0, None, ALU.is_gt)
            dve.wait_ge(group_used, groups)
            nc.vector.tensor_scalar(deg[:], deg_ps, 1.0, None, ALU.add).then_inc(deg_done, 1)
            dve.wait_ge(squared, m.tiles)
            nc.vector.tensor_scalar(m.mean[:], sums[:], 1.0 / D, None, ALU.mult)
            nc.vector.tensor_scalar(veps[:], squares[:], 1.0 / D, EPS, ALU.mult, ALU.add).then_inc(veps_done, 1)
            dve.wait_ge(root_done, 1)
            nc.vector.reciprocal(m.dinv[:], root[:]).then_inc(dinv_done, 1)
            dve.wait_ge(std_done, 1)
            nc.vector.reciprocal(veps[:], std[:]).then_inc(std_inverted, 1)
            dve.wait_ge(std_inverted, 1)
            dve.wait_ge(dinv_done, 1)
            nc.vector.tensor_tensor(m.scale[:], veps[:], m.dinv[:], ALU.mult)

        @block.gpsimd
        def _(pool):
            c = m.full_chunks
            pool.wait_ge(dloc_made, 1)
            for targets in (m.dloc, dst_f):
                nc.gpsimd.affine_select(out=targets[:, c:c + 1], in_=targets[:, c:c + 1], compare_op=ALU.is_ge,
                                        fill=0.5, base=m.tail_edges - 1, pattern=[[0, 1]],
                                        channel_multiplier=-1).then_inc(pads_marked, 1)
            nc.gpsimd.memset(m.dloc[:, c + 1:m.chunks], 0.5)
            nc.gpsimd.memset(dst_f[:, c + 1:m.chunks], 0.5).then_inc(pads_marked, 1)
            nc.gpsimd.affine_select(out=hi[:, c:c + 1], in_=hi[:, c:c + 1], compare_op=ALU.is_ge, fill=-1.0,
                                    base=m.tail_edges - 1, pattern=[[0, 1]],
                                    channel_multiplier=-1).then_inc(pads_marked, 1)
            nc.gpsimd.memset(hi[:, c + 1:m.chunks], -1.0).then_inc(pads_marked, 1)

        @block.tensor
        def _(pe):
            pe.wait_ge(floats_done, 1)
            for h in range(2):
                last = nc.tensor.matmul(base_ps[:, h, :], m.first_row[:], dst_f[:, h * half:(h + 1) * half],
                                        start=True, stop=True)
            last.then_inc(base_spread, 1)
            pe.wait_ge(astray_done, 2)
            nc.tensor.matmul(m.ps[0:1, 3, 0:2], m.ones[:, 0:1], astray[:, 0:2], start=True, stop=True).then_inc(counted, 1)
            pe.wait_ge(hot_ready, 1)
            for j in range(GROUP):
                mm = nc.tensor.matmul(deg_ps, hot_lo[:, 0, :, j], hot_hi[:, 0, :, j], start=(j == 0), stop=False,
                                      skip_group_check=True)
            mm.then_inc(group_used, 1)
            with pe.Fori(0, (groups - 2) // 2) as g:
                for h in range(2):
                    pe.wait_ge(hot_ready, g * 2 + (2 + h))
                    for j in range(GROUP):
                        mm = nc.tensor.matmul(deg_ps, hot_lo[:, 1 - h, :, j], hot_hi[:, 1 - h, :, j], start=False,
                                              stop=False, skip_group_check=True)
                    mm.then_inc(group_used, 1)
            pe.wait_ge(hot_ready, groups)
            for j in range(GROUP):
                mm = nc.tensor.matmul(deg_ps, hot_lo[:, 1, :, j], hot_hi[:, 1, :, j], start=False,
                                      stop=(j == GROUP - 1), skip_group_check=True)
            mm.then_inc(group_used, 1)

        @block.scalar
        def _(act):
            def sum_rows(t, j, again, round_):
                if again:
                    act.wait_ge(squared, t + (1 - TILE_RING))
                    nc.scalar.nop(nofuse=True)
                nc.scalar.activation(scrap[:, j, :], tile_of(m.x, t), ACT.Identity,
                                     accum_out=sums[:, ds(t, 1)]).then_inc(summed, 1)

            def centre(t, j, again, round_):
                act.wait_ge(summed, t + 1)
                nc.scalar.nop(nofuse=True)
                nc.scalar.mul(minus_mean[:, j:j + 1], sums[:, ds(t, 1)], -1.0 / D).then_inc(centred, 1)

            def square_rows(t, j, again, round_):
                act.wait_ge(centred, t + 1)
                nc.scalar.nop(nofuse=True)
                nc.scalar.activation(scrap[:, j, :], tile_of(m.x, t), ACT.Square, bias=minus_mean[:, j:j + 1],
                                     accum_out=squares[:, ds(t, 1)]).then_inc(squared, 1)

            act.wait_ge(m.x_landed, 32)
            act.wait_ge(m.w_landed, 16 * 8)
            tile_loop(act, m.tiles, [(0, sum_rows), (1, centre), (2, square_rows)])
            act.wait_ge(deg_done, 1)
            nc.scalar.activation(root[:], deg[:], ACT.Sqrt).then_inc(root_done, 1)
            act.wait_ge(veps_done, 1)
            nc.scalar.activation(std[:], veps[:], ACT.Sqrt).then_inc(std_done, 1)


def tile_loop(eng, tiles, steps):
    R = TILE_RING
    lags = max(lag for lag, _ in steps)
    peeled = 1 + max(1, ceil_div(lags, R))
    assert tiles % R == 0 and peeled < tiles // R
    for s in range(peeled * R):
        for lag, body in steps:
            if s >= lag:
                body(s - lag, (s - lag) % R, s - lag >= R, (s - lag) // R)
    with eng.Fori(peeled, tiles // R) as g:
        for j in range(R):
            for lag, body in steps:
                body(g * R + (j - lag), (j - lag) % R, True, g + (j - lag) // R)
    for s in range(tiles, tiles + lags):
        for lag, body in steps:
            if s - lag < tiles:
                body(s - lag, (s - lag) % R, True, (s - lag) // R)


def tile_of(buf, t):
    return buf[:, ds(t, 1), :].rearrange("p t d -> p (t d)")


class RowStats:

    def __init__(self, nc, m, ctx, tag):
        sem = lambda name: ctx.sem(f"{tag}_{name}")
        buf = lambda name: ctx.enter_context(nc.sbuf_tensor(f"{tag}_{name}", [P, m.tiles], F32))
        self.nc, self.m = nc, m
        self.done, self.chain, self.veps_done, self.std_done = sem("tile_stats"), sem("chain"), sem("veps"), sem("std")
        self.spread, self.veps, self.std = buf("spread"), buf("veps"), buf("std")

    def of_tile(self, t, rows):
        self.nc.vector.nop(nofuse=True)
        self.nc.vector.bn_stats(tile_of(self.m.stats, t), rows).then_inc(self.done, 1)

    def on_vector(self, dve, tiles):
        nc, m = self.nc, self.m
        links = [0]

        def link(ins):
            links[0] += 1
            ins.then_inc(self.chain, 1)
            dve.wait_ge(self.chain, links[0])

        dve.wait_ge(self.done, tiles)
        mean, var = (m.stats[:, :, 1], m.stats[:, :, 4]), (m.stats[:, :, 2], m.stats[:, :, 5])
        nc.vector.tensor_tensor(m.mean[:], mean[0], mean[1], ALU.add)
        link(nc.vector.tensor_tensor(self.spread[:], mean[0], mean[1], ALU.subtract))
        link(nc.vector.tensor_tensor(self.spread[:], self.spread[:], self.spread[:], ALU.mult))
        link(nc.vector.tensor_scalar(self.spread[:], self.spread[:], 0.25, EPS, ALU.mult, ALU.add))
        nc.vector.tensor_scalar(m.mean[:], m.mean[:], 0.5, None, ALU.mult)
        link(nc.vector.tensor_tensor(self.veps[:], var[0], var[1], ALU.add))
        nc.vector.scalar_tensor_tensor(self.veps[:], self.veps[:], 1.0 / D, self.spread[:], ALU.mult,
                                       ALU.add).then_inc(self.veps_done, 1)
        dve.wait_ge(self.std_done, 1)
        nc.vector.reciprocal(m.scale[:], self.std[:])

    def on_scalar(self, act):
        act.wait_ge(self.veps_done, 1)
        self.nc.scalar.activation(self.std[:], self.veps[:], ACT.Sqrt).then_inc(self.std_done, 1)


def normalize(nc, m, tag, table=None, column_sums=False):
    R = TILE_RING
    with Stage(nc) as ctx:
        sem = lambda name: ctx.sem(f"{tag}_{name}")
        ring = ctx.enter_context(nc.sbuf_tensor(f"{tag}_ring", [P, R, D], F32))
        rows_ready, turned, turned_kept, sums_done = sem("rows"), sem("turned"), sem("turned_kept"), sem("sums")
        stored = [sem(f"stored{j}") for j in range(R)]
        block = ctx.enter_context(nc.Block())

        def turned_ps(j):
            return m.ps[:, j, 0:D].rearrange("p (k n) -> p k n", k=DK)

        @block.vector
        def _(dve):
            def rows(t, j, again, round_):
                if again:
                    dve.wait_ge(turned, t + (1 - R))
                    if table is not None:
                        dve.wait_ge(stored[j], round_ * 16)
                nc.vector.tensor_scalar(ring[:, j, :], tile_of(m.x, t), m.mean[:, ds(t, 1)], m.scale[:, ds(t, 1)],
                                        ALU.subtract, ALU.mult).then_inc(rows_ready, 1)
            tile_loop(dve, m.tiles, [(0, rows)])
            if column_sums:
                dve.wait_ge(turned, m.tiles)
                nc.vector.tensor_scalar(m.mean_row[0:1, :], m.ps[0:1, R, 0:D], 1.0 / m.nodes, None, ALU.mult)

        @block.scalar
        def _(act):
            def keep(t, j, again, round_):
                act.wait_ge(turned, t + 1)
                nc.scalar.copy(m.agg[:, :, ds(t * P, P)], turned_ps(j)).then_inc(turned_kept, 1)
            tile_loop(act, m.tiles, [(0, keep)])

        @block.tensor
        def _(pe):
            def turn(t, j, again, round_):
                pe.wait_ge(rows_ready, t + 1)
                if again:
                    pe.wait_ge(turned_kept, t + (1 - R))
                if column_sums:
                    nc.tensor.matmul(m.ps[0:1, R, 0:D], m.ones[:, 0:1], ring[:, j, :], start=not again and j == 0,
                                     stop=False, skip_group_check=True)
                for k in range(DK):
                    last = nc.tensor.transpose(turned_ps(j)[:, k, :], ring[:, j, k * P:(k + 1) * P], m.ident[:])
                last.then_inc(turned, 1)
            tile_loop(pe, m.tiles, [(0, turn)])

        if table is not None:
            @block.sync
            def _(sp):
                def store(t, j, again, round_):
                    sp.wait_ge(rows_ready, t + 1)
                    sp.dma_start(table[ds(t * P, P), :], ring[:, j, :]).then_inc(stored[j], 16)
                tile_loop(sp, m.tiles, [(0, store)])
                for j in range(R):
                    sp.wait_ge(stored[j], m.tiles // R * 16)


def sum_edges(nc, m, tag, table):
    R = 2 * CHUNK_RING
    B = 8
    H = CHUNK_RING
    loops = m.chunks // R
    with Stage(nc) as ctx:
        sem = lambda name: ctx.sem(f"{tag}_{name}")
        rows = ctx.enter_context(nc.sbuf_tensor(f"{tag}_rows", [P, R, D], F32))
        hot = ctx.enter_context(nc.sbuf_tensor(f"{tag}_hot", [P, R, P], F32))
        index = ctx.enter_context(nc.sbuf_tensor(f"{tag}_index", [P, R], I32))
        landed = [sem(f"landed{j}") for j in range(R)]
        group_free, tile_free, moved = sem("group_free"), sem("tile_free"), sem("moved")
        index_ready, hot_ready, summed, added = sem("index_ready"), sem("hot_ready"), sem("summed"), sem("added")
        places = ctx.enter_context(nc.sbuf_tensor(f"{tag}_places", [P, P], F32))
        block = ctx.enter_context(nc.Block())

        def branch(eng, in_windows, anywhere):
            astray = eng.value_load(m.astray[0:1, 0:1], min_val=0, max_val=1)
            with eng.If(astray == 0):
                in_windows()
            with eng.Else():
                anywhere()

        def part_ps(j):
            return m.ps[:, j % B, 0:DK * P].rearrange("p (k n) -> p k n", k=DK)

        @block.scalar
        def _(act):
            def in_windows():
                def put(g, h):
                    nc.scalar.copy(index[:, h * H:(h + 1) * H], m.src[:, ds(g * R + h * H, H)]).then_inc(index_ready, 1)
                for h in range(2):
                    put(0, h)
                with act.Fori(1, loops) as g:
                    for h in range(2):
                        for j in range(h * H, (h + 1) * H):
                            act.wait_ge(landed[j], g * 16)
                        put(g, h)

            def anywhere():
                with act.Fori(0, m.tiles) as w:
                    with act.Fori(0, loops) as g:
                        act.wait_ge(group_free, w * loops + (g + 1))
                        nc.scalar.copy(index[:], m.src[:, ds(g * R, R)]).then_inc(index_ready, 1)

            branch(act, in_windows, anywhere)

        @block.gpsimd
        def _(pool):
            def in_windows():
                def gather_half(g, h):
                    pool.wait_ge(index_ready, g * 2 + (1 + h))
                    nc.gpsimd.nop(nofuse=True)
                    for j in range(h * H, (h + 1) * H):
                        nc.gpsimd.indirect_dma_start(
                            out=rows[:, j, :], out_offset=None, in_=table[:, :],
                            in_offset=bass.IndirectOffsetOnAxis(ap=index[:, j:j + 1], axis=0)).then_inc(landed[j], 16)

                for h in range(2):
                    gather_half(0, h)
                with pool.Fori(1, loops) as g:
                    for h in range(2):
                        pool.wait_ge(summed, g * R + ((h + 1) * H - R))
                        gather_half(g, h)

            def anywhere():
                with pool.Fori(0, m.tiles) as w:
                    with pool.Fori(0, loops) as g:
                        pool.wait_ge(index_ready, w * loops + (g + 1))
                        nc.gpsimd.nop(nofuse=True)
                        for j in range(R):
                            nc.gpsimd.indirect_dma_start(
                                out=rows[:, j, :], out_offset=None, in_=table[:, :],
                                in_offset=bass.IndirectOffsetOnAxis(ap=index[:, j:j + 1], axis=0)).then_inc(landed[j], 16)

            branch(pool, in_windows, anywhere)

        @block.vector
        def _(dve):
            def in_windows():
                def make_hot(c, j):
                    nc.vector.tensor_scalar(hot[:, j, :], m.iota[:], m.dloc[:, ds(c, 1)], None,
                                            ALU.is_equal).then_inc(hot_ready, 1)

                for j in range(R):
                    make_hot(j, j)

                def add(c, j, base, first=False):
                    dve.wait_ge(summed, c + 1)
                    if not first:
                        dve.wait_ge(added, c)
                    window = m.agg[:, :, ds(base, WINDOW)]
                    nc.vector.tensor_tensor(window, window, part_ps(j), ALU.add).then_inc(added, 1)

                def bases(c):
                    _, values = nc.values_load_multi_w_load_instructions(
                        m.dst[0:1, ds(c, H)], engines=(dve.engine,), min_val=0, max_val=m.nodes - 1,
                        skip_runtime_bounds_check_because="targets are node numbers")
                    return values

                for h in range(2):
                    for j, base in enumerate(bases(h * H), h * H):
                        add(j, j, base, first=(j == 0))
                        make_hot(R + j, j)
                with dve.Fori(1, loops - 1) as g:
                    for h in range(2):
                        for j, base in enumerate(bases(g * R + h * H), h * H):
                            add(g * R + j, j, base)
                            make_hot((g + 1) * R + j, j)
                for h in range(2):
                    for j, base in enumerate(bases((loops - 1) * R + h * H), h * H):
                        add((loops - 1) * R + j, j, base)

            def anywhere():
                nc.vector.tensor_copy(places[:], m.iota[:]).then_inc(moved, 1)
                nc.vector.nop().then_inc(tile_free, 1)
                with dve.Fori(0, m.tiles) as w:
                    dve.wait_ge(moved, w + 1)
                    nc.vector.nop(nofuse=True)
                    with dve.Fori(0, loops) as g:
                        dve.wait_ge(group_free, w * loops + (g + 1))
                        for j in range(R):
                            nc.vector.tensor_scalar(hot[:, j, :], places[:], m.dst_f[:, ds(g * R + j, 1)], None,
                                                    ALU.is_equal).then_inc(hot_ready, 1)
                    dve.wait_ge(summed, w + 1)
                    tile = m.agg[:, :, ds(w * P, P)]
                    nc.vector.tensor_tensor(tile, tile, m.ps[:, 0:DK, 0:P], ALU.add).then_inc(tile_free, 1)
                    nc.vector.tensor_scalar(places[:], places[:], float(P), None, ALU.add).then_inc(moved, 1)

            branch(dve, in_windows, anywhere)

        @block.tensor
        def _(pe):
            def in_windows():
                def multiply(c, j, round_):
                    pe.wait_ge(landed[j], round_ * 16)
                    pe.wait_ge(hot_ready, c + 1)
                    for k in range(DK):
                        last = nc.tensor.matmul(part_ps(j)[:, k, :], rows[:, j, k * P:(k + 1) * P], hot[:, j, :],
                                                start=True, stop=True)
                    last.then_inc(summed, 1)

                for j in range(R):
                    if j >= B:
                        pe.wait_ge(added, j + 1 - B)
                    multiply(j, j, 1)
                with pe.Fori(1, loops) as g:
                    for j in range(R):
                        pe.wait_ge(added, g * R + (j + 1 - B))
                        multiply(g * R + j, j, g + 1)

            def anywhere():
                def group(w, g, first, last):
                    pe.wait_ge(hot_ready, (w * loops + g) * R + R)
                    for j in range(R):
                        pe.wait_ge(landed[j], (w * loops + (g + 1)) * 16)
                        for k in range(DK):
                            mm = nc.tensor.matmul(m.ps[:, k, 0:P], rows[:, j, k * P:(k + 1) * P], hot[:, j, :],
                                                  start=first and j == 0, stop=last and j == R - 1,
                                                  skip_group_check=True)
                    mm.then_inc(group_free, 1)
                    return mm

                nc.tensor.nop().then_inc(group_free, 1)
                with pe.Fori(0, m.tiles) as w:
                    pe.wait_ge(tile_free, w + 1)
                    group(w, 0, True, False)
                    with pe.Fori(1, loops - 1) as g:
                        group(w, g, False, False)
                    group(w, loops - 1, False, True)
                    nc.tensor.drain().then_inc(summed, 1)

            branch(pe, in_windows, anywhere)


def update_nodes(nc, m, tag, w, bias, table):
    R = TILE_RING
    with Stage(nc) as ctx:
        sem = lambda name: ctx.sem(f"{tag}_{name}")
        cols = ctx.enter_context(nc.sbuf_tensor(f"{tag}_cols", [P, R, DK, P], F32))
        biased = ctx.enter_context(nc.sbuf_tensor(f"{tag}_biased", [P, R, D], F32))
        rows = ctx.enter_context(nc.sbuf_tensor(f"{tag}_rows", [P, R, D], F32))
        cols_ready, multiplied, biased_ready, rows_ready = sem("cols"), sem("multiplied"), sem("biased"), sem("rows")
        turned, kept = sem("turned"), sem("kept")
        stored = [sem(f"stored{j}") for j in range(R)]
        block = ctx.enter_context(nc.Block())

        def product_ps(j):
            return m.ps[:, j, 0:D]

        def turned_ps(j):
            return m.ps[:, j, D:2 * D].rearrange("p (k n) -> p k n", k=DK)

        @block.gpsimd
        def _(pool):
            def fetch(t, j, again, round_):
                if again:
                    pool.wait_ge(multiplied, t + (1 - R))
                    nc.gpsimd.nop(nofuse=True)
                nc.gpsimd.tensor_copy(cols[:, j, :, :], m.agg[:, :, ds(t * P, P)]).then_inc(cols_ready, 1)
            tile_loop(pool, m.tiles, [(0, fetch)])

        @block.tensor
        def _(pe):
            def multiply(t, j, again, round_):
                pe.wait_ge(cols_ready, t + 1)
                if again:
                    pe.wait_ge(kept, t + (1 - R))
                for k in range(DK):
                    last = nc.tensor.matmul(product_ps(j), cols[:, j, k, :], w[:, k, :], start=(k == 0),
                                            stop=(k == DK - 1))
                last.then_inc(multiplied, 1)

            def turn(t, j, again, round_):
                pe.wait_ge(rows_ready, t + 1)
                for k in range(DK):
                    last = nc.tensor.transpose(turned_ps(j)[:, k, :], rows[:, j, k * P:(k + 1) * P], m.ident[:])
                last.then_inc(turned, 1)
            tile_loop(pe, m.tiles, [(0, multiply), (3, turn)])

        @block.vector
        def _(dve):
            def add_bias(t, j, again, round_):
                dve.wait_ge(multiplied, t + 1)
                if again:
                    dve.wait_ge(rows_ready, t + (1 - R))
                nc.vector.scalar_tensor_tensor(biased[:, j, :], product_ps(j), m.dinv[:, ds(t, 1)], bias[:],
                                               ALU.mult, ALU.add).then_inc(biased_ready, 1)

            def keep(t, j, again, round_):
                dve.wait_ge(turned, t + 1)
                nc.vector.tensor_copy(m.agg[:, :, ds(t * P, P)], turned_ps(j)).then_inc(kept, 1)
            tile_loop(dve, m.tiles, [(0, add_bias), (4, keep)])

        @block.scalar
        def _(act):
            def rectify(t, j, again, round_):
                act.wait_ge(biased_ready, t + 1)
                if again:
                    act.wait_ge(turned, t + (1 - R))
                    act.wait_ge(stored[j], round_ * 16)
                nc.scalar.activation(rows[:, j, :], biased[:, j, :], ACT.Relu,
                                     scale=m.dinv[:, ds(t, 1)]).then_inc(rows_ready, 1)
            tile_loop(act, m.tiles, [(0, rectify)])

        @block.sync
        def _(sp):
            def store(t, j, again, round_):
                sp.wait_ge(rows_ready, t + 1)
                sp.dma_start(table[ds(t * P, P), :], rows[:, j, :]).then_inc(stored[j], 16)
            tile_loop(sp, m.tiles, [(0, store)])
            for j in range(R):
                sp.wait_ge(stored[j], m.tiles // R * 16)


def finish_gcn(nc, m, tag):
    R = TILE_RING
    with Stage(nc) as ctx:
        sem = lambda name: ctx.sem(f"{tag}_{name}")
        cols = ctx.enter_context(nc.sbuf_tensor(f"{tag}_cols", [P, R, DK, P], F32))
        biased = ctx.enter_context(nc.sbuf_tensor(f"{tag}_biased", [P, R, P], F32))
        rows = ctx.enter_context(nc.sbuf_tensor(f"{tag}_rows", [P, R, P], F32))
        turned = ctx.enter_context(nc.sbuf_tensor(f"{tag}_turned", [P, R, P], F32))
        cols_ready, multiplied, biased_ready, rows_ready = sem("cols"), sem("multiplied"), sem("biased"), sem("rows")
        turn_done, turned_ready, projected, x_biased, added = (sem("turn_done"), sem("turned"), sem("projected"),
                                                               sem("x_biased"), sem("added"))
        stats, pads_zero = RowStats(nc, m, ctx, "stats1"), sem("pads_zero")
        block = ctx.enter_context(nc.Block())

        @block.gpsimd
        def _(pool):
            def add_bias(t, j, again, round_):
                nc.gpsimd.tensor_tensor(tile_of(m.x, t), tile_of(m.x, t), m.bp[:], ALU.add).then_inc(x_biased, 1)
            tile_loop(pool, m.tiles, [(0, add_bias)])
            pool.wait_ge(stats.done, m.tiles)
            nc.gpsimd.affine_select(out=m.x[:, m.full_tiles, :], in_=m.x[:, m.full_tiles, :], compare_op=ALU.is_ge,
                                    fill=0.0, base=m.tail_nodes - 1, pattern=[[0, D]],
                                    channel_multiplier=-1).then_inc(pads_zero, 1)

        @block.tensor
        def _(pe):
            def multiply(t, j, again, round_):
                pe.wait_ge(cols_ready, t + 1)
                if again:
                    pe.wait_ge(added, t + (1 - R))
                for k in range(DK):
                    last = nc.tensor.matmul(m.ps[:, j, 0:P], cols[:, j, k, :], m.w3[:, k, :], start=(k == 0),
                                            stop=(k == DK - 1))
                last.then_inc(multiplied, 1)

            def turn(t, j, again, round_):
                pe.wait_ge(rows_ready, t + 1)
                nc.tensor.transpose(m.ps[:, j, P:2 * P], rows[:, j, :], m.ident[:]).then_inc(turn_done, 1)

            def project(t, j, again, round_):
                pe.wait_ge(turned_ready, t + 1)
                nc.tensor.matmul(m.ps[:, j, D:2 * D], turned[:, j, :], m.wp[:], start=True,
                                 stop=True).then_inc(projected, 1)
            tile_loop(pe, m.tiles, [(0, multiply), (2, turn), (4, project)])

        @block.vector
        def _(dve):
            def add_bias(t, j, again, round_):
                dve.wait_ge(multiplied, t + 1)
                if again:
                    dve.wait_ge(rows_ready, t + (1 - R))
                nc.vector.scalar_tensor_tensor(biased[:, j, :], m.ps[:, j, 0:P], m.dinv[:, ds(t, 1)], m.b3[:],
                                               ALU.mult, ALU.add).then_inc(biased_ready, 1)

            def add(t, j, again, round_):
                dve.wait_ge(projected, t + 1)
                dve.wait_ge(x_biased, t + 1)
                nc.vector.tensor_tensor(tile_of(m.x, t), tile_of(m.x, t), m.ps[:, j, D:2 * D],
                                        ALU.add).then_inc(added, 1)

            def measure(t, j, again, round_):
                dve.wait_ge(added, t + 1)
                stats.of_tile(t, tile_of(m.x, t))
            tile_loop(dve, m.tiles, [(0, add_bias), (5, add), (6, measure)])
            dve.wait_ge(pads_zero, 1)
            stats.of_tile(m.full_tiles, m.x[:, m.full_tiles, :])
            stats.on_vector(dve, m.tiles + 1)

        @block.scalar
        def _(act):
            def fetch(t, j, again, round_):
                if again:
                    act.wait_ge(multiplied, t + (1 - R))
                nc.scalar.copy(cols[:, j, :, :], m.agg[:, :, ds(t * P, P)]).then_inc(cols_ready, 1)

            def rectify(t, j, again, round_):
                act.wait_ge(biased_ready, t + 1)
                if again:
                    act.wait_ge(turn_done, t + (1 - R))
                nc.scalar.activation(rows[:, j, :], biased[:, j, :], ACT.Relu).then_inc(rows_ready, 1)

            def keep(t, j, again, round_):
                act.wait_ge(turn_done, t + 1)
                if again:
                    act.wait_ge(projected, t + (1 - R))
                nc.scalar.copy(turned[:, j, :], m.ps[:, j, P:2 * P]).then_inc(turned_ready, 1)
            tile_loop(act, m.tiles, [(0, fetch), (2, rectify), (4, keep)])
            stats.on_scalar(act)


def route_all(nc, m, a):
    E = m.experts
    capacity = float(ceil_div(m.nodes * 5, 4 * E))
    with Stage(nc) as ctx:
        sem = lambda name: ctx.sem(f"route_{name}")
        buf = lambda name, shape, dt=F32: ctx.enter_context(nc.sbuf_tensor(f"route_{name}", shape, dt))
        wr, br, mean_col = buf("wr", [P, DK, E]), buf("br", [1, E]), buf("mean_col", [P, DK])
        row, tmp, prob = buf("row", [1, E]), buf("tmp", [1, E]), buf("prob", [1, E])
        over, ratio, expd = buf("over", [1, E]), buf("ratio", [1, E]), buf("expd", [1, E])
        rev_i, rev = buf("rev_i", [1, E], I32), buf("rev", [1, E])
        peak, total, inv = buf("peak", [1, 4]), buf("total", [1, 2]), buf("inv", [1, 2])
        top, code = buf("top", [1, 2]), buf("code", [1, 2])
        choice_f, choice, share = buf("choice_f", [1, 2]), buf("choice", [1, 2], I32), buf("share", [1, 4])
        shares, b2_rows = buf("shares", [P, 2]), buf("b2_rows", [P, 2, D])
        w1, w2 = buf("w1", [P, 2, DK, m.hidden0]), buf("w2", [P, 2, m.hidden0 // P, D])
        rounded, w2_scaled = sem("rounded"), sem("w2_scaled")
        loaded, turned, col_ready, scored = sem("loaded"), sem("turned"), sem("col_ready"), sem("scored")
        chain, exp_asked, exp_done, rev_made = sem("chain"), sem("exp_asked"), sem("exp_done"), sem("rev_made")
        chosen, share_ready, spread, fetched = sem("chosen"), sem("share_ready"), sem("spread"), sem("fetched")
        block = ctx.enter_context(nc.Block())

        @block.sync
        def _(sp):
            sp.dma_start(wr[:], a["ffn0_wr"].rearrange("(k p) e -> p k e", p=P)).then_inc(loaded, 16)
            sp.dma_start(br[:], a["ffn0_br"].rearrange("(o e) -> o e", o=1)).then_inc(loaded, 16)
            sp.wait_ge(chosen, 1)
            for n in range(2):
                e = sp.value_load(choice[0:1, n:n + 1], min_val=0, max_val=E - 1)
                sp.dma_start(w1[:, n, :, :], a["ffn0_w1"][ds(e, 1), :, :]
                             .rearrange("o (k p) f -> p (o k) f", p=P)).then_inc(fetched, 16)
                sp.dma_start(w2[:, n, :, :], a["ffn0_w2"][ds(e, 1), :, :]
                             .rearrange("o (k p) f -> p (o k) f", p=P)).then_inc(fetched, 16)
                sp.dma_start(m.f0_b1[:, n, :], a["ffn0_b1"][ds(e, 1), :, :]
                             .rearrange("o p f -> p (o f)")).then_inc(fetched, 16)
                sp.dma_start(b2_rows[:, n, :], a["ffn0_b2"][ds(e, 1), :]
                             .rearrange("o d -> (o d)").partition_broadcast(P)).then_inc(fetched, 16)
            sp.dma_start(m.gamma[:], a["ffn0_gamma"].partition_broadcast(P)).then_inc(fetched, 16)
            sp.dma_start(m.beta[:], a["ffn0_beta"].partition_broadcast(P)).then_inc(fetched, 16)
            sp.wait_ge(fetched, 16 * 10)

        @block.gpsimd
        def _(pool):
            nc.gpsimd.iota(rev_i[:], pattern=[[-1, E]], base=E, channel_multiplier=0).then_inc(rev_made, 1)

        @block.tensor
        def _(pe):
            for k in range(DK):
                last = nc.tensor.matmul(m.ps[:, 0, k:k + 1], m.mean_row[0:1, k * P:(k + 1) * P], m.ones[0:1, 0:1],
                                        start=True, stop=True)
            last.then_inc(turned, 1)
            pe.wait_ge(col_ready, 1)
            pe.wait_ge(loaded, 32)
            for k in range(DK):
                last = nc.tensor.matmul(m.ps[0:1, 1, 0:E], mean_col[:, k:k + 1], wr[:, k, :], start=(k == 0),
                                        stop=(k == DK - 1))
            last.then_inc(scored, 1)
            pe.wait_ge(share_ready, 1)
            nc.tensor.matmul(m.ps[:, 2, 0:2], m.ones[0:1, :], share[0:1, 2:4], start=True, stop=True).then_inc(spread, 1)

        @block.scalar
        def _(act):
            for n in range(2):
                act.wait_ge(exp_asked, n + 1)
                nc.scalar.activation(expd[:], row[:], ACT.Exp, bias=peak[0:1, n:n + 1],
                                     accum_out=total[0:1, n:n + 1]).then_inc(exp_done, 1)
            act.wait_ge(exp_asked, 3)
            nc.scalar.activation(share[0:1, 1:2], share[0:1, 0:1], ACT.Exp).then_inc(exp_done, 1)
            act.wait_ge(fetched, 16 * 10)
            nc.scalar.copy(m.f0_w1_hi[:], w1[:]).then_inc(rounded, 1)
            for n in range(2):
                act.wait_ge(w2_scaled, n + 1)
                nc.scalar.copy(m.f0_w2_hi[:, n, :, :], w2[:, n, :, :]).then_inc(rounded, 1)

        @block.vector
        def _(dve):
            links = [0]

            def link(ins):
                links[0] += 1
                ins.then_inc(chain, 1)
                dve.wait_ge(chain, links[0])

            def softmax(n, out):
                link(nc.vector.reduce_max(peak[0:1, 2:3], row[:], AX.X))
                nc.vector.tensor_scalar(peak[0:1, n:n + 1], peak[0:1, 2:3], -1.0, None, ALU.mult).then_inc(exp_asked, 1)
                dve.wait_ge(exp_done, n + 1)
                link(nc.vector.reciprocal(inv[0:1, n:n + 1], total[0:1, n:n + 1]))
                link(nc.vector.tensor_scalar(out, expd[:], inv[0:1, n:n + 1], None, ALU.mult))

            dve.wait_ge(turned, 1)
            nc.vector.tensor_copy(mean_col[:], m.ps[:, 0, 0:DK]).then_inc(col_ready, 1)
            dve.wait_ge(rev_made, 1)
            nc.vector.tensor_copy(rev[:], rev_i[:])
            dve.wait_ge(scored, 1)
            link(nc.vector.tensor_tensor(row[:], m.ps[0:1, 1, 0:E], br[:], ALU.add))
            softmax(0, prob[:])
            link(nc.vector.tensor_scalar(tmp[:], prob[:], float(m.nodes), None, ALU.mult))
            link(nc.vector.tensor_scalar(over[:], tmp[:], capacity, None, ALU.is_gt))
            link(nc.vector.tensor_scalar(tmp[:], tmp[:], capacity, None, ALU.max))
            link(nc.vector.reciprocal(ratio[:], tmp[:]))
            link(nc.vector.scalar_tensor_tensor(ratio[:], ratio[:], capacity, over[:], ALU.mult, ALU.mult))
            link(nc.vector.tensor_scalar(over[:], over[:], -1.0, 1.0, ALU.mult, ALU.add))
            link(nc.vector.tensor_tensor(ratio[:], ratio[:], over[:], ALU.add))
            link(nc.vector.tensor_tensor(row[:], prob[:], ratio[:], ALU.mult))
            softmax(1, prob[:])
            for n in range(2):
                link(nc.vector.reduce_max(top[0:1, n:n + 1], prob[:], AX.X))
                link(nc.vector.tensor_scalar(tmp[:], prob[:], top[0:1, n:n + 1], None, ALU.is_equal))
                link(nc.vector.tensor_tensor(tmp[:], tmp[:], rev[:], ALU.mult))
                link(nc.vector.reduce_max(code[0:1, n:n + 1], tmp[:], AX.X))
                if n == 0:
                    link(nc.vector.tensor_scalar(tmp[:], rev[:], code[0:1, 0:1], -2.0, ALU.is_equal, ALU.mult))
                    link(nc.vector.tensor_tensor(prob[:], prob[:], tmp[:], ALU.add))
            link(nc.vector.tensor_scalar(choice_f[:], code[:], -1.0, float(E), ALU.mult, ALU.add))
            nc.vector.tensor_copy(choice[:], choice_f[:]).then_inc(chosen, 1)
            nc.vector.tensor_tensor(share[0:1, 0:1], top[0:1, 1:2], top[0:1, 0:1], ALU.subtract).then_inc(exp_asked, 1)
            dve.wait_ge(exp_done, 3)
            link(nc.vector.tensor_scalar(inv[0:1, 0:1], share[0:1, 1:2], 1.0, None, ALU.add))
            link(nc.vector.reciprocal(share[0:1, 2:3], inv[0:1, 0:1]))
            nc.vector.tensor_tensor(share[0:1, 3:4], share[0:1, 1:2], share[0:1, 2:3], ALU.mult).then_inc(share_ready, 1)
            dve.wait_ge(spread, 1)
            link(nc.vector.tensor_copy(shares[:], m.ps[:, 2, 0:2]))
            dve.wait_ge(fetched, 16 * 10)
            for n in range(2):
                nc.vector.tensor_scalar(w2[:, n, :, :], w2[:, n, :, :], shares[:, n:n + 1], None,
                                        ALU.mult).then_inc(w2_scaled, 1)
            link(nc.vector.tensor_scalar(m.f0_b2[:], b2_rows[:, 0, :], shares[:, 0:1], None, ALU.mult))
            nc.vector.scalar_tensor_tensor(m.f0_b2[:], b2_rows[:, 1, :], shares[:, 1:2], m.f0_b2[:],
                                           ALU.mult, ALU.add)
            dve.wait_ge(rounded, 1)
            nc.vector.tensor_tensor(m.f0_w1_lo[:], w1[:], m.f0_w1_hi[:].bitcast(F32), ALU.subtract)
            for n in range(2):
                dve.wait_ge(rounded, n + 2)
                nc.vector.tensor_tensor(m.f0_w2_lo[:, n, :, :], w2[:, n, :, :], m.f0_w2_hi[:, n, :, :].bitcast(F32),
                                        ALU.subtract)


def multiply_halves(nc, out, left, right, start, stop):
    for n, (i, j) in enumerate(((1, 0), (0, 1), (0, 0))):
        last = nc.tensor.matmul(out, left[i], right[j], start=start and n == 0, stop=stop and n == 2,
                                skip_group_check=True)
    return last


def two_experts(nc, m):
    T = 4
    F = 2 * m.hidden0 // P
    LAG, HID_RING = 4, 2
    chunks = m.tiles // T
    assert m.tiles % T == 1
    with Stage(nc) as ctx:
        sem = lambda name: ctx.sem(f"two_{name}")
        cols_hi, cols_lo = (ctx.enter_context(nc.sbuf_tensor(f"two_cols_{half}", [P, DK, T * P], F32R))
                            for half in ("hi", "lo"))
        hid = ctx.enter_context(nc.sbuf_tensor("two_hid", [P, HID_RING, T * P], F32))
        hid_hi, hid_lo = (ctx.enter_context(nc.sbuf_tensor(f"two_hid_{half}", [P, F, T * P], F32R))
                          for half in ("hi", "lo"))
        up_done, gelu_done, down_done = sem("up"), sem("gelu"), sem("down")
        own_made, own_biased, added = sem("own_made"), sem("own_biased"), sem("added")
        stats = RowStats(nc, m, ctx, "stats2")
        cols_rounded, cols_split, hid_rounded, hid_split = (sem("cols_rounded"), sem("cols_split"),
                                                            sem("hid_rounded"), sem("hid_split"))
        block = ctx.enter_context(nc.Block())

        def cols_of(c, width):
            return m.agg[:, :, ds(c * T * P, width)]

        def down_ps(i):
            return m.ps[:, 4 + i // 2, i % 2 * D:(i % 2 + 1) * D]

        @block.tensor
        def _(pe):
            def up(c, f, width, first):
                if not first or f >= 4:
                    pe.wait_ge(gelu_done, c * F + (f - 3))
                e, at = f // (F // 2), ds(f % (F // 2) * P, P)
                for k in range(DK):
                    last = multiply_halves(nc, m.ps[:, f % 4, 0:width], (m.f0_w1_hi[:, e, k, at], m.f0_w1_lo[:, e, k, at]),
                                           (cols_hi[:, k, 0:width], cols_lo[:, k, 0:width]), k == 0, k == DK - 1)
                last.then_inc(up_done, 1)

            def down(c, f, tiles, first):
                pe.wait_ge(hid_split, c * F + (f + 1))
                if f == 0 and not first:
                    pe.wait_ge(added, c * T)
                e, s = f // (F // 2), f % (F // 2)
                for i in range(tiles):
                    at = slice(i * P, (i + 1) * P)
                    last = multiply_halves(nc, down_ps(i), (hid_hi[:, f, at], hid_lo[:, f, at]),
                                           (m.f0_w2_hi[:, e, s, :], m.f0_w2_lo[:, e, s, :]),
                                           f == 0 and i % 2 == 0, f == F - 1)
                last.then_inc(down_done, 1)

            def both(c, first=False, width=T * P, tiles=T):
                pe.wait_ge(cols_split, c + 1)
                for f in range(F):
                    up(c, f, width, first)
                    if f >= LAG:
                        down(c, f - LAG, tiles, first)
                for f in range(F - LAG, F):
                    down(c, f, tiles, first)

            both(0, first=True)
            with pe.Fori(1, chunks) as c:
                both(c)
            both(chunks, width=P, tiles=1)

        @block.scalar
        def _(act):
            def gelu(c, width, first=False):
                nc.scalar.copy(cols_hi[:, :, 0:width], cols_of(c, width)).then_inc(cols_rounded, 1)
                for f in range(F):
                    if not first or f >= HID_RING:
                        act.wait_ge(hid_split, c * F + (f + 1 - HID_RING))
                    act.wait_ge(up_done, c * F + (f + 1))
                    nc.scalar.activation(hid[:, f % HID_RING, 0:width], m.ps[:, f % 4, 0:width], ACT.Gelu,
                                         bias=m.f0_b1[:, f // (F // 2), f % (F // 2):f % (F // 2) + 1])\
                        .then_inc(gelu_done, 1)
                    act.wait_ge(gelu_done, c * F + (f + 1))
                    if not first:
                        act.wait_ge(down_done, c * F + (f + 1 - F))
                    nc.scalar.copy(hid_hi[:, f, 0:width], hid[:, f % HID_RING, 0:width]).then_inc(hid_rounded, 1)

            gelu(0, T * P, first=True)
            with act.Fori(1, chunks) as c:
                act.wait_ge(up_done, c * F)
                gelu(c, T * P)
            act.wait_ge(up_done, chunks * F)
            gelu(chunks, P)
            stats.on_scalar(act)

        @block.vector
        def _(dve):
            def split_cols(c, width):
                dve.wait_ge(cols_rounded, c + 1)
                nc.vector.tensor_tensor(cols_lo[:, :, 0:width], cols_of(c, width),
                                        cols_hi[:, :, 0:width].bitcast(F32), ALU.subtract).then_inc(cols_split, 1)

            def split_hid(c, fs, width):
                for f in fs:
                    dve.wait_ge(hid_rounded, c * F + (f + 1))
                    nc.vector.tensor_tensor(hid_lo[:, f, 0:width], hid[:, f % HID_RING, 0:width],
                                            hid_hi[:, f, 0:width].bitcast(F32), ALU.subtract).then_inc(hid_split, 1)

            def rows_of(c, i):
                return m.agg[:, :, ds((c * T + i) * P, P)]

            def make_own(c, tiles):
                dve.wait_ge(cols_split, c + 1)
                for i in range(tiles):
                    t = c * T + i
                    nc.vector.tensor_scalar(rows_of(c, i), m.x[:, ds(t, 1), :].rearrange("p t (k n) -> p (t k) n", k=DK),
                                            m.mean[:, ds(t, 1)], m.scale[:, ds(t, 1)],
                                            ALU.subtract, ALU.mult).then_inc(own_made, 1)
                for i in range(tiles):
                    dve.wait_ge(own_made, c * T + (i + 1))
                    nc.vector.tensor_tensor(rows_of(c, i), rows_of(c, i), m.f0_b2[:].rearrange("p (k n) -> p k n", k=DK),
                                            ALU.add).then_inc(own_biased, 1)

            def combine(c, tiles):
                dve.wait_ge(down_done, c * F + F)
                for i in range(tiles):
                    dve.wait_ge(own_biased, c * T + (i + 1))
                    nc.vector.tensor_tensor(rows_of(c, i), rows_of(c, i),
                                            down_ps(i).rearrange("p (k n) -> p k n", k=DK), ALU.add).then_inc(added, 1)
                for i in range(tiles):
                    dve.wait_ge(added, c * T + (i + 1))
                    stats.of_tile(c * T + i, rows_of(c, i))

            def hidden_and_own(c, width, tiles):
                split_hid(c, range(LAG), width)
                make_own(c, tiles)
                split_hid(c, range(LAG, F), width)

            split_cols(0, T * P)
            with dve.Fori(0, chunks - 1) as c:
                hidden_and_own(c, T * P, T)
                dve.wait_ge(up_done, c * F + F)
                split_cols(c + 1, T * P)
                combine(c, T)
            hidden_and_own(chunks - 1, T * P, T)
            split_cols(chunks, P)
            combine(chunks - 1, T)
            hidden_and_own(chunks, P, 1)
            combine(chunks, 1)
            stats.on_vector(dve, m.tiles)


def add_and_project(nc, m, a, heads_table, left_table):
    R = TILE_RING
    H = m.heads
    with Stage(nc) as ctx:
        sem = lambda name: ctx.sem(f"proj_{name}")
        buf = lambda name, shape, dt=F32: ctx.enter_context(nc.sbuf_tensor(f"proj_{name}", shape, dt))
        w, attn, prod = buf("w", [P, DK, D + 2 * H]), buf("attn", [P, 2, D]), buf("prod", [P, D])
        scaled, off_mean = buf("scaled", [P, R, D]), buf("off_mean", [P, R, D])
        cols, out = buf("cols", [P, R, DK, P]), buf("out", [P, R, D + 2 * H])
        stats, mv, minus_mean = buf("stats", [P, R, 6]), buf("mv", [P, R, 2]), buf("minus_mean", [P, R])
        std, inv, eps = buf("std", [P, R]), buf("inv", [P, R]), buf("eps", [P, 1])
        loaded, prod_made, wa_made, eps_made = sem("loaded"), sem("prod_made"), sem("wa_made"), sem("eps_made")
        x_shifted, scaled_made, x_done = sem("x_shifted"), sem("scaled"), sem("x_done")
        stats_done, mv_done, mean_ready, std_done, inv_done = (sem("stats"), sem("mv"), sem("mean"), sem("std"),
                                                               sem("inv"))
        off_mean_ready, turned, cols_ready, multiplied = sem("off_mean"), sem("turned"), sem("cols"), sem("multiplied")
        heads_kept = sem("heads_kept")
        stored = [sem(f"stored{j}") for j in range(R)]
        block = ctx.enter_context(nc.Block())

        @block.sync
        def _(sp):
            sp.dma_start(w[:, :, 0:D], a["gat_w"].rearrange("(k p) n -> p k n", p=P)).then_inc(loaded, 16)
            sp.dma_start(attn[:, 0, :], a["gat_l"].rearrange("h d -> (h d)").partition_broadcast(P)).then_inc(loaded, 16)
            sp.dma_start(attn[:, 1, :], a["gat_r"].rearrange("h d -> (h d)").partition_broadcast(P)).then_inc(loaded, 16)

            def store(t, j, again, round_):
                sp.wait_ge(heads_kept, t + 1)
                sp.dma_start(heads_table[ds(t * P, P), :], out[:, j, 0:D + H]).then_inc(stored[j], 16)
                sp.dma_start(left_table[ds(t * P, P), :], out[:, j, D + H:D + 2 * H]).then_inc(stored[j], 16)
            tile_loop(sp, m.tiles, [(0, store)])
            for j in range(R):
                sp.wait_ge(stored[j], m.tiles // R * 32)

        @block.gpsimd
        def _(pool):
            def shift(t, j, again, round_):
                nc.gpsimd.tensor_tensor(tile_of(m.x, t), tile_of(m.x, t), m.beta[:], ALU.add).then_inc(x_shifted, 1)
            tile_loop(pool, m.tiles, [(0, shift)])

        @block.vector
        def _(dve):
            nc.vector.memset(eps[:], EPS).then_inc(eps_made, 1)
            dve.wait_ge(loaded, 48)
            for n, side in enumerate((1, 0)):
                for k in range(DK):
                    s = n * DK + k
                    if s:
                        dve.wait_ge(wa_made, s)
                    nc.vector.tensor_tensor(prod[:], w[:, k, 0:D], attn[:, side, :], ALU.mult).then_inc(prod_made, 1)
                    dve.wait_ge(prod_made, s + 1)
                    nc.vector.reduce_sum(w[:, k, D + n * H:D + (n + 1) * H], prod[:].rearrange("p (h d) -> p h d", h=H),
                                         AX.X).then_inc(wa_made, 1)

            def scale(t, j, again, round_):
                if again:
                    dve.wait_ge(x_done, t + (1 - R))
                nc.vector.scalar_tensor_tensor(scaled[:, j, :].rearrange("p (k n) -> p k n", k=DK),
                                               m.agg[:, :, ds(t * P, P)], m.mean[:, ds(t, 1)],
                                               m.gamma[:].rearrange("p (k n) -> p k n", k=DK),
                                               ALU.subtract, ALU.mult).then_inc(scaled_made, 1)

            def add(t, j, again, round_):
                dve.wait_ge(scaled_made, t + 1)
                dve.wait_ge(x_shifted, t + 1)
                nc.vector.scalar_tensor_tensor(tile_of(m.x, t), scaled[:, j, :], m.scale[:, ds(t, 1)],
                                               tile_of(m.x, t), ALU.mult, ALU.add).then_inc(x_done, 1)

            def measure(t, j, again, round_):
                dve.wait_ge(x_done, t + 1)
                if again:
                    dve.wait_ge(mv_done, t + (1 - R))
                nc.vector.nop(nofuse=True)
                nc.vector.bn_stats(stats[:, j, :], tile_of(m.x, t)).then_inc(stats_done, 1)

            def aggregate(t, j, again, round_):
                dve.wait_ge(stats_done, t + 1)
                if again:
                    dve.wait_ge(std_done, t + (1 - R))
                    dve.wait_ge(mean_ready, t + (1 - R))
                nc.vector.nop(nofuse=True)
                nc.vector.bn_aggr(mv[:, j, :], stats[:, j, :]).then_inc(mv_done, 1)

            def negate_mean(t, j, again, round_):
                dve.wait_ge(mv_done, t + 1)
                if again:
                    dve.wait_ge(off_mean_ready, t + (1 - R))
                nc.vector.tensor_scalar(minus_mean[:, j:j + 1], mv[:, j, 0:1], -1.0, None, ALU.mult)\
                    .then_inc(mean_ready, 1)

            def invert(t, j, again, round_):
                dve.wait_ge(std_done, t + 1)
                if again:
                    dve.wait_ge(heads_kept, t + (1 - R))
                nc.vector.reciprocal(inv[:, j:j + 1], std[:, j:j + 1]).then_inc(inv_done, 1)
            tile_loop(dve, m.tiles, [(0, scale), (1, add), (2, measure), (3, aggregate), (4, negate_mean), (6, invert)])

        @block.scalar
        def _(act):
            act.wait_ge(eps_made, 1)

            def root(t, j, again, round_):
                act.wait_ge(mv_done, t + 1)
                if again:
                    act.wait_ge(inv_done, t + (1 - R))
                nc.scalar.activation(std[:, j:j + 1], mv[:, j, 1:2], ACT.Sqrt, bias=eps[:]).then_inc(std_done, 1)

            def subtract_mean(t, j, again, round_):
                act.wait_ge(mean_ready, t + 1)
                if again:
                    act.wait_ge(turned, t + (1 - R))
                nc.scalar.nop(nofuse=True)
                nc.scalar.activation(off_mean[:, j, :], tile_of(m.x, t), ACT.Identity,
                                     bias=minus_mean[:, j:j + 1]).then_inc(off_mean_ready, 1)

            def keep_cols(t, j, again, round_):
                act.wait_ge(turned, t + 1)
                if again:
                    act.wait_ge(multiplied, t + (1 - R))
                nc.scalar.copy(cols[:, j, :, :],
                               m.ps[:, j, 0:D].rearrange("p (k n) -> p k n", k=DK)).then_inc(cols_ready, 1)

            def keep_heads(t, j, again, round_):
                act.wait_ge(multiplied, t + 1)
                act.wait_ge(inv_done, t + 1)
                if again:
                    act.wait_ge(stored[j], round_ * 32)
                nc.scalar.activation(out[:, j, :], m.ps[:, j, 0:D + 2 * H], ACT.Identity,
                                     scale=inv[:, j:j + 1]).then_inc(heads_kept, 1)
            tile_loop(act, m.tiles, [(0, root), (1, subtract_mean), (2, keep_cols), (4, keep_heads)])

        @block.tensor
        def _(pe):
            def turn(t, j, again, round_):
                pe.wait_ge(off_mean_ready, t + 1)
                if again:
                    pe.wait_ge(heads_kept, t + (1 - R))
                for k in range(DK):
                    last = nc.tensor.transpose(m.ps[:, j, k * P:(k + 1) * P], off_mean[:, j, k * P:(k + 1) * P],
                                               m.ident[:])
                last.then_inc(turned, 1)

            def multiply(t, j, again, round_):
                pe.wait_ge(cols_ready, t + 1)
                for k in range(DK):
                    last = nc.tensor.matmul(m.ps[:, j, 0:D + 2 * H], cols[:, j, k, :], w[:, k, :], start=(k == 0),
                                            stop=(k == DK - 1))
                last.then_inc(multiplied, 1)

            pe.wait_ge(wa_made, 2 * DK)
            tile_loop(pe, m.tiles, [(0, turn), (2, multiply)])


def attend(nc, m, a, heads_table, left_table):
    R = TILE_RING
    H = m.heads
    with Stage(nc) as ctx:
        sem = lambda name: ctx.sem(f"att_{name}")
        buf = lambda name, shape, dt=F32: ctx.enter_context(nc.sbuf_tensor(f"att_{name}", shape, dt))
        src_col, dst_col = buf("src_col", [P, R], I32), buf("dst_col", [P, R], I32)
        rows, left = buf("rows", [P, R, D + H]), buf("left", [P, R, H])
        score, flat, peak = buf("score", [P, R, H]), buf("flat", [P, R, H]), buf("peak", [P, R])
        weight, total, inv = buf("weight", [P, R, H]), buf("total", [P, R]), buf("inv", [P, R])
        prod, head_sum = buf("prod", [P, R, D]), buf("head_sum", [P, R, D // H])
        index_ready, chain, scores_ready, exp_done, used = (sem("index_ready"), sem("chain"), sem("scores_ready"),
                                                            sem("exp_done"), sem("used"))
        landed = [sem(f"landed{j}") for j in range(R)]
        stats = RowStats(nc, m, ctx, "stats4")
        E = m.experts
        gate_w, off_mean, cols = buf("gate_w", [P, DK, E]), buf("off_mean", [P, R, D]), buf("cols", [P, R, DK, P])
        minus_mean = buf("minus_mean", [P, R])
        loaded, mean_ready, off_mean_ready = sem("loaded"), sem("mean_ready"), sem("off_mean_ready")
        turned, cols_ready, gated, gates_kept = sem("turned"), sem("cols_ready"), sem("gated"), sem("gates_kept")
        block = ctx.enter_context(nc.Block())

        @block.scalar
        def _(act):
            def put_index(t, j, again, round_):
                if again:
                    act.wait_ge(landed[j], round_ * 32)
                nc.scalar.copy(src_col[:, j:j + 1], m.src[:, ds(t, 1)]).then_inc(index_ready, 1)
                nc.scalar.copy(dst_col[:, j:j + 1], m.dst[:, ds(t, 1)]).then_inc(index_ready, 1)

            def exps(t, j, again, round_):
                act.wait_ge(scores_ready, t + 1)
                if again:
                    act.wait_ge(used, t + (1 - R))
                nc.scalar.activation(weight[:, j, :], score[:, j, :], ACT.Exp, bias=peak[:, j:j + 1],
                                     accum_out=total[:, j:j + 1]).then_inc(exp_done, 1)
            def subtract_mean(t, j, again, round_):
                act.wait_ge(mean_ready, t + 1)
                if again:
                    act.wait_ge(turned, t + (1 - R))
                nc.scalar.nop(nofuse=True)
                nc.scalar.activation(off_mean[:, j, :], tile_of(m.x, t), ACT.Identity,
                                     bias=minus_mean[:, j:j + 1]).then_inc(off_mean_ready, 1)

            def keep_cols(t, j, again, round_):
                act.wait_ge(turned, t + 1)
                if again:
                    act.wait_ge(gated, t + (1 - R))
                nc.scalar.copy(cols[:, j, :, :],
                               m.ps[:, j, 0:D].rearrange("p (k n) -> p k n", k=DK)).then_inc(cols_ready, 1)

            def keep_gates(t, j, again, round_):
                act.wait_ge(gated, t + 1)
                nc.scalar.copy(tile_of(m.gates, t), m.ps[:, j, D:D + E]).then_inc(gates_kept, 1)
            tile_loop(act, m.tiles, [(0, put_index), (5, exps), (8, subtract_mean), (9, keep_cols), (10, keep_gates)])
            stats.on_scalar(act)

        @block.sync
        def _(sp):
            sp.dma_start(gate_w[:], a["gate_w"].rearrange("(k p) n -> p k n", p=P)).then_inc(loaded, 16)

        @block.tensor
        def _(pe):
            def turn(t, j, again, round_):
                pe.wait_ge(off_mean_ready, t + 1)
                if again:
                    pe.wait_ge(gates_kept, t + (1 - R))
                for k in range(DK):
                    last = nc.tensor.transpose(m.ps[:, j, k * P:(k + 1) * P], off_mean[:, j, k * P:(k + 1) * P],
                                               m.ident[:])
                last.then_inc(turned, 1)

            def gate(t, j, again, round_):
                pe.wait_ge(cols_ready, t + 1)
                for k in range(DK):
                    last = nc.tensor.matmul(m.ps[:, j, D:D + E], cols[:, j, k, :], gate_w[:, k, :],
                                            start=(k == 0), stop=(k == DK - 1))
                last.then_inc(gated, 1)
            pe.wait_ge(loaded, 16)
            tile_loop(pe, m.tiles, [(0, turn), (1, gate)])

        @block.gpsimd
        def _(pool):
            def gather(t, j, again, round_):
                pool.wait_ge(index_ready, t * 2 + 2)
                if again:
                    pool.wait_ge(used, t + (1 - R))
                nc.gpsimd.nop(nofuse=True)
                nc.gpsimd.indirect_dma_start(
                    out=rows[:, j, :], out_offset=None, in_=heads_table[:, :],
                    in_offset=bass.IndirectOffsetOnAxis(ap=dst_col[:, j:j + 1], axis=0)).then_inc(landed[j], 16)
                nc.gpsimd.indirect_dma_start(
                    out=left[:, j, :], out_offset=None, in_=left_table[:, :],
                    in_offset=bass.IndirectOffsetOnAxis(ap=src_col[:, j:j + 1], axis=0)).then_inc(landed[j], 16)
            tile_loop(pool, m.tiles, [(0, gather)])

        @block.vector
        def _(dve):
            STEPS = 7

            def scores(t, j, again, round_):
                dve.wait_ge(landed[j], (round_ + 1) * 32)
                nc.vector.tensor_tensor(flat[:, j, :], left[:, j, :], rows[:, j, D:D + H], ALU.add).then_inc(chain, 1)

            def leak(t, j, again, round_):
                dve.wait_ge(chain, 1 + t)
                nc.vector.scalar_tensor_tensor(score[:, j, :], flat[:, j, :], 0.01, flat[:, j, :], ALU.mult,
                                               ALU.max).then_inc(leaked, 1)

            def peaks(t, j, again, round_):
                dve.wait_ge(leaked, 1 + t)
                nc.vector.tensor_reduce(peak[:, j:j + 1], score[:, j, :], AX.X, ALU.max,
                                        negate=True).then_inc(scores_ready, 1)

            def weigh(t, j, again, round_):
                dve.wait_ge(exp_done, t + 1)
                nc.vector.reciprocal(inv[:, j:j + 1], total[:, j:j + 1]).then_inc(inverted, 1)
                nc.vector.tensor_tensor(prod[:, j, :].rearrange("p (h d) -> p h d", h=H),
                                        rows[:, j, 0:D].rearrange("p (h d) -> p h d", h=H),
                                        weight[:, j, :].unsqueeze(2).to_broadcast([P, H, D // H]),
                                        ALU.mult).then_inc(weighed, 1)

            def sum_heads(t, j, again, round_):
                dve.wait_ge(weighed, t + 1)
                nc.vector.reduce_sum(head_sum[:, j, :], prod[:, j, :].rearrange("p (h d) -> p d h", h=H),
                                     AX.X).then_inc(head_summed, 1)

            def add(t, j, again, round_):
                dve.wait_ge(head_summed, t + 1)
                dve.wait_ge(inverted, t + 1)
                xt = tile_of(m.x, t).rearrange("p (h d) -> p h d", h=H)
                nc.vector.scalar_tensor_tensor(xt, head_sum[:, j, :].unsqueeze(1).to_broadcast([P, H, D // H]),
                                               inv[:, j:j + 1], xt, ALU.mult, ALU.add).then_inc(used, 1)

            leaked, inverted, weighed, head_summed = sem("leaked"), sem("inverted"), sem("weighed"), sem("head_summed")
            def measure(t, j, again, round_):
                dve.wait_ge(used, t + 1)
                stats.of_tile(t, tile_of(m.x, t))

            def means(t, j, again, round_):
                dve.wait_ge(stats.done, t + 1)
                if again:
                    dve.wait_ge(off_mean_ready, t + (1 - R))
                halves = m.stats[:, ds(t, 1), :]
                nc.vector.tensor_scalar(minus_mean[:, j:j + 1], halves[:, :, 1], halves[:, :, 4], -0.5, ALU.add,
                                        ALU.mult).then_inc(mean_ready, 1)
            tile_loop(dve, m.tiles, [(0, scores), (2, measure), (0, leak), (1, weigh), (0, peaks), (1, sum_heads),
                                     (3, means), (1, add)])
            stats.on_vector(dve, m.tiles)


def assign_slots(nc, m, a):
    E, T, C = m.experts, m.tiles, m.capacity
    with Stage(nc) as ctx:
        sem = lambda name: ctx.sem(f"slot_{name}")
        buf = lambda name, shape, dt=F32: ctx.enter_context(nc.sbuf_tensor(f"slot_{name}", shape, dt))
        peak, total, code = buf("peak", [P, T]), buf("total", [P, T]), buf("code", [P, T])
        low, one_hot = buf("low", [P, T, E]), buf("one_hot", [P, T, E])
        rev_i, rev = buf("rev_i", [P, E], I32), buf("rev", [P, E])
        upper, bias, loaded = buf("upper", [P, P]), buf("bias", [P, E]), sem("loaded")
        sums = buf("sums", [P, 2, T, E])
        totals, place, kept_f = buf("totals", [P, T, E]), buf("place", [P, T]), buf("kept_f", [P, T])
        first, to, back = buf("first", [P, T]), buf("to", [P, T]), buf("back", [P, T])
        chain, rev_made, upper_made, low_ready, exp_done = (sem("chain"), sem("rev_made"), sem("upper_made"),
                                                            sem("low_ready"), sem("exp_done"))
        hot_ready, counted, to_ready, to_masked = sem("hot_ready"), sem("counted"), sem("to_ready"), sem("to_masked")
        block = ctx.enter_context(nc.Block())
        wide = lambda v: v.unsqueeze(2).to_broadcast([P, T, E])
        flat = lambda v: v.rearrange("p t e -> p (t e)")

        @block.sync
        def _(sp):
            sp.dma_start(bias[:], a["gate_b"].partition_broadcast(P)).then_inc(loaded, 16)

        @block.gpsimd
        def _(pool):
            nc.gpsimd.iota(rev_i[:], pattern=[[-1, E]], base=E, channel_multiplier=0).then_inc(rev_made, 1)
            nc.gpsimd.memset(upper[:], 1.0).then_inc(rev_made, 1)
            pool.wait_ge(rev_made, 2)
            nc.gpsimd.affine_select(out=upper[:], in_=upper[:], compare_op=ALU.is_ge, fill=0.0, base=0,
                                    pattern=[[1, P]], channel_multiplier=-1).then_inc(upper_made, 1)
            pool.wait_ge(to_ready, 1)
            nc.gpsimd.affine_select(out=to[:, T - 1:T], in_=to[:, T - 1:T], compare_op=ALU.is_ge,
                                    fill=float(4 * E * C), base=m.tail_nodes - 1, pattern=[[0, 1]],
                                    channel_multiplier=-1).then_inc(to_masked, 1)

        @block.scalar
        def _(act):
            act.wait_ge(low_ready, 1)
            nc.scalar.activation(low[:], low[:], ACT.Exp).then_inc(exp_done, 1)

        @block.tensor
        def _(pe):
            pe.wait_ge(hot_ready, 1)
            pe.wait_ge(upper_made, 1)
            nc.tensor.matmul(m.ps[:, 0, 0:T * E], upper[:], flat(one_hot[:]), start=True, stop=True)
            nc.tensor.matmul(m.ps[:, 1, 0:T * E], m.ones[:], flat(one_hot[:]), start=True, stop=True).then_inc(counted, 1)

        @block.vector
        def _(dve):
            links = [0]

            def link(ins):
                links[0] += 1
                ins.then_inc(chain, 1)
                dve.wait_ge(chain, links[0])

            link(nc.vector.tensor_tensor(m.gates[:], m.gates[:], wide(m.scale[:]), ALU.mult))
            dve.wait_ge(loaded, 16)
            link(nc.vector.tensor_tensor(m.gates[:], m.gates[:], bias[:].unsqueeze(1).to_broadcast([P, T, E]), ALU.add))
            dve.wait_ge(rev_made, 1)
            link(nc.vector.tensor_copy(rev[:], rev_i[:]))
            revs = rev[:].unsqueeze(1).to_broadcast([P, T, E])
            link(nc.vector.reduce_max(peak[:], m.gates[:], AX.X))
            nc.vector.tensor_tensor(low[:], m.gates[:], wide(peak[:]), ALU.subtract).then_inc(low_ready, 1)
            link(nc.vector.tensor_tensor(one_hot[:], m.gates[:], wide(peak[:]), ALU.is_equal))
            link(nc.vector.tensor_tensor(one_hot[:], one_hot[:], revs, ALU.mult))
            link(nc.vector.reduce_max(code[:], one_hot[:], AX.X))
            nc.vector.tensor_tensor(one_hot[:], revs, wide(code[:]), ALU.is_equal).then_inc(hot_ready, 1)
            nc.vector.tensor_scalar(first[:], code[:], -float(C), float(E * C), ALU.mult, ALU.add)
            dve.wait_ge(exp_done, 1)
            link(nc.vector.reduce_sum(total[:], low[:], AX.X))
            link(nc.vector.reciprocal(m.prob[:], total[:]))
            dve.wait_ge(counted, 1)
            link(nc.vector.tensor_copy(flat(totals[:]), m.ps[:, 1, 0:T * E]))
            link(nc.vector.tensor_copy(sums[:, 0, :, :], totals[:]))
            now, step = 0, 1
            while step < T:
                nc.vector.tensor_copy(sums[:, 1 - now, 0:step, :], sums[:, now, 0:step, :])
                link(nc.vector.tensor_tensor(sums[:, 1 - now, step:T, :], sums[:, now, step:T, :],
                                             sums[:, now, 0:T - step, :], ALU.add))
                now, step = 1 - now, 2 * step
            link(nc.vector.tensor_tensor(totals[:], sums[:, now, :, :], totals[:], ALU.subtract))
            link(nc.vector.tensor_tensor(flat(totals[:]), flat(totals[:]), m.ps[:, 0, 0:T * E], ALU.add))
            link(nc.vector.tensor_tensor(totals[:], totals[:], one_hot[:], ALU.mult))
            link(nc.vector.reduce_sum(place[:], totals[:], AX.X))
            link(nc.vector.tensor_scalar(place[:], place[:], -1.0, None, ALU.add))
            link(nc.vector.tensor_scalar(kept_f[:], place[:], float(C), None, ALU.is_lt))
            link(nc.vector.tensor_tensor(first[:], first[:], place[:], ALU.add))
            link(nc.vector.tensor_scalar(place[:], kept_f[:], -4.0 * E * C, 4.0 * E * C, ALU.mult, ALU.add))
            nc.vector.tensor_tensor(to[:], first[:], place[:], ALU.add).then_inc(to_ready, 1)
            link(nc.vector.tensor_scalar(first[:], first[:], -float(E * C), None, ALU.add))
            link(nc.vector.tensor_tensor(first[:], first[:], kept_f[:], ALU.mult))
            link(nc.vector.tensor_scalar(back[:], first[:], float(E * C), None, ALU.add))
            nc.vector.tensor_copy(m.back[:], back[:])
            dve.wait_ge(to_masked, 1)
            nc.vector.tensor_copy(m.to[:], to[:])


def load_expert(nc, m, a, e, p, which):
    w, b, landed = (m.ffn1_w1, m.ffn1_b1, m.w1_landed) if which == 1 else (m.ffn1_w2, m.ffn1_b2, m.w2_landed)
    nc.sync.dma_start(w[:], a[f"ffn1_w{which}"][ds(e, 1), :, :].rearrange("o (k p) f -> p (o k) f", p=P))\
        .then_inc(landed, 16)
    if which == 1:
        bias = a["ffn1_b1"][ds(e, 1), :, :].rearrange("o p f -> p (o f)")
    else:
        bias = a["ffn1_b2"][ds(e, 1), :].rearrange("o d -> (o d)").partition_broadcast(P)
    nc.sync.dma_start(b[:, p, :], bias).then_inc(landed, 16)


def dispatch(nc, m, a, slots):
    R = TILE_RING
    with Stage(nc) as ctx:
        sem = lambda name: ctx.sem(f"disp_{name}")
        ring = ctx.enter_context(nc.sbuf_tensor("disp_ring", [P, R, D + 1], F32))
        index = ctx.enter_context(nc.sbuf_tensor("disp_index", [P, R], I32))
        rows_ready, index_ready, prob_ready = sem("rows"), sem("index"), sem("prob")
        landed = [sem(f"landed{j}") for j in range(R)]
        block = ctx.enter_context(nc.Block())

        @block.sync
        def _(sp):
            for which in (1, 2):
                load_expert(nc, m, a, 0, 0, which)

        @block.vector
        def _(dve):
            def rows(t, j, again, round_):
                if again:
                    dve.wait_ge(landed[j], round_ * 16)
                nc.vector.tensor_scalar(ring[:, j, 0:D], tile_of(m.x, t), m.mean[:, ds(t, 1)], m.scale[:, ds(t, 1)],
                                        ALU.subtract, ALU.mult).then_inc(rows_ready, 1)
            tile_loop(dve, m.tiles, [(0, rows)])

        @block.scalar
        def _(act):
            def fill(t, j, again, round_):
                if again:
                    act.wait_ge(landed[j], round_ * 16)
                nc.scalar.copy(ring[:, j, D:D + 1], m.prob[:, ds(t, 1)]).then_inc(prob_ready, 1)
                nc.scalar.copy(index[:, j:j + 1], m.to[:, ds(t, 1)]).then_inc(index_ready, 1)
            tile_loop(act, m.tiles, [(0, fill)])

        @block.gpsimd
        def _(pool):
            pool.wait_ge(m.slots_zeroed, 48)

            def scatter(t, j, again, round_):
                pool.wait_ge(rows_ready, t + 1)
                pool.wait_ge(prob_ready, t + 1)
                pool.wait_ge(index_ready, t + 1)
                nc.gpsimd.nop(nofuse=True)
                nc.gpsimd.indirect_dma_start(
                    out=slots[:, :], out_offset=bass.IndirectOffsetOnAxis(ap=index[:, j:j + 1], axis=0),
                    in_=ring[:, j, :], in_offset=None, bounds_check=m.experts * m.capacity - 1,
                    oob_is_err=False).then_inc(landed[j], 16)
            tile_loop(pool, m.tiles, [(0, scatter)])
            for j in range(R):
                pool.wait_ge(landed[j], m.tiles // R * 16)


def expert_slots(nc, m, a, slots, results):
    E, C = m.experts, m.capacity
    F = m.hidden1 // P
    LAG, HID_RING, T = 4, 4, 4
    TE = 2 * T
    middle = C - 2 * ceil_div(C - T * P, 2)
    starts = [i * P for i in range(T)] + [middle + i * P for i in range(T - 1)] + [C - P]
    fresh = [0] + [start + P for start in starts[:-1]]
    halves = [(0, T * P), (middle, C)]
    assert ceil_div(C, P) == TE and C - middle <= 512 and m.experts % 2 == 0
    with Stage(nc) as ctx:
        sem = lambda name: ctx.sem(f"exp_{name}")
        buf = lambda name, shape, dt=F32: ctx.enter_context(nc.sbuf_tensor(f"exp_{name}", shape, dt))
        w1, w2, b1, b2 = m.ffn1_w1, m.ffn1_w2, m.ffn1_b1, m.ffn1_b2
        w1_landed, w2_landed = m.w1_landed, m.w2_landed
        w1_hi, w1_lo = buf("w1_hi", [P, DK, F * P], F32R), buf("w1_lo", [P, DK, F * P], F32R)
        w2_hi, w2_lo = buf("w2_hi", [P, F, D], F32R), buf("w2_lo", [P, F, D], F32R)
        rows = buf("rows", [P, TE, D + 1])
        prob = buf("prob", [P, 2, TE])
        cols_hi, cols_lo = buf("cols_hi", [P, 2, DK, C], F32R), buf("cols_lo", [P, 2, DK, C], F32R)
        hid = buf("hid", [P, HID_RING, T * P])
        hid_hi, hid_lo = buf("hid_hi", [P, F, T * P], F32R), buf("hid_lo", [P, F, T * P], F32R)
        y, res, zero = buf("y", [P, T, D]), buf("res", [P, T, D]), buf("zero", [P, D])
        mask, good, clamp = buf("mask", [P, 2, D], I32), buf("good", [P, 2, D], I32), buf("clamp", [P, 2, D])
        rows_landed = [sem(f"rows_landed{i}") for i in range(TE)]
        turned, up_done, relu_done, down_done = sem("turned"), sem("up"), sem("relu"), sem("down")
        w1_rounded, w1_split, w2_rounded, w2_split = sem("w1_rounded"), sem("w1_split"), sem("w2_rounded"), sem("w2_split")
        cols_rounded, cols_split, hid_rounded, hid_split = (sem("cols_rounded"), sem("cols_split"),
                                                            sem("hid_rounded"), sem("hid_split"))
        prob_kept, biased, scaled, clamped, masked, merged, res_zeroed, res_done, zero_made = (
            sem("prob_kept"), sem("biased"), sem("scaled"), sem("clamped"), sem("masked"), sem("merged"),
            sem("res_zeroed"), sem("res_done"), sem("zero_made"))
        stored = [sem(f"stored{i}") for i in range(T)]
        block = ctx.enter_context(nc.Block())

        def turned_ps(i):
            return m.ps[:, 6 + i % 2, 0:D].rearrange("p (k n) -> p k n", k=DK)

        def down_ps(i):
            return m.ps[:, 4 + i // 2, i % 2 * D:(i % 2 + 1) * D]

        def w1_part(buf, q):
            return buf[:, :, q * F // 2 * P:(q + 1) * F // 2 * P]

        def w2_part(buf, q):
            return buf[:, q * F // 2:(q + 1) * F // 2, :]

        @block.sync
        def _(sp):
            def load(e, p, first=False, second=False):
                for i in range(TE):
                    if not first:
                        sp.wait_ge(turned, e * TE + (i + 1 - TE))
                        sp.wait_ge(prob_kept, e * TE + (i + 1 - TE))
                        nc.sync.nop(nofuse=True)
                    sp.dma_start(rows[:, i, :], slots[ds(e * C + starts[i], P), :]).then_inc(rows_landed[i], 16)
                if first:
                    return
                sp.wait_ge(w1_split, e * 2)
                nc.sync.nop(nofuse=True)
                if not second:
                    sp.wait_ge(relu_done, e * 2 * F - 2 * F)
                nc.sync.nop(nofuse=True)
                load_expert(nc, m, a, e, p, 1)
                sp.wait_ge(w2_split, e * 2)
                nc.sync.nop(nofuse=True)
                if not second:
                    sp.wait_ge(biased, e * TE - TE)
                nc.sync.nop(nofuse=True)
                load_expert(nc, m, a, e, p, 2)

            load(0, 0, first=True)
            load(1, 1, second=True)
            with sp.Fori(1, E // 2) as g:
                load(g * 2, 0)
                load(g * 2 + 1, 1)

        @block.tensor
        def _(pe):
            def turn(e, i, first=False):
                pe.wait_ge(rows_landed[i], (e + 1) * 16)
                if not first or i >= 2:
                    pe.wait_ge(cols_split, e * TE + (i - 1))
                for k in range(DK):
                    last = nc.tensor.transpose(turned_ps(i)[:, k, :], rows[:, i, k * P:(k + 1) * P], m.ident[:])
                last.then_inc(turned, 1)

            def up(e, p, h, f, first):
                if f % (F // 2) == 0 and h == 0:
                    pe.wait_ge(w1_split, e * 2 + (1 + f // (F // 2)))
                if not first or h or f >= 4:
                    pe.wait_ge(relu_done, e * 2 * F + (h * F + f - 3))
                lo, hi = halves[h]
                at = slice(f * P, (f + 1) * P)
                for k in range(DK):
                    last = multiply_halves(nc, m.ps[:, f % 4, 0:hi - lo], (w1_hi[:, k, at], w1_lo[:, k, at]),
                                           (cols_hi[:, p, k, lo:hi], cols_lo[:, p, k, lo:hi]), k == 0, k == DK - 1)
                last.then_inc(up_done, 1)

            def down(e, h, f, first):
                if f % (F // 2) == 0 and h == 0:
                    pe.wait_ge(w2_split, e * 2 + (1 + f // (F // 2)))
                pe.wait_ge(hid_split, e * 2 * F + (h * F + f + 1))
                if f == 0 and (h or not first):
                    pe.wait_ge(biased, e * TE + h * T)
                for i in range(T):
                    start = starts[h * T + i] - halves[h][0]
                    at = slice(start, start + P)
                    last = multiply_halves(nc, down_ps(i), (hid_hi[:, f, at], hid_lo[:, f, at]),
                                           (w2_hi[:, f, :], w2_lo[:, f, :]), f == 0 and i % 2 == 0, f == F - 1)
                last.then_inc(down_done, 1)

            def expert(e, p, first=False, last=False):
                pe.wait_ge(cols_split, (e + 1) * TE)
                for h in range(2):
                    for f in range(F):
                        up(e, p, h, f, first)
                        if f >= LAG:
                            down(e, h, f - LAG, first)
                        if h and not last:
                            turn(e + 1, f)
                    for f in range(F - LAG, F):
                        down(e, h, f, first)

            for i in range(TE):
                turn(0, i, first=True)
            expert(0, 0, first=True)
            with pe.Fori(0, E // 2 - 1) as g:
                expert(g * 2 + 1, 1)
                expert(g * 2 + 2, 0)
            expert(E - 1, 1, last=True)

        @block.scalar
        def _(act):
            def round_cols(e, p, i):
                act.wait_ge(turned, e * TE + (i + 1))
                nc.scalar.copy(cols_hi[:, p, :, fresh[i]:starts[i] + P],
                               turned_ps(i)[:, :, fresh[i] - starts[i]:P]).then_inc(cols_rounded, 1)

            def round_w1(e, first=False):
                act.wait_ge(w1_landed, (e + 1) * 32)
                if not first:
                    act.wait_ge(up_done, e * 2 * F)
                for q in range(2):
                    nc.scalar.copy(w1_part(w1_hi, q), w1_part(w1, q)).then_inc(w1_rounded, 1)

            def round_w2(e, first=False):
                act.wait_ge(w2_landed, (e + 1) * 32)
                if not first:
                    act.wait_ge(down_done, e * 2 * F)
                for q in range(2):
                    nc.scalar.copy(w2_part(w2_hi, q), w2_part(w2, q)).then_inc(w2_rounded, 1)

            def expert(e, p, first=False, last=False):
                for h in range(2):
                    width = halves[h][1] - halves[h][0]
                    for f in range(F):
                        n = e * 2 * F + (h * F + f)
                        if not first or h or f >= HID_RING:
                            act.wait_ge(hid_split, n + (1 - HID_RING))
                        act.wait_ge(up_done, n + 1)
                        nc.scalar.activation(hid[:, f % HID_RING, 0:width], m.ps[:, f % 4, 0:width], ACT.Relu,
                                             bias=b1[:, p, f:f + 1]).then_inc(relu_done, 1)
                        act.wait_ge(relu_done, n + 1)
                        if not first or h:
                            act.wait_ge(down_done, n + (1 - F))
                        nc.scalar.copy(hid_hi[:, f, 0:width], hid[:, f % HID_RING, 0:width]).then_inc(hid_rounded, 1)
                        if h == 0 and f == 0 and not first:
                            round_w2(e)
                        if h and not last:
                            round_cols(e + 1, 1 - p, f)
                if not last:
                    round_w1(e + 1)

            for i in range(TE):
                round_cols(0, 0, i)
            round_w1(0, first=True)
            round_w2(0, first=True)
            expert(0, 0, first=True)
            with act.Fori(0, E // 2 - 1) as g:
                expert(g * 2 + 1, 1)
                expert(g * 2 + 2, 0)
            expert(E - 1, 1, last=True)

        @block.vector
        def _(dve):
            def split_cols(e, p, i):
                dve.wait_ge(cols_rounded, e * TE + (i + 1))
                at = slice(fresh[i], starts[i] + P)
                nc.vector.tensor_tensor(cols_lo[:, p, :, at], turned_ps(i)[:, :, fresh[i] - starts[i]:P],
                                        cols_hi[:, p, :, at].bitcast(F32), ALU.subtract).then_inc(cols_split, 1)

            def split_weights(e, part, full, high, low, rounded, split):
                for q in range(2):
                    dve.wait_ge(rounded, e * 2 + (q + 1))
                    nc.vector.tensor_tensor(part(low, q), part(full, q), part(high, q).bitcast(F32),
                                            ALU.subtract).then_inc(split, 1)

            def split_w1(e):
                split_weights(e, w1_part, w1, w1_hi, w1_lo, w1_rounded, w1_split)

            def split_w2(e):
                split_weights(e, w2_part, w2, w2_hi, w2_lo, w2_rounded, w2_split)

            def add_bias(k, p, first=False):
                dve.wait_ge(down_done, k * F + F)
                for i in range(T):
                    if not first:
                        dve.wait_ge(merged, k * T + (i + 1 - T))
                    nc.vector.tensor_tensor(y[:, i, :], down_ps(i), b2[:, p, :], ALU.add).then_inc(biased, 1)

            def examine(k, i, first=False):
                s, n = i % 2, k * T + i
                dve.wait_ge(scaled, n + 1)
                if not first or i >= 2:
                    dve.wait_ge(res_done, n - 1)
                nc.vector.tensor_scalar(clamp[:, s, :], y[:, i, :], 1e4, -1e4, ALU.min, ALU.max).then_inc(clamped, 1)
                nc.vector.tensor_scalar(mask[:, s, :], y[:, i, :], 0.0, 0.0, ALU.mult,
                                        ALU.is_equal).then_inc(masked, 1)
                nc.vector.tensor_tensor(good[:, s, :], y[:, i, :], y[:, i, :], ALU.is_equal).then_inc(masked, 1)

            def take_finite(k, i):
                s, n = i % 2, k * T + i
                dve.wait_ge(clamped, n + 1)
                dve.wait_ge(masked, n * 2 + 2)
                nc.vector.nop(nofuse=True)
                nc.vector.copy_predicated(clamp[:, s, :], mask[:, s, :], y[:, i, :]).then_inc(merged, 1)

            def take_good(k, i):
                s, n = i % 2, k * T + i
                dve.wait_ge(merged, n + 1)
                dve.wait_ge(res_zeroed, n + 1)
                nc.vector.nop(nofuse=True)
                nc.vector.copy_predicated(res[:, i, :], good[:, s, :], clamp[:, s, :]).then_inc(res_done, 1)

            def expert(e, p, first=False, last=False):
                for h in range(2):
                    width = halves[h][1] - halves[h][0]
                    before, p_before = e * 2 + (h - 1), p if h else 1 - p
                    some_before = h or not first
                    if some_before:
                        add_bias(before, p_before, first=first)
                    for f in range(F):
                        dve.wait_ge(hid_rounded, e * 2 * F + (h * F + f + 1))
                        nc.vector.tensor_tensor(hid_lo[:, f, 0:width], hid[:, f % HID_RING, 0:width],
                                                hid_hi[:, f, 0:width].bitcast(F32), ALU.subtract).then_inc(hid_split, 1)
                        if h == 0 and f == 0 and not first:
                            split_w2(e)
                        if some_before and f % 2 == 0:
                            examine(before, f // 2, first=first)
                        if some_before and f % 2:
                            take_finite(before, f // 2)
                        if h and not last:
                            split_cols(e + 1, 1 - p, f)
                        if some_before and f % 2:
                            take_good(before, f // 2)
                if not last:
                    split_w1(e + 1)

            nc.vector.memset(zero[:], 0.0).then_inc(zero_made, 1)
            for i in range(TE):
                split_cols(0, 0, i)
            split_w1(0)
            split_w2(0)
            expert(0, 0, first=True)
            with dve.Fori(0, E // 2 - 1) as g:
                expert(g * 2 + 1, 1)
                expert(g * 2 + 2, 0)
            expert(E - 1, 1, last=True)
            add_bias(2 * E - 1, 1)
            for i in range(T):
                examine(2 * E - 1, i)
                take_finite(2 * E - 1, i)
                take_good(2 * E - 1, i)

        @block.gpsimd
        def _(pool):
            def keep_probs(e, p):
                for i in range(TE):
                    pool.wait_ge(rows_landed[i], (e + 1) * 16)
                    nc.gpsimd.nop(nofuse=True)
                    nc.gpsimd.tensor_copy(prob[:, p, i:i + 1], rows[:, i, D:D + 1]).then_inc(prob_kept, 1)

            def scale_and_store(e, p, h, first=False):
                for i in range(T):
                    n = e * TE + (h * T + i)
                    pool.wait_ge(biased, n + 1)
                    pool.wait_ge(prob_kept, n + 1)
                    nc.gpsimd.nop(nofuse=True)
                    nc.gpsimd.tensor_scalar(y[:, i, :], y[:, i, :], prob[:, p, h * T + i:h * T + i + 1], None,
                                            ALU.mult).then_inc(scaled, 1)
                    if h or not first:
                        pool.wait_ge(stored[i], e * 32 + h * 16)
                        nc.gpsimd.nop(nofuse=True)
                    nc.gpsimd.memset(res[:, i, :], 0.0).then_inc(res_zeroed, 1)
                for i in range(T):
                    tile = h * T + i
                    skip = fresh[tile] - starts[tile]
                    pool.wait_ge(res_done, e * TE + (tile + 1))
                    nc.gpsimd.nop(nofuse=True)
                    pool.dma_start(results[ds(e * C + fresh[tile], P - skip), :], res[skip:P, i, :])\
                        .then_inc(stored[i], 16)

            def expert(e, p, first=False, last=False):
                scale_and_store(e, p, 0, first)
                if not last:
                    if not first:
                        pool.wait_ge(scaled, e * TE)
                    keep_probs(e + 1, 1 - p)
                scale_and_store(e, p, 1, first)

            pool.wait_ge(zero_made, 1)
            pool.dma_start(results[E * C:E * C + 1, :], zero[0:1, :]).then_inc(m.zero_row, 16)
            keep_probs(0, 0)
            expert(0, 0, first=True)
            with pool.Fori(0, E // 2 - 1) as g:
                expert(g * 2 + 1, 1)
                expert(g * 2 + 2, 0)
            expert(E - 1, 1, last=True)
            pool.wait_ge(m.zero_row, 16)
            for i in range(T):
                pool.wait_ge(stored[i], E * 32)


def collect(nc, m, results, out):
    R = TILE_RING
    with Stage(nc) as ctx:
        sem = lambda name: ctx.sem(f"coll_{name}")
        rows = ctx.enter_context(nc.sbuf_tensor("coll_rows", [P, R, D], F32))
        index = ctx.enter_context(nc.sbuf_tensor("coll_index", [P, R], I32))
        index_ready, added, stored = sem("index"), sem("added"), sem("stored")
        landed = [sem(f"landed{j}") for j in range(R)]
        block = ctx.enter_context(nc.Block())

        @block.scalar
        def _(act):
            def put_index(t, j, again, round_):
                if again:
                    act.wait_ge(landed[j], round_ * 16)
                nc.scalar.copy(index[:, j:j + 1], m.back[:, ds(t, 1)]).then_inc(index_ready, 1)
            tile_loop(act, m.tiles, [(0, put_index)])

        @block.gpsimd
        def _(pool):
            def gather(t, j, again, round_):
                pool.wait_ge(index_ready, t + 1)
                if again:
                    pool.wait_ge(added, t + (1 - R))
                nc.gpsimd.nop(nofuse=True)
                nc.gpsimd.indirect_dma_start(
                    out=rows[:, j, :], out_offset=None, in_=results[:, :],
                    in_offset=bass.IndirectOffsetOnAxis(ap=index[:, j:j + 1], axis=0)).then_inc(landed[j], 16)
            tile_loop(pool, m.tiles, [(0, gather)])

        @block.vector
        def _(dve):
            def add(t, j, again, round_):
                dve.wait_ge(landed[j], (round_ + 1) * 16)
                nc.vector.tensor_tensor(tile_of(m.x, t), tile_of(m.x, t), rows[:, j, :], ALU.add).then_inc(added, 1)
            tile_loop(dve, m.tiles, [(0, add)])

        @block.sync
        def _(sp):
            with sp.Fori(0, m.full_tiles // 4) as g:
                sp.wait_ge(added, g * 4 + 4)
                sp.dma_start(out[ds(g * 4 * P, 4 * P), :].rearrange("(t p) d -> p t d", p=P),
                             m.x[:, ds(g * 4, 4), :]).then_inc(stored, 16)
            sp.wait_ge(added, m.tiles)
            sp.dma_start(out[m.full_tiles * P:m.nodes, :], m.x[0:m.tail_nodes, m.full_tiles, :]).then_inc(stored, 16)
            sp.wait_ge(stored, 16 * (m.full_tiles // 4 + 1))


def graph_network(nc, a, out):
    nodes, width = a["x"].shape
    full_chunks, tail_edges = a["src_main"].shape[1], a["src_tail"].shape[0]
    m = Shared()
    m.nodes, m.tiles, m.full_tiles, m.tail_nodes = nodes, ceil_div(nodes, P), nodes // P, nodes % P
    m.full_chunks, m.tail_edges = full_chunks, tail_edges
    m.chunks = ceil_div(full_chunks + 1, 4 * CHUNK_RING) * 4 * CHUNK_RING
    m.experts = a["gate_w"].shape[1]
    m.capacity = ceil_div(nodes * 5, 4 * m.experts)
    m.hidden0, m.hidden1, m.heads = a["ffn0_w1"].shape[2], a["ffn1_w1"].shape[2], a["gat_l"].shape[0]
    table = [nc.dram_tensor(f"table{i}", [m.tiles * P, D], F32, kind="Internal").ap() for i in range(2)]
    heads_table = nc.dram_tensor("heads_table", [m.tiles * P, D + m.heads], F32, kind="Internal").ap()
    left_table = nc.dram_tensor("left_table", [m.tiles * P, m.heads], F32, kind="Internal").ap()
    slots = nc.dram_tensor("slots", [m.experts * m.capacity, D + 1], F32, kind="Internal").ap()
    results = nc.dram_tensor("results", [m.experts * m.capacity + 1, D], F32, kind="Internal").ap()
    with ExitStack() as ctx:
        def sb(name, shape, dt=F32):
            return ctx.enter_context(nc.sbuf_tensor(name, shape, dt))
        m.x = sb("x", [P, m.tiles, D])
        m.mean_row = sb("mean_row", [1, D])
        m.slots_zeroed = ctx.enter_context(nc.semaphore("slots_zeroed"))
        m.x_landed, m.w_landed = (ctx.enter_context(nc.semaphore(name)) for name in ("x_landed", "w_landed"))
        m.zero_made = ctx.enter_context(nc.semaphore("zero_made"))
        m.zero = sb("zero", [P, D + 1])
        m.zero_row = ctx.enter_context(nc.semaphore("zero_row"))
        m.ones = sb("ones", [P, P])
        m.iota_i = sb("iota_i", [P, P], I32)
        m.part_i = sb("part_i", [P, 1], I32)
        m.iota, m.iota_b, m.part = sb("iota", [P, P]), sb("iota_b", [P, P], BF16), sb("part", [P, 1])
        m.stats, m.mean, m.scale = sb("stats", [P, m.tiles, 6]), sb("mean", [P, m.tiles]), sb("scale", [P, m.tiles])
        m.ident, m.first_row = sb("ident", [P, P]), sb("first_row", [P, P])
        m.src, m.dst = sb("src", [P, m.chunks], I32), sb("dst", [P, m.chunks], I32)
        m.ps = ctx.enter_context(nc.psum_tensor("ps", [P, 8, 512], F32))
        wide = ctx.enter_context(ExitStack())
        agg_flat = wide.enter_context(nc.sbuf_tensor("agg", [P, DK * (m.tiles * P + P)], F32))
        m.agg = agg_flat[:].rearrange("p (k n) -> p k n", k=DK)
        with ExitStack() as gcn:
            def gb(name, shape, dt=F32):
                return gcn.enter_context(nc.sbuf_tensor(name, shape, dt))
            m.dloc = gb("dloc", [P, m.chunks])
            m.dinv = gb("dinv", [P, m.tiles])
            m.dst_f = gb("dst_f", [P, m.chunks])
            m.astray = gb("astray_flag", [1, 1], I32)
            m.w1, m.w2, m.w3, m.wp = gb("w1", [P, DK, D]), gb("w2", [P, DK, D]), gb("w3", [P, DK, P]), gb("wp", [P, D])
            m.b1, m.b2, m.b3, m.bp = gb("b1", [P, D]), gb("b2", [P, D]), gb("b3", [P, P]), gb("bp", [P, D])
            load_inputs(nc, m, a, slots)
            degrees(nc, m)
            normalize(nc, m, "norm0", table=table[0])
            sum_edges(nc, m, "e1", table[0])
            update_nodes(nc, m, "n1", m.w1, m.b1, table[1])
            sum_edges(nc, m, "e2", table[1])
            update_nodes(nc, m, "n2", m.w2, m.b2, table[0])
            sum_edges(nc, m, "e3", table[0])
            finish_gcn(nc, m, "n3")
        normalize(nc, m, "norm1", column_sums=True)
        with ExitStack() as ffn:
            def fb(name, shape, dt=F32):
                return ffn.enter_context(nc.sbuf_tensor(name, shape, dt))
            w1_shape, w2_shape = [P, 2, DK, m.hidden0], [P, 2, m.hidden0 // P, D]
            m.f0_w1_hi, m.f0_w1_lo = fb("f0_w1_hi", w1_shape, F32R), fb("f0_w1_lo", w1_shape, F32R)
            m.f0_w2_hi, m.f0_w2_lo = fb("f0_w2_hi", w2_shape, F32R), fb("f0_w2_lo", w2_shape, F32R)
            m.f0_b1, m.f0_b2 = fb("f0_b1", [P, 2, m.hidden0 // P]), fb("f0_b2", [P, D])
            m.gamma, m.beta = fb("gamma", [P, D]), fb("beta", [P, D])
            route_all(nc, m, a)
            two_experts(nc, m)
            add_and_project(nc, m, a, heads_table, left_table)
        wide.close()
        m.gates = sb("gates", [P, m.tiles, m.experts])
        attend(nc, m, a, heads_table, left_table)
        m.prob = sb("prob", [P, m.tiles])
        m.to, m.back = sb("to", [P, m.tiles], I32), sb("back", [P, m.tiles], I32)
        assign_slots(nc, m, a)
        m.ffn1_w1, m.ffn1_w2 = sb("exp_w1", [P, DK, m.hidden1]), sb("exp_w2", [P, m.hidden1 // P, D])
        m.ffn1_b1, m.ffn1_b2 = sb("exp_b1", [P, 2, m.hidden1 // P]), sb("exp_b2", [P, 2, D])
        m.w1_landed, m.w2_landed = (ctx.enter_context(nc.semaphore(name)) for name in ("exp_w1_landed", "exp_w2_landed"))
        dispatch(nc, m, a, slots)
        expert_slots(nc, m, a, slots, results)
        collect(nc, m, results, out)


def kernel(**inputs):
    import numpy as np
    import concourse.bacc as bacc
    from concourse.bass_utils import run_bass_kernel_spmd

    nc = bacc.Bacc("TRN2", target_bir_lowering=False, num_devices=1)
    src, dst = np.asarray(inputs["src"]), np.asarray(inputs["dst"])
    main = src.shape[0] // P * P

    def by_partition(b):
        b = np.asarray(b)
        return b.reshape(b.shape[0], -1, P).transpose(0, 2, 1)

    data = {
        "x": inputs["x"],
        "src_main": src[:main].reshape(-1, P).T, "src_tail": src[main:].reshape(-1, 1),
        "dst_main": dst[:main].reshape(-1, P).T, "dst_tail": dst[main:].reshape(-1, 1),
        "gnn_w1": inputs["L0_gnn_W1"], "gnn_b1": inputs["L0_gnn_b1"],
        "gnn_w2": inputs["L0_gnn_W2"], "gnn_b2": inputs["L0_gnn_b2"],
        "gnn_w3": inputs["L0_gnn_W3"], "gnn_b3": inputs["L0_gnn_b3"],
        "gnn_wp": inputs["L0_gnn_Wp"], "gnn_bp": inputs["L0_gnn_bp"],
        "ffn0_wr": inputs["L0_ffn_Wr"], "ffn0_br": inputs["L0_ffn_br"],
        "ffn0_w1": inputs["L0_ffn_W1"], "ffn0_b1": by_partition(inputs["L0_ffn_b1"]),
        "ffn0_w2": inputs["L0_ffn_W2"], "ffn0_b2": inputs["L0_ffn_b2"],
        "ffn0_gamma": inputs["L0_ffn_gamma"], "ffn0_beta": inputs["L0_ffn_beta"],
        "gat_w": inputs["L1_gnn_weight"], "gat_l": inputs["L1_gnn_attn_l"], "gat_r": inputs["L1_gnn_attn_r"],
        "gate_w": inputs["L1_ffn_gate_w"], "gate_b": inputs["L1_ffn_gate_b"],
        "ffn1_w1": inputs["L1_ffn_w1"], "ffn1_b1": by_partition(inputs["L1_ffn_b1"]),
        "ffn1_w2": inputs["L1_ffn_w2"], "ffn1_b2": inputs["L1_ffn_b2"],
    }
    arrays, a = {}, {}
    for name, value in data.items():
        value = np.ascontiguousarray(value)
        arrays[f"in_{name}"] = value
        a[name] = nc.dram_tensor(f"in_{name}", value.shape, mybir.dt.from_np(value.dtype),
                                 kind="ExternalInput").ap()
    out = nc.dram_tensor("out", inputs["x"].shape, F32, kind="ExternalOutput").ap()
    graph_network(nc, a, out)
    return run_bass_kernel_spmd(nc, [arrays], core_ids=[0]).results[0]["out"]
```
